# Optimizing a Trainium2 kernel written in Bass

```python
import numpy as np
import jax
import jax.numpy as jnp

def _softmax(x, axis=-1):
    return jax.nn.softmax(x, axis=axis)

def _gelu(x):
    return jax.nn.gelu(x, approximate=True)

def _silu(x):
    return jax.nn.silu(x)

def _sigmoid(x):
    return jax.nn.sigmoid(x)

def _layernorm(x, axis=-1, eps=1e-05):
    m = jnp.mean(x, axis=axis, keepdims=True)
    v = jnp.var(x, axis=axis, keepdims=True)
    return (x - m) / jnp.sqrt(v + eps)

def _scatter_add(tgt, idx, src, axis=0):
    return tgt.at[idx].add(src)

def _segment_sum(src, seg, n):
    return jax.ops.segment_sum(src, seg, n)
kernel_name = 'mk_macaron_d1_jaxref_r8_32adeb'

def setup_inputs(seed: int=0):
    np.random.seed(seed)
    _w = jnp.asarray

    def _L0_attn_setup():
        import jax, jax.numpy as jnp
        import numpy as np
        D_MODEL = 128
        NUM_HEADS = 16
        D_K = D_MODEL // NUM_HEADS
        MAX_SEQ_LEN = 512
        THETA = 10000.0

        def _rope_tables(seq_len):
            pos = jnp.arange(seq_len, dtype=jnp.float32)
            pair = jnp.arange(D_K // 2, dtype=jnp.float32)
            rates = THETA ** (-(2.0 * pair) / D_K)
            angles = pos[:, None] * rates[None, :]
            return (jnp.cos(angles), jnp.sin(angles))

        def _apply_rope(x, cos, sin):
            x_even = x[..., 0::2]
            x_odd = x[..., 1::2]
            r_even = x_even * cos - x_odd * sin
            r_odd = x_even * sin + x_odd * cos
            out = jnp.stack([r_even, r_odd], axis=-1)
            return out.reshape(x.shape)
        key = jax.random.key(seed)
        ks = jax.random.split(key, 5)
        x = jax.random.normal(ks[0], (1, 512, D_MODEL), dtype=jnp.float32)
        Wq = jax.random.truncated_normal(ks[1], -2.0, 2.0, (D_MODEL, D_MODEL), dtype=jnp.float32) * D_MODEL ** (-0.5)
        Wk = jax.random.truncated_normal(ks[2], -2.0, 2.0, (D_MODEL, D_MODEL), dtype=jnp.float32) * D_MODEL ** (-0.5)
        Wv = jax.random.truncated_normal(ks[3], -2.0, 2.0, (D_MODEL, D_MODEL), dtype=jnp.float32) * D_MODEL ** (-0.5)
        Wo = jax.random.truncated_normal(ks[4], -2.0, 2.0, (D_MODEL, D_MODEL), dtype=jnp.float32) * D_MODEL ** (-0.5)
        return {'x': x, 'Wq': Wq, 'Wk': Wk, 'Wv': Wv, 'Wo': Wo}
    _L0_attn_in = _L0_attn_setup()

    def _L0_ffn_setup():
        import jax, jax.numpy as jnp
        import numpy as np
        TOP_K = 2
        key = jax.random.key(seed)
        ks = jax.random.split(key, 6)
        B, L, D, E, F = (2, 256, 128, 8, 512)
        x = jax.random.normal(ks[0], (B, L, D), dtype=jnp.float32)
        Wg = jax.random.normal(ks[1], (D, E), dtype=jnp.float32) * D ** (-0.5)
        W1 = jax.random.normal(ks[2], (E, D, F), dtype=jnp.float32) * D ** (-0.5)
        b1 = jnp.zeros((E, F), dtype=jnp.float32)
        W2 = jax.random.normal(ks[3], (E, F, D), dtype=jnp.float32) * F ** (-0.5)
        b2 = jnp.zeros((E, D), dtype=jnp.float32)
        return {'x': x, 'Wg': Wg, 'W1': W1, 'b1': b1, 'W2': W2, 'b2': b2}
    _L0_ffn_in = _L0_ffn_setup()
    _d = {'L0_attn_x': _L0_attn_in['x'], 'L0_attn_Wq': _L0_attn_in['Wq'], 'L0_attn_Wk': _L0_attn_in['Wk'], 'L0_attn_Wv': _L0_attn_in['Wv'], 'L0_attn_Wo': _L0_attn_in['Wo'], 'L0_ffn_Wg': _L0_ffn_in['Wg'], 'L0_ffn_W1': _L0_ffn_in['W1'], 'L0_ffn_b1': _L0_ffn_in['b1'], 'L0_ffn_W2': _L0_ffn_in['W2'], 'L0_ffn_b2': _L0_ffn_in['b2']}
    _x0 = _d['L0_attn_x']
    _d['L0_attn_x'] = jax.random.normal(jax.random.fold_in(jax.random.key(seed), 1), (16, 256, 128), dtype=_x0.dtype)
    del _x0
    return _d

def reference(L0_attn_x, L0_attn_Wq, L0_attn_Wk, L0_attn_Wv, L0_attn_Wo, L0_ffn_Wg, L0_ffn_W1, L0_ffn_b1, L0_ffn_W2, L0_ffn_b2):

    def _L0_attn_ref(x, Wq, Wk, Wv, Wo):
        import jax, jax.numpy as jnp
        import numpy as np
        D_MODEL = 128
        NUM_HEADS = 16
        D_K = D_MODEL // NUM_HEADS
        MAX_SEQ_LEN = 512
        THETA = 10000.0

        def _rope_tables(seq_len):
            pos = jnp.arange(seq_len, dtype=jnp.float32)
            pair = jnp.arange(D_K // 2, dtype=jnp.float32)
            rates = THETA ** (-(2.0 * pair) / D_K)
            angles = pos[:, None] * rates[None, :]
            return (jnp.cos(angles), jnp.sin(angles))

        def _apply_rope(x, cos, sin):
            x_even = x[..., 0::2]
            x_odd = x[..., 1::2]
            r_even = x_even * cos - x_odd * sin
            r_odd = x_even * sin + x_odd * cos
            out = jnp.stack([r_even, r_odd], axis=-1)
            return out.reshape(x.shape)
        b, s, _ = x.shape

        def split_heads(t):
            return t.reshape(b, s, NUM_HEADS, D_K).transpose(0, 2, 1, 3)
        q = split_heads(x @ Wq.T)
        k = split_heads(x @ Wk.T)
        v = split_heads(x @ Wv.T)
        cos, sin = _rope_tables(s)
        q = _apply_rope(q, cos, sin)
        k = _apply_rope(k, cos, sin)
        scores = jnp.einsum('bhqd,bhkd->bhqk', q, k) / jnp.sqrt(jnp.float32(D_K))
        causal = jnp.tril(jnp.ones((s, s), dtype=bool))
        scores = jnp.where(causal, scores, jnp.float32(-1000000000.0))
        probs = jax.nn.softmax(scores, axis=-1)
        attn = jnp.einsum('bhqk,bhkd->bhqd', probs, v)
        attn = attn.transpose(0, 2, 1, 3).reshape(b, s, D_MODEL)
        return attn @ Wo.T

    def _L0_ffn_ref(x, Wg, W1, b1, W2, b2):
        import jax, jax.numpy as jnp
        import numpy as np
        TOP_K = 2
        b, l, d = x.shape
        E = Wg.shape[1]
        xt = x.reshape(b * l, d)
        N = xt.shape[0]
        S = jax.nn.sigmoid(xt @ Wg)
        G, I = jax.lax.top_k(S, TOP_K)
        h = jax.nn.gelu(jnp.einsum('nd,edf->enf', xt, W1) + b1[:, None, :])
        y = jnp.einsum('enf,efd->end', h, W2) + b2[:, None, :]
        combine = jnp.zeros((N, E), dtype=x.dtype).at[jnp.arange(N)[:, None], I].add(G)
        out = jnp.einsum('ne,end->nd', combine, y)
        return out.reshape(b, l, d)
    x = L0_attn_x
    x = x + 0.5 * _L0_ffn_ref(_layernorm(x, axis=-1), L0_ffn_Wg, L0_ffn_W1, L0_ffn_b1, L0_ffn_W2, L0_ffn_b2)
    x = x + _L0_attn_ref(_layernorm(x, axis=-1), L0_attn_Wq, L0_attn_Wk, L0_attn_Wv, L0_attn_Wo)
    x = x + 0.5 * _L0_ffn_ref(_layernorm(x, axis=-1), L0_ffn_Wg, L0_ffn_W1, L0_ffn_b1, L0_ffn_W2, L0_ffn_b2)
    return x

_drawn_inputs = setup_inputs


def setup_inputs(seed=0):
    import zlib

    import numpy as np

    out = dict(_drawn_inputs(seed))
    spreads = {'L0_ffn_b1': (0.0, 0.1), 'L0_ffn_b2': (0.0, 0.1)}
    factors = {}
    for name, (base, spread) in spreads.items():
        noise = np.random.default_rng([zlib.crc32(name.encode()), seed]).standard_normal(out[name].shape)
        drawn = base * np.exp(spread * noise) if base else spread * noise
        out[name] = jnp.asarray(drawn.astype(out[name].dtype))
    for name, factor in factors.items():
        out[name] = (out[name] * factor).astype(out[name].dtype)
    return out
```

```python
from contextlib import ExitStack

import numpy as np

import concourse.bass as bass
from concourse import mybir

F32, F16, BF16 = mybir.dt.float32, mybir.dt.float16, mybir.dt.bfloat16
I32, U32 = mybir.dt.int32, mybir.dt.uint32
ALU, ACT, AX = mybir.AluOpType, mybir.ActivationFunctionType, mybir.AxisListType
Offset = bass.IndirectOffsetOnAxis

P = 128
EPS = 1e-5
TOPK = 2
TILE = 256
SUB = TILE // P
SAT = 16.635532
BIG = 1e30
CH = 8


def later(j, n):
    return not isinstance(j, int) or j >= n


class Steps:

    def __init__(self, eng, sem):
        self.eng, self.sem, self.base, self.n = eng, sem, 0, 0

    def did(self, ins):
        self.n += 1
        ins.then_inc(self.sem, 1)

    def wait(self):
        self.eng.wait_ge(self.sem, self.base + self.n)

    def enter(self, i, per):
        self.start, self.per = self.n, per
        self.base, self.n = self.start + i * per, 0

    def leave(self, rounds):
        assert self.n == self.per, (self.n, self.per)
        self.base, self.n = 0, self.start + rounds * self.per


def macaron(nc, x_in, Wq, Wk, Wv, Wo, Wg, W1, b1, W2, b2, rope_c, rope_s, out, parts=("f0", "at", "f1")):
    B, L, D = x_in.shape
    E, _, F = W1.shape
    N = B * L
    NT = N // P
    NC = NT // CH
    FT = F // P
    KT = TOPK * NT
    NJ = TOPK * N // TILE + E - 1
    NJ += -NJ % 3
    NR = NJ // 3
    NS = NJ * SUB
    H, DK = 16, D // 16
    HW = 32
    G = 4
    QK = 2 * D
    SC = float(DK) ** -0.5
    assert D == P and L == 2 * P

    x_rows = x_in.rearrange("b l d -> (b l) d")
    out_rows = out.rearrange("b l d -> (b l) d")

    ctx = ExitStack()
    with ctx:
        def sb(name, shape, dt):
            return ctx.enter_context(nc.sbuf_tensor(name, shape, dt))

        def sem(name):
            return ctx.enter_context(nc.semaphore(name))

        xn_table = nc.dram_tensor("xn_table", [N, 2 * D], F16, kind="Internal").ap()
        y_table = nc.dram_tensor("y_table", [TOPK * N + NS * P, D], F32, kind="Internal").ap()

        bank = [ctx.enter_context(nc.psum_tensor(f"bank{i}", [P, 512], F32)) for i in range(8)]

        x = sb("x", [P, NT, D], F32)
        stats = sb("stats", [P, CH, 6], F32)
        mean = sb("mean", [P, NT], F32)
        rstd = sb("rstd", [P, NT], F32)
        var = sb("var", [P, CH], F32)
        sd = sb("sd", [P, CH], F32)
        ln_a = sb("ln_a", [P, CH], F32)
        ln_b = sb("ln_b", [P, CH], F32)
        ln_c = sb("ln_c", [P, CH], F32)
        ln_d = sb("ln_d", [P, CH], F32)
        warm = sb("warm", [1, 8], F32)
        eps_c = sb("eps_c", [P, 1], F32)
        xf = sb("xf", [P, CH, D], F32)

        ident = sb("ident", [P, P], F32)
        ident_h = sb("ident_h", [P, P], F16)
        ident_b = sb("ident_b", [P, P], BF16)
        below = sb("below", [P, P], F16)
        ones_h = sb("ones_h", [P, P], F16)
        ones_f = sb("ones_f", [P, E * NT], F32)
        iota_lo = sb("iota_lo", [P, P], F16)
        part1 = sb("part1", [P, 1], F32)
        iota_f = sb("iota_f", [P, P], F32)
        rank_c = sb("rank_c", [P, E], F32)
        slot_c = sb("slot_c", [P, NS], F32)
        tile_lo = sb("tile_lo", [1, NJ], F32)

        w1_hl = sb("w1_hl", [P, 2, E * F], F16)
        w2_hl = sb("w2_hl", [P, 2, E * F], F16)
        wg_f = sb("wg_f", [P, E], F32)
        wg_hl = sb("wg_hl", [P, 2, E], F16)
        b1_rows = sb("b1_rows", [E * FT, P], F32)
        b1_c = sb("b1_c", [P, E * FT], F32)
        b2_r = sb("b2_r", [P, E * D], F32)

        xn_hl = sb("xn_hl", [P, NT, 2, D], F16)
        xnT = sb("xnT", [P, CH, 2, P], F16)
        lg = sb("lg", [P, NT, E], F32)
        lg2 = sb("lg2", [P, NT, E], F32)
        eq = sb("eq", [P, NT, E], F32)
        top = sb("top", [P, TOPK, NT], F32)
        cmx = sb("cmx", [P, NT], F32)
        oh = sb("oh", [P, TOPK, NT, E], F32)
        member = sb("member", [P, NT, E], F16)
        tot = sb("tot", [P, E, NT], F32)
        cum = sb("cum", [P, E, NT], F32)
        before = sb("before", [P, E], F32)
        cnt = sb("cnt", [P, E], F32)
        cnt_i = sb("cnt_i", [P, E], I32)
        cnt_j = sb("cnt_j", [P, E], I32)
        ends = sb("ends", [P, E], F32)
        off = sb("off", [P, E], F32)
        pos = sb("pos", [P, TOPK, NT], F32)
        pos_i = sb("pos_i", [P, KT], I32)
        half_i = sb("half_i", [P, 2, KT], I32)
        half = sb("half", [P, 2, KT], F32)
        gate = sb("gate", [P, TOPK, NT], F32)
        oh_lo = sb("oh_lo", [P, KT, P], F16)
        oh_hi = sb("oh_hi", [P, KT, 2, NS], F16)
        stage = oh_lo[:, :, :].rearrange("p a b -> p (a b)").bitcast(F32)
        used = sb("used", [P, NS], F32)
        rows = sb("rows", [P, NS], F32)
        rows2 = sb("rows2", [P, NS], F32)
        idx = sb("idx", [P, NJ + 3, 2, SUB], U32)
        cur = sb("cur", [P, 3, 2, SUB], U32)
        zero_h = sb("zero_h", [P, P], F16)
        past = sb("past", [1, NJ, E], F32)
        exp_f = sb("exp_f", [1, NJ], F32)
        exp_i = sb("exp_i", [1, NJ], I32)

        xs = sb("xs", [P, 3, SUB, 2 * D], F16)
        xT = sb("xT", [P, 3, 2, TILE], F16)
        hid = sb("hid", [P, 3, FT, TILE], F32)
        hid_hl = sb("hid_hl", [P, 3, 2, FT, TILE], F16)
        ys = sb("ys", [P, 3, SUB, D], F32)
        yc = sb("yc", [P, 2, TOPK, CH // 2, D], F32)

        w_rows = sb("w_rows", [P, 4, D], F32)
        w_qkv = sb("w_qkv", [P, 3 * D], F32)
        w_o = sb("w_o", [P, D], F32)
        cos = sb("cos", [P, 2, DK], F32)
        sin = sb("sin", [P, 2, DK], F32)
        mask_qk = sb("mask_qk", [P, 4, P], BF16)
        mask_kq = sb("mask_kq", [P, 4, P], BF16)
        xa = sb("xa", [P, 2, D], F32)
        xaT = sb("xaT", [P, L], F32)
        v_tmp = sb("v_tmp", [P, 2, D], F32)
        v_ext = sb("v_ext", [P, 2, 2, H, HW], F32)
        r_a = sb("r_a", [P, 2 * H, DK], F32)
        r_b = sb("r_b", [P, 2 * H, DK], F32)
        rot = sb("rot", [P, 2, 2, H, DK], F32)
        q_s = sb("q_s", [P, 2, 2, H, HW], F16)
        k_s = sb("k_s", [P, 2, H, HW], F16)
        qT, kT, qmT = hid_hl[:, 0], hid_hl[:, 1], hid_hl[:, 2, 0]
        pr = hid[:, :, :, :].rearrange("p a b c -> p (a b c)").rearrange("p (r n k) -> p r n k", r=2, n=3)
        o_sb = xf[:, :, :].rearrange("p a d -> p (a d)").rearrange("p (j s) -> p j s", j=4)
        den = sb("den", [P, 2, 4, G], F32)
        att = sb("att", [P, 2, G, 4, DK], F32)
        attT = sb("attT", [P, L], F32)

        s_x = sem("s_x")
        s_wa = sem("s_wa"); s_wt = sem("s_wt"); s_wtc = sem("s_wtc"); s_aconst = sem("s_aconst"); s_vz = sem("s_vz")
        at = {n: sem(f"at_{n}") for n in (
            "var", "sd", "xa", "xaT", "xaTc", "qkv", "vtmp", "vext", "rot", "hi", "lo", "qkT", "qkTc", "S", "max",
            "qmT", "qmTc", "ST", "exp", "PV", "Oc", "OT", "att", "attT", "attTc", "wo", "xadd")}
        s_xc = [sem(f"s_xc{c}") for c in range(NC)]
        s_const = sem("s_const")
        s_w1 = sem("s_w1"); s_w2 = sem("s_w2"); s_small = sem("s_small")
        s_w1h = sem("s_w1h"); s_w1l = sem("s_w1l"); s_w2h = sem("s_w2h"); s_w2l = sem("s_w2l")
        s_wg = sem("s_wg"); s_b1 = sem("s_b1")
        s_dve = sem("s_dve")
        s_pool = sem("s_pool"); s_steps = sem("s_steps")
        s_out = sem("s_out")


        def ffn_sems(k):
            one = ("var", "sd", "split", "tab", "tr", "trc", "lgt", "member", "count", "top", "gate", "slots", "lo",
                   "hi", "inv", "idx", "rows_in", "xT", "hmm", "gelu", "hs", "ymm", "y", "comb", "cur")
            f = {name: sem(f"f{k}_{name}") for name in one}
            f["got"] = [sem(f"f{k}_got{u}") for u in range(3)]
            f["put"] = [sem(f"f{k}_put{u}") for u in range(3)]
            f["yc"] = [sem(f"f{k}_yc{u}") for u in range(2)]
            return f

        ffns = [ffn_sems(0), ffn_sems(1)]
        todo = [k for k in range(2) if f"f{k}" in parts]

        def wait(eng, name, value):
            if not isinstance(value, int) or value > 0:
                eng.wait_ge(at[name], value)

        def sequences(eng, turn, st=None, per=0):
            def at_b(b):
                turn(b, b % 2, 0 <= b < B, 0 <= b + 1 < B, 0 <= b + 2 < B, 0 <= b - 1 < B)
            for b in (-2, -1, 0, 1):
                at_b(b)
            with eng.Fori(0, (B - 4) // 2) as i:
                if st is not None:
                    st.enter(i, 2 * per)
                for u in range(2):
                    turn(2 * i + u + 2, u, True, True, True, True)
            if st is not None:
                st.leave((B - 4) // 2)
            for b in range(B - 2, B + 1):
                at_b(b)

        block = ctx.enter_context(nc.Block())

        @block.sync
        def _(sp):
            sp.dma_start(x[:, :, :], x_rows.rearrange("(t p) d -> p t d", p=P)).then_inc(s_x, 16)
            sp.dma_start(wg_f[:, :], Wg).then_inc(s_small, 16)
            sp.dma_start(stage.rearrange("p (e f) -> p e f", e=E), W1.rearrange("e d f -> d e f")).then_inc(s_w1, 16)
            sp.dma_start(b1_rows[:, :], b1.rearrange("e (t p) -> (e t) p", p=P)).then_inc(s_small, 16)
            sp.dma_start(b2_r[:, :], b2.rearrange("(o e) d -> o (e d)", o=1).broadcast_to([P, E * D])).then_inc(s_small, 16)
            for n, w in enumerate((Wq, Wk, Wv, Wo)):
                sp.dma_start(w_rows[:, n, :], w).then_inc(s_wa, 16)
            for t, r in ((cos, rope_c), (sin, rope_s)):
                sp.dma_start(t[:, :, :], r.rearrange("(t p) d -> p t d", p=P)).then_inc(s_wa, 16)
            sp.wait_ge(s_w1h, 1)
            sp.wait_ge(s_w1l, 1)
            sp.dma_start(stage.rearrange("p (e t d) -> p e t d", e=E, t=FT),
                         W2.rearrange("e (t p) d -> p e t d", p=P)).then_inc(s_w2, 16)

            def attention():
                pass

            def ffn(k):
                f = ffns[k]
                with sp.Fori(0, NC) as c:
                    sp.wait_ge(f["split"], c + 1)
                    sp.dma_start(xn_table.rearrange("(c t p) w -> c p t w", p=P, t=CH)[bass.ds(c, 1)].rearrange("c p t w -> p (c t) w"),
                                 xn_hl[:, bass.ds(c * CH, CH), :, :].rearrange("p t h d -> p t (h d)")).then_inc(f["tab"], 16)
                for u in range(3):
                    sp.wait_ge(f["put"][u], 32 * NR)
                yt = y_table[0:TOPK * N, :].rearrange("(k c t p) d -> k c p t d", k=TOPK, t=CH // 2, p=P)

                def fetch(c, u):
                    for kk in range(TOPK):
                        sp.dma_start(yc[:, u, kk, :, :], yt[kk][bass.ds(c, 1)].rearrange("c p t d -> p (c t) d")).then_inc(f["yc"][u], 16)

                fetch(0, 0)
                fetch(1, 1)
                with sp.Fori(1, NC) as i:
                    for u in range(2):
                        sp.wait_ge(f["comb"], 2 * i + u - 1)
                        fetch(2 * i + u, u)

            def store(k):
                if k is None:
                    sp.wait_ge(at["xadd"], B)
                    sp.dma_start(out_rows.rearrange("(t p) d -> p t d", p=P), x[:, :, :]).then_inc(s_out, 16)
                    sp.wait_ge(s_out, 16)
                    return
                f = ffns[k]
                with sp.Fori(0, 2 * NC) as c:
                    sp.wait_ge(f["comb"], c + 1)
                    sp.dma_start(out_rows.rearrange("(c t p) d -> c p t d", p=P, t=CH // 2)[bass.ds(c, 1)].rearrange("c p t d -> p (c t) d"),
                                 x[:, bass.ds(c * (CH // 2), CH // 2), :]).then_inc(s_out, 16)
                sp.wait_ge(s_out, 16 * 2 * NC)

            for phase in parts:
                if phase == "at":
                    attention()
                else:
                    ffn(int(phase[1]))
            store(1 if 'f1' in parts else None if 'at' in parts else 0)

        @block.gpsimd
        def _(pool):
            st = Steps(pool, s_pool)
            for m in (ident, ident_h, ident_b, zero_h):
                st.did(pool.memset(m[:, :], 0.0))
            st.did(pool.memset(below[:, :], 1.0))
            pool.memset(ones_h[:, :], 1.0)
            pool.memset(ones_f[:, :], 1.0)
            st.wait()
            for m in (ident, ident_h, ident_b):
                pool.affine_select(out=m[:, :], in_=m[:, :], compare_op=ALU.not_equal, fill=1.0, base=0,
                                   pattern=[[-1, P]], channel_multiplier=1)
            pool.affine_select(out=below[:, :], in_=below[:, :], compare_op=ALU.is_gt, fill=0.0, base=0,
                               pattern=[[1, P]], channel_multiplier=-1)
            iota = dict(allow_small_or_imprecise_dtypes=True)
            pool.iota(iota_lo[:, :], pattern=[[1, P]], base=0, channel_multiplier=0, **iota)
            pool.iota(part1[:, :], pattern=[[0, 1]], base=1, channel_multiplier=1, **iota)
            pool.iota(rank_c[:, :], pattern=[[-1, E]], base=E, channel_multiplier=0, **iota)
            pool.iota(slot_c[:, :], pattern=[[P, NS]], base=TOPK * N + 1, channel_multiplier=1, **iota)
            pool.iota(tile_lo[:, :], pattern=[[TILE, NJ]], base=0, channel_multiplier=0, **iota).then_inc(s_const, 1)
            st.did(pool.memset(mask_qk[:, :, :], 0.0))
            st.did(pool.memset(mask_kq[:, :, :], 0.0))
            pool.memset(q_s[:, :, :, :, :], 0.0)
            st.did(pool.memset(k_s[:, :, :, :], 0.0))
            st.did(pool.memset(v_ext[:, :, :, :, :], 0.0))
            st.wait()
            pool.affine_select(out=mask_qk[:, :, :], in_=mask_qk[:, :, :], compare_op=ALU.is_ge, fill=-1e9, base=0,
                               pattern=[[0, 4], [-1, P]], channel_multiplier=1)
            pool.affine_select(out=mask_kq[:, :, :], in_=mask_kq[:, :, :], compare_op=ALU.is_ge, fill=-1e9, base=0,
                               pattern=[[0, 4], [1, P]], channel_multiplier=-1)
            pool.memset(k_s[:, :, :, 3 * DK], 1.0)
            pool.memset(v_ext[:, :, :, :, DK], 1.0).then_inc(s_aconst, 1)
            pool.wait_ge(s_w1h, 1)
            pool.tensor_tensor(w1_hl[:, 1, :], stage, w1_hl[:, 0, :], ALU.subtract).then_inc(s_w1l, 1)
            pool.wait_ge(s_w2h, 1)
            pool.tensor_tensor(w2_hl[:, 1, :], stage, w2_hl[:, 0, :], ALU.subtract).then_inc(s_w2l, 1)

            def settle(j):
                if not isinstance(j, int):
                    pool.sem_inc(s_steps, 1)

            def attention():
                def turn(b, par, scores, maxima, front, back):
                    if front:
                        wait(pool, "PV", 4 * (b + 1))
                        pool.wait_ge(at["vtmp"], 2 * (b + 3))
                        settle(b)
                        pool.tensor_copy(v_ext[:, par, :, :, 0:DK],
                                         v_tmp[:, :, :].rearrange("p t (h d) -> p t h d", d=DK)).then_inc(at["vext"], 1)
                sequences(pool, turn)

            def ffn(k):
                f = ffns[k]
                pool.wait_ge(f["slots"], 1)
                if k == 0:
                    pool.wait_ge(s_w2l, 1)
                for kt in range(KT):
                    ins = pool.tensor_scalar(oh_hi[:, kt, 1, :], iota_lo[:, 0:NS], half[:, 0, kt:kt + 1], float(kt),
                                             ALU.is_equal, ALU.mult)
                    if kt % 8 == 7:
                        ins.then_inc(f["hi"], 1)

                pool.wait_ge(f["idx"], 1)
                pool.wait_ge(f["tab"], 16 * NC)

                def pick(j, u):
                    pool.tensor_copy(cur[:, u, :, :].rearrange("p a b -> p (a b)"),
                                     idx[:, bass.ds(j, 1), :, :].rearrange("p j a b -> p (j a b)")).then_inc(f["cur"], 1)

                def gather(j, u):
                    pool.wait_ge(f["tab"], 16 * NC)
                    settle(j)
                    for h in range(SUB):
                        pool.indirect_dma_start(out=xs[:, u, h, :], out_offset=None, in_=xn_table,
                                                in_offset=Offset(ap=cur[:, u, 0, h:h + 1], axis=0)).then_inc(f["got"][u], 16)

                def scatter(j, u):
                    pool.wait_ge(f["y"], j - 2)
                    settle(j)
                    for h in range(SUB):
                        pool.indirect_dma_start(out=y_table, out_offset=Offset(ap=cur[:, u, 1, h:h + 1], axis=0),
                                                in_=ys[:, u, h, :], in_offset=None).then_inc(f["put"][u], 16)

                pick(0, 0)
                for j in range(3):
                    if j < 2:
                        pick(j + 1, j + 1)
                    pool.wait_ge(f["cur"], j + 1)
                    gather(j, j)
                def step(i, u, again):
                    j = 3 * i + u
                    pool.wait_ge(f["got"][u], 32 * i)
                    if again:
                        pool.wait_ge(f["put"][u], 32 * (i - 1))
                    pick(j, u)
                    pool.wait_ge(f["rows_in"], j - 2)
                    pool.wait_ge(f["cur"], j + 1)
                    gather(j, u)
                    scatter(j, u)

                for u in range(3):
                    step(1, u, False)
                with pool.Fori(2, NR) as i:
                    for u in range(3):
                        step(i, u, True)
                for u in range(3):
                    j = NJ + u
                    pool.wait_ge(f["got"][u], 32 * NR)
                    pool.wait_ge(f["put"][u], 32 * (NR - 1))
                    pick(j, u)
                    pool.wait_ge(f["cur"], j + 1)
                    scatter(j, u)

            for phase in parts:
                if phase == "at":
                    attention()
                else:
                    ffn(int(phase[1]))

        @block.tensor
        def _(pe):
            pe.wait_ge(s_const, 1)
            pe.wait_ge(s_small, 48)
            pe.transpose(bank[5][:, 0:E * FT], b1_rows[:, :], ident[0:E * FT, 0:E * FT]).then_inc(s_b1, 1)

            def h16(b):
                return bank[b][:, :].bitcast(F16)

            def attention():
                pe.wait_ge(s_wa, 16 * 6)
                pe.wait_ge(s_b1, 2)
                for n in range(4):
                    ins = pe.transpose(bank[5][:, n * D:(n + 1) * D], w_rows[:, n, :], ident[:, :])
                ins.then_inc(s_wt, 1)
                pe.wait_ge(s_wtc, 1)
                pe.wait_ge(s_aconst, 1)

                def job_s(b, par, n):
                    j, part = (n // 3 + 2) % 4, n % 3
                    wait(pe, "max", 12 * b + n - 1)
                    r = slice(HW * j, HW * j + 3 * DK)
                    dst = bank[n % 2]
                    if part == 0:
                        pe.matmul(dst[:, :], ident_b[:, :], mask_qk[:, :, :], start=True, stop=False, skip_group_check=True)
                        for g in range(G):
                            ins = pe.matmul(dst[:, g * P:(g + 1) * P], qT[r, par, g, 0:P], kT[r, par, g, 0:P],
                                            start=False, stop=True, skip_group_check=True)
                    else:
                        pe.matmul(dst[:, :].rearrange("p (g k) -> p g k", g=2)[:, :, P:L], ident_b[:, :], mask_qk[:, 0:2, :],
                                  start=True, stop=False, skip_group_check=True)
                        for gg in range(2):
                            g = 2 * (part - 1) + gg
                            ins = pe.matmul(dst[:, gg * L:(gg + 1) * L], qT[r, par, g, P:L], kT[r, par, g, :],
                                            start=False, stop=True, skip_group_check=True)
                    ins.then_inc(at["S"], 1)

                def job_st(b, par, n):
                    j, part = n // 3, n % 3
                    wait(pe, "exp", 12 * b + n - 1)
                    r = slice(HW * j, HW * (j + 1))
                    dst = bank[2 + n % 2]
                    if part == 0:
                        pe.matmul(dst[:, :], ident_b[:, :], mask_kq[:, :, :], start=True, stop=False, skip_group_check=True)
                        for g in range(G):
                            ins = pe.matmul(dst[:, g * P:(g + 1) * P], kT[r, par, g, P:L], qmT[r, g, P:L],
                                            start=False, stop=True, skip_group_check=True)
                    else:
                        pe.matmul(dst[:, :].rearrange("p (g q) -> p g q", g=2)[:, :, 0:P], ident_b[:, :], mask_kq[:, 0:2, :],
                                  start=True, stop=False, skip_group_check=True)
                        for gg in range(2):
                            g = 2 * (part - 1) + gg
                            ins = pe.matmul(dst[:, gg * L:(gg + 1) * L], kT[r, par, g, 0:P], qmT[r, g, :],
                                            start=False, stop=True, skip_group_check=True)
                    ins.then_inc(at["ST"], 1)

                def job_pv(b, par, j):
                    pe.wait_ge(at["exp"], 12 * b + 3 * j + 3)
                    pe.wait_ge(at["vext"], b + 1)
                    wait(pe, "Oc", 4 * b + j)
                    for g in range(G):
                        c = slice(HW * g, HW * (g + 1))
                        pe.matmul(bank[4][c, 0:L], v_ext[:, par, 0, 4 * g + j, :],
                                  pr[:, j % 2, 1 + g // 2, (g % 2) * L:(g % 2 + 1) * L], start=True, stop=False)
                    for g in range(G):
                        c = slice(HW * g, HW * (g + 1))
                        ins = pe.matmul(bank[4][c, P:L], v_ext[:, par, 1, 4 * g + j, :],
                                        pr[:, j % 2, 0, g * P:(g + 1) * P], start=False, stop=True)
                    ins.then_inc(at["PV"], 1)

                def turn(b, par, scores, maxima, front, back):
                    if back:
                        pe.wait_ge(at["Oc"], 4 * b)
                        wait(pe, "qkTc", 2 * (b + 2) if not isinstance(b, int) or b + 1 < B else 2 * B)
                        for j in range(4):
                            for t in range(2):
                                ins = pe.transpose(bank[6 + t][:, j * P:(j + 1) * P], o_sb[:, j, t * P:(t + 1) * P], ident[:, :])
                        ins.then_inc(at["OT"], 1)
                    for n in range(12):
                        if scores:
                            if n == 0:
                                pe.wait_ge(at["qmTc"], b + 1)
                            job_st(b, par, n)
                        if maxima:
                            if n == 0:
                                pe.wait_ge(at["qkTc"], 2 * (b + 2))
                            job_s(b + 1, 1 - par, n)
                        if scores and n % 3 == 0 and n > 0:
                            job_pv(b, par, n // 3 - 1)
                        if front and n == 1:
                            pe.wait_ge(at["xa"], b + 3)
                            wait(pe, "qmTc", b + 1)
                            for t in range(2):
                                ins = pe.transpose(bank[5][:, t * P:(t + 1) * P], xa[:, t, :], ident[:, :])
                            ins.then_inc(at["xaT"], 1)
                        if back and n == 2:
                            pe.wait_ge(at["att"], b)
                            wait(pe, "xaTc", b + 3 if front else B)
                            for t in range(2):
                                ins = pe.transpose(bank[5][:, t * P:(t + 1) * P],
                                                   att[:, t, :, :, :].rearrange("p g j d -> p (g j d)"), ident[:, :])
                            ins.then_inc(at["attT"], 1)
                        if front and n == 4:
                            pe.wait_ge(at["xaTc"], b + 3)
                            wait(pe, "qkTc", 2 * (b + 2))
                            wait(pe, "att", b)
                            for t in range(2):
                                pe.matmul(bank[6 + t][:, 0:3 * D], xaT[:, t * P:(t + 1) * P], w_qkv[:, :],
                                          start=True, stop=True).then_inc(at["qkv"], 1)
                        if back and n == 5:
                            pe.wait_ge(at["attTc"], b)
                            for t in range(2):
                                ins = pe.matmul(bank[5][:, t * P:(t + 1) * P], attT[:, t * P:(t + 1) * P], w_o[:, :],
                                                start=True, stop=True)
                            ins.then_inc(at["wo"], 1)
                    if scores:
                        job_pv(b, par, 3)
                    if front:
                        for t in range(2):
                            pe.wait_ge(at["lo"], 2 * (b + 2) + t + 1)
                            for g in range(G):
                                c = slice(4 * g, 4 * g + 4)
                                pe.transpose(h16(6 + t)[:, g * P:(g + 1) * P],
                                             q_s[:, par, t, c, :].rearrange("p h w -> p (h w)"), ident_h[:, :])
                                ins = pe.transpose(h16(6 + t)[:, (G + g) * P:(G + g + 1) * P],
                                                   k_s[:, t, c, :].rearrange("p h w -> p (h w)"), ident_h[:, :])
                            ins.then_inc(at["qkT"], 1)
                    if maxima:
                        pe.wait_ge(at["max"], 12 * (b + 2))
                        wait(pe, "xadd", b)
                        wait(pe, "xaTc", b + 3 if front else B)
                        for t in range(2):
                            for g in range(G):
                                ins = pe.transpose(h16(5)[:, g * L + t * P:g * L + (t + 1) * P],
                                                   q_s[:, 1 - par, t, 4 * g:4 * g + 4, :].rearrange("p h w -> p (h w)"),
                                                   ident_h[:, :])
                        ins.then_inc(at["qmT"], 1)

                sequences(pe, turn)

            def ffn(k):
                f = ffns[k]
                with pe.Fori(0, NC) as c:
                    pe.wait_ge(f["split"], c + 1)
                    for t in range(CH):
                        for h in range(2):
                            ins = pe.transpose(h16(t // 4)[:, (t % 4 * 2 + h) * P:(t % 4 * 2 + h + 1) * P],
                                               xn_hl[:, bass.ds(c * CH + t, 1), h, :].rearrange("p a d -> p (a d)"), ident_h[:, :])
                        if t % 4 == 3:
                            ins.then_inc(f["tr"], 1)
                    if k == 0:
                        pe.wait_ge(s_wg, 3)
                    for t in range(CH):
                        if t % 4 == 0:
                            pe.wait_ge(f["trc"], c * 2 + t // 4 + 1)
                        dst = bank[2][:, bass.ds((c * CH + t) * E, E)]
                        pe.matmul(dst, xnT[:, t, 0, :], wg_hl[:, 0, :], start=True, stop=False)
                        pe.matmul(dst, xnT[:, t, 1, :], wg_hl[:, 0, :], start=False, stop=False)
                        ins = pe.matmul(dst, xnT[:, t, 0, :], wg_hl[:, 1, :], start=False, stop=True)
                    ins.then_inc(f["lgt"], 1)
                pe.wait_ge(f["member"], 1)
                m = member[:, :, :].rearrange("p t e -> p e t")
                pe.matmul(bank[3][:, 0:E * NT], below[:, :], m, start=True, stop=True)
                pe.matmul(bank[3][:, E * NT:2 * E * NT], ones_h[:, :], m, start=True, stop=True).then_inc(f["count"], 1)
                inv = bank[4][:, 0:2 * NS]
                pe.wait_ge(f["lo"], 1)
                pe.wait_ge(f["hi"], 1)
                pe.matmul(inv, zero_h[:, :], oh_hi[:, 0, :, :], start=True, stop=False)
                with pe.Fori(0, KT // 8) as i:
                    pe.wait_ge(f["lo"], i + 1)
                    pe.wait_ge(f["hi"], i + 1)
                    for mm in range(8):
                        kt = i * 8 + mm
                        pe.matmul(inv, oh_lo[:, bass.ds(kt, 1), :].rearrange("p a s -> p (a s)"),
                                  oh_hi[:, bass.ds(kt, 1), :, :].rearrange("p a b s -> p (a b s)"), start=False, stop=False)
                pe.matmul(inv, zero_h[:, :], oh_hi[:, 0, :, :], start=False, stop=True).then_inc(f["inv"], 1)

                pe.wait_ge(f["idx"], 1)
                if k == 0:
                    pe.wait_ge(s_w1l, 1)
                    pe.wait_ge(s_w2l, 1)
                    pe.wait_ge(s_b1, 2)

                def expert(j):
                    return pe.value_load(exp_i[0:1, bass.ds(j, 1)], min_val=0, max_val=E - 1)

                def turn(j, u, i):
                    pe.wait_ge(f["got"][u], 32 * (i + 1))
                    if later(j, 1):
                        pe.wait_ge(f["xT"], j)
                    for s in range(SUB):
                        for h in range(2):
                            ins = pe.transpose(h16(6)[:, h * TILE + s * P:h * TILE + (s + 1) * P],
                                               xs[:, u, s, h * P:(h + 1) * P], ident_h[:, :])
                    ins.then_inc(f["rows_in"], 1)

                def first(j, u, ex):
                    pe.wait_ge(f["xT"], j + 1)
                    if later(j, 3):
                        pe.wait_ge(f["gelu"], j - 2)
                    for ft in range(FT):
                        dst = bank[2 * u + ft // 2][:, (ft % 2) * TILE:(ft % 2 + 1) * TILE]
                        w = [w1_hl[:, h, bass.ds(ex * F + ft * P, P)] for h in range(2)]
                        pe.matmul(dst, w[0], xT[:, u, 0, :], start=True, stop=False)
                        pe.matmul(dst, w[0], xT[:, u, 1, :], start=False, stop=False)
                        ins = pe.matmul(dst, w[1], xT[:, u, 0, :], start=False, stop=True)
                    ins.then_inc(f["hmm"], 1)

                def second(j, u, ex):
                    pe.wait_ge(f["hs"], j + 1)
                    if later(j, 1):
                        pe.wait_ge(f["y"], j)
                    for s in range(SUB):
                        dst = bank[7][:, s * D:(s + 1) * D]
                        for ft in range(FT):
                            hh = [hid_hl[:, u, h, ft, s * P:(s + 1) * P] for h in range(2)]
                            w = [w2_hl[:, h, bass.ds(ex * F + ft * D, D)] for h in range(2)]
                            pe.matmul(dst, hh[0], w[0], start=(ft == 0), stop=False)
                            pe.matmul(dst, hh[0], w[1], start=False, stop=False)
                            ins = pe.matmul(dst, hh[1], w[0], start=False, stop=(ft == FT - 1))
                    ins.then_inc(f["ymm"], 1)

                def steps(i, head=False, tail=False):
                    ex = [expert(3 * i + u) for u in range(3)]
                    prev = None if head else expert(3 * i - 1)
                    for u in range(3):
                        j = 3 * i + u
                        first(j, u, ex[u])
                        if not (tail and u == 2):
                            turn(j + 1, (u + 1) % 3, i + (u == 2))
                        if not (head and u == 0):
                            second(j - 1, (u + 2) % 3, prev if u == 0 else ex[u - 1])

                turn(0, 0, 0)
                steps(0, head=True)
                with pe.Fori(1, NR - 1) as i:
                    steps(i)
                steps(NR - 1, tail=True)
                second(NJ - 1, 2, expert(NJ - 1))

            for phase in parts:
                if phase == "at":
                    attention()
                else:
                    ffn(int(phase[1]))

        @block.scalar
        def _(act):
            act.wait_ge(s_const, 1)
            act.wait_ge(s_small, 48)
            act.activation(wg_hl[:, 0, :], wg_f[:, :], ACT.Copy).then_inc(s_wg, 2)
            act.wait_ge(s_b1, 1)
            act.activation(b1_c[:, :], bank[5][:, 0:E * FT], ACT.Copy).then_inc(s_b1, 1)
            act.wait_ge(s_w1, 16)
            act.activation(w1_hl[:, 0, :], stage, ACT.Copy).then_inc(s_w1h, 1)
            act.wait_ge(s_w2, 16)
            act.activation(w2_hl[:, 0, :], stage, ACT.Copy).then_inc(s_w2h, 1)

            def attention():
                act.wait_ge(s_wt, 1)
                act.activation(w_qkv[:, :], bank[5][:, 0:3 * D], ACT.Copy)
                act.activation(w_o[:, :], bank[5][:, 3 * D:4 * D], ACT.Copy).then_inc(s_wtc, 1)
                act.activation(warm[0:1, 6:7], ident[0:1, 0:1], ACT.Sqrt)
                with act.Fori(0, NC) as c:
                    act.wait_ge(at["var"], c + 1)
                    act.activation(sd[:, :], var[:, :], ACT.Sqrt, bias=eps_c[:, :], scale=1.0 / D).then_inc(at["sd"], 1)
                act.activation(warm[0:1, 7:8], ident[0:1, 0:1], ACT.Exp)
                act.wait_ge(s_aconst, 1)

                def outputs(b, j):
                    act.wait_ge(at["PV"], 4 * b + j + 1)
                    if j == 0:
                        wait(act, "OT", b)
                    act.activation(o_sb[:, j, :], bank[4][:, 0:L], ACT.Copy).then_inc(at["Oc"], 1)

                def turn(b, par, scores, maxima, front, back):
                    for n in range(12):
                        if scores:
                            j, part = n // 3, n % 3
                            act.wait_ge(at["ST"], 12 * b + n + 1)
                            wait(act, "PV", 4 * b + j - 1)
                            act.activation(pr[:, j % 2, part, :], bank[2 + n % 2][:, :], ACT.Exp, scale=SC).then_inc(at["exp"], 1)
                            if n % 3 == 1 and n > 3:
                                outputs(b, n // 3 - 1)
                        if front and n == 1:
                            act.wait_ge(at["xaT"], b + 3)
                            wait(act, "qkv", 2 * (b + 2))
                            act.activation(xaT[:, :], bank[5][:, 0:L], ACT.Copy).then_inc(at["xaTc"], 1)
                        if back and n == 2:
                            act.wait_ge(at["attT"], b)
                            wait(act, "wo", b - 1)
                            act.activation(attT[:, :], bank[5][:, 0:L], ACT.Copy).then_inc(at["attTc"], 1)
                        if front and n == 4:
                            wait(act, "vext", b + 2)
                            for t in range(2):
                                act.wait_ge(at["qkv"], 2 * (b + 2) + t + 1)
                                act.activation(v_tmp[:, t, :], bank[6 + t][:, 2 * D:3 * D], ACT.Copy).then_inc(at["vtmp"], 1)
                        if front and n in (6, 8):
                            t = n // 2 - 3
                            act.wait_ge(at["rot"], 2 * (b + 2) + t + 1)
                            wait(act, "qmT", b + 1)
                            wait(act, "qkT", 2 * (b + 2))
                            act.activation(q_s[:, par, t, :, 0:2 * DK].rearrange("p h (c d) -> p h c d", c=2),
                                           rot[:, t, 0, :, :].unsqueeze(2).broadcast_to([P, H, 2, DK]), ACT.Copy)
                            act.activation(k_s[:, t, :, 0:4 * DK].rearrange("p h (c d) -> p h c d", c=4)[:, :, 0:3:2, :],
                                           rot[:, t, 1, :, :].unsqueeze(2).broadcast_to([P, H, 2, DK]),
                                           ACT.Copy).then_inc(at["hi"], 1)
                    if scores:
                        outputs(b, 3)
                    if front:
                        act.wait_ge(at["qkT"], 2 * (b + 2) + 2)
                        wait(act, "ST", 12 * (b + 1))
                        wait(act, "S", 12 * (b + 1))
                        for dst, first in ((qT, 0), (kT, G)):
                            ins = act.activation(dst[:, par, :, P:L], bank[7][:, :].bitcast(F16)[:, first * P:(first + G) * P]
                                                 .rearrange("p (g s) -> p g s", g=G), ACT.Copy)
                        ins.then_inc(at["qkTc"], 1)
                    if maxima:
                        act.wait_ge(at["qmT"], b + 2)
                        wait(act, "ST", 12 * (b + 1))
                        act.activation(qmT[:, :, :].rearrange("p g s -> p (g s)"), bank[5][:, :].bitcast(F16), ACT.Copy).then_inc(at["qmTc"], 1)

                sequences(act, turn)

            def ffn(k):
                f = ffns[k]
                act.activation(warm[0:1, 3 * k:3 * k + 1], ident[0:1, 0:1], ACT.Sqrt)
                with act.Fori(0, NC) as c:
                    act.wait_ge(f["var"], c + 1)
                    act.activation(sd[:, :], var[:, :], ACT.Sqrt, bias=eps_c[:, :], scale=1.0 / D).then_inc(f["sd"], 1)
                    for q in range(2):
                        act.wait_ge(f["tr"], 2 * c + q + 1)
                        act.activation(xnT[:, 4 * q:4 * q + 4, :, :].rearrange("p a b c -> p (a b c)"),
                                       bank[q][:, :].bitcast(F16), ACT.Copy).then_inc(f["trc"], 1)
                act.wait_ge(f["top"], 1)
                act.activation(gate[:, :, :], top[:, :, :], ACT.Sigmoid).then_inc(f["gate"], 1)

                act.activation(warm[0:1, 3 * k + 1:3 * k + 2], ident[0:1, 0:1], ACT.Gelu_apprx_tanh)
                act.wait_ge(f["idx"], 1)

                def gelu(j, u, i):
                    ex = act.value_load(exp_i[0:1, bass.ds(j, 1)], min_val=0, max_val=E - 1)
                    act.wait_ge(f["hmm"], j + 1)
                    if later(j, 3):
                        act.wait_ge(f["hs"], j - 2)
                    for ft in range(FT):
                        ins = act.activation(hid[:, u, ft, :], bank[2 * u + ft // 2][:, (ft % 2) * TILE:(ft % 2 + 1) * TILE],
                                             ACT.Gelu_apprx_tanh, bias=b1_c[:, bass.ds(ex * FT + ft, 1)])
                    ins.then_inc(f["gelu"], 1)

                for u in range(3):
                    gelu(u, u, 0)
                with act.Fori(1, NR) as i:
                    for u in range(3):
                        gelu(3 * i + u, u, i)

            for phase in parts:
                if phase == "at":
                    attention()
                else:
                    ffn(int(phase[1]))

        @block.vector
        def _(dve):
            st = Steps(dve, s_dve)
            st.did(dve.memset(eps_c[:, :], EPS))
            dve.memset(idx[:, :, :, :], 0)
            st.did(dve.memset(before[:, :], 0.0))
            st.wait()
            dve.wait_ge(s_small, 48)
            dve.wait_ge(s_wg, 2)
            dve.tensor_tensor(wg_hl[:, 1, :], wg_f[:, :], wg_hl[:, 0, :], ALU.subtract).then_inc(s_wg, 1)
            dve.wait_ge(s_x, 16)

            def deviations(c, f):
                for t in range(CH):
                    ins = dve.bn_stats(stats[:, t, :], x[:, bass.ds(c * CH + t, 1), :].rearrange("p a d -> p (a d)"))
                st.did(ins)
                st.wait()
                even, odd = stats[:, :, 1], stats[:, :, 4]
                dve.tensor_tensor(ln_a[:, :], even, odd, ALU.add)
                dve.tensor_tensor(ln_b[:, :], even, odd, ALU.subtract)
                st.did(dve.tensor_tensor(ln_c[:, :], stats[:, :, 2], stats[:, :, 5], ALU.add))
                st.wait()
                dve.tensor_scalar(mean[:, bass.ds(c * CH, CH)], ln_a[:, :], 0.5, None, ALU.mult)
                st.did(dve.tensor_tensor(ln_d[:, :], ln_b[:, :], ln_b[:, :], ALU.mult))
                st.wait()
                dve.scalar_tensor_tensor(out=var[:, :], in0=ln_d[:, :], scalar=D / 4.0, in1=ln_c[:, :],
                                         op0=ALU.mult, op1=ALU.add).then_inc(f["var"], 1)
                dve.wait_ge(f["sd"], c + 1)
                st.did(dve.reciprocal(rstd[:, bass.ds(c * CH, CH)], sd[:, :]))
                st.wait()

            def norm(c, f):
                deviations(c, f)
                for t in range(CH):
                    tt = c * CH + t
                    ins = dve.tensor_scalar(xf[:, t, :], x[:, bass.ds(tt, 1), :].rearrange("p a d -> p (a d)"),
                                            mean[:, bass.ds(tt, 1)], rstd[:, bass.ds(tt, 1)], ALU.subtract, ALU.mult)
                st.did(ins)
                st.wait()

            def attention():
                with dve.Fori(0, NC) as c:
                    st.enter(c, 4)
                    deviations(c, at)
                st.leave(NC)
                dve.wait_ge(s_aconst, 1)
                dve.wait_ge(s_wa, 16 * 6)

                def maximum(b, par, n):
                    j, part = (n // 3 + 2) % 4, n % 3
                    dve.wait_ge(at["S"], 12 * b + n + 1)
                    t, g0, ng = (0, 0, G) if part == 0 else (1, 2 * (part - 1), 2)
                    dst = q_s[:, par, t, :, 3 * DK].rearrange("p (g j) -> p g j", g=G)[:, g0:g0 + ng, j]
                    dve.tensor_reduce(dst, bank[n % 2][:, :].rearrange("p (g k) -> p g k", g=ng), AX.X, ALU.max,
                                      negate=True).then_inc(at["max"], 1)

                def rope(b, t):
                    dve.wait_ge(at["qkv"], 2 * b + t + 1)
                    dve.wait_ge(at["vtmp"], 2 * b + t + 1)
                    wait(dve, "lo", 2 * b + t - 1)
                    wait(dve, "hi", 2 * b + t - 1)
                    src = bank[6 + t][:, 0:QK].rearrange("p (h d) -> p h d", d=DK)
                    c = cos[:, t, :].unsqueeze(1).broadcast_to([P, 2 * H, DK])
                    s = sin[:, t, :].rearrange("p (i c) -> p i c", c=2)
                    dve.tensor_tensor(r_a[:, :, :], src, c, ALU.mult)
                    pairs = src.rearrange("p h (i c) -> p h i c", c=2)
                    rb = r_b[:, :, :].rearrange("p h (i c) -> p h i c", c=2)
                    for c in range(2):
                        ins = dve.tensor_tensor(rb[:, :, :, c], pairs[:, :, :, 1 - c],
                                                s[:, :, c].unsqueeze(1).broadcast_to([P, 2 * H, DK // 2]), ALU.mult)
                    st.did(ins)
                    st.wait()
                    dve.tensor_tensor(rot[:, t, :, :, :].rearrange("p a h d -> p (a h) d"), r_a[:, :, :], r_b[:, :, :],
                                      ALU.add).then_inc(at["rot"], 1)
                    dve.wait_ge(at["rot"], 2 * b + t + 1)

                def low(b, par, t):
                    dve.wait_ge(at["hi"], 2 * b + t + 1)
                    dve.tensor_tensor(q_s[:, par, t, :, 2 * DK:3 * DK], rot[:, t, 0, :, :], q_s[:, par, t, :, 0:DK], ALU.subtract)
                    dve.tensor_tensor(k_s[:, t, :, DK:2 * DK], rot[:, t, 1, :, :], k_s[:, t, :, 0:DK],
                                      ALU.subtract).then_inc(at["lo"], 1)

                def turn(b, par, scores, maxima, front, back):
                    if front:
                        wait(dve, "xaT", b + 2)
                        for t in range(2):
                            tt = 2 * (b + 2) + t
                            ins = dve.tensor_scalar(xa[:, t, :], x[:, bass.ds(tt, 1), :].rearrange("p a d -> p (a d)"),
                                                    mean[:, bass.ds(tt, 1)], rstd[:, bass.ds(tt, 1)], ALU.subtract, ALU.mult)
                        ins.then_inc(at["xa"], 1)
                    if back:
                        dve.wait_ge(at["OT"], b)
                        wait(dve, "attT", b - 1)
                        views = [bank[6 + t][:, :].rearrange("p (j g w) -> p j g w", j=4, g=G) for t in range(2)]
                        for t in range(2):
                            ins = dve.reciprocal(den[:, t, :, :], views[t][:, :, :, DK])
                        st.did(ins)
                        st.wait()
                        for t in range(2):
                            ins = dve.tensor_tensor(att[:, t, :, :, :].rearrange("p g j d -> p j g d"), views[t][:, :, :, 0:DK],
                                                    den[:, t, :, :].unsqueeze(3).broadcast_to([P, 4, G, DK]), ALU.mult)
                        ins.then_inc(at["att"], 1)
                    for n in range(12):
                        if maxima:
                            maximum(b + 1, 1 - par, n)
                        if back and n == 5:
                            dve.wait_ge(at["wo"], b)
                            xt = x[:, bass.ds(2 * (b - 1), 2), :]
                            dve.tensor_tensor(xt, bank[5][:, 0:L].rearrange("p (t d) -> p t d", t=2), xt, ALU.add).then_inc(at["xadd"], 1)
                        if front and n in (4, 6):
                            rope(b + 2, n // 2 - 2)
                        if front and n in (7, 8):
                            low(b + 2, par, n - 7)
                    if front:
                        dve.wait_ge(at["qkT"], 2 * (b + 2) + 1)
                        wait(dve, "ST", 12 * (b + 1))
                        wait(dve, "S", 12 * (b + 1))
                        for dst, first in ((qT, 0), (kT, G)):
                            ins = dve.tensor_copy(dst[:, par, :, 0:P], bank[6][:, :].bitcast(F16)[:, first * P:(first + G) * P]
                                                  .rearrange("p (g s) -> p g s", g=G))
                        ins.then_inc(at["qkTc"], 1)

                sequences(dve, turn, st, 3)
                dve.wait_ge(at["xadd"], B)

            def ffn(k):
                f = ffns[k]
                with dve.Fori(0, NC) as c:
                    st.enter(c, 6)
                    norm(c, f)
                    hi = xn_hl[:, bass.ds(c * CH, CH), 0, :]
                    lo = xn_hl[:, bass.ds(c * CH, CH), 1, :]
                    st.did(dve.tensor_copy(hi, xf[:, :, :]))
                    st.wait()
                    dve.tensor_tensor(lo, xf[:, :, :], hi, ALU.subtract).then_inc(f["split"], 1)
                st.leave(NC)

                dve.wait_ge(f["lgt"], NC)
                st.did(dve.tensor_scalar(lg[:, :, :].rearrange("p t e -> p (t e)"), bank[2][:, 0:NT * E], SAT, None, ALU.min))
                rank_b = rank_c[:, :].unsqueeze(1).broadcast_to([P, NT, E])

                def over_e(a):
                    return a.unsqueeze(2).broadcast_to([P, NT, E])

                dve.wait_ge(s_const, 1)
                for kk, src in enumerate((lg, lg2)):
                    st.wait()
                    st.did(dve.tensor_reduce(top[:, kk, :], src[:, :, :], AX.X, ALU.max))
                    st.wait()
                    st.did(dve.tensor_tensor(eq[:, :, :], src[:, :, :], over_e(top[:, kk, :]), ALU.is_equal))
                    st.wait()
                    st.did(dve.tensor_tensor(eq[:, :, :], eq[:, :, :], rank_b, ALU.mult))
                    st.wait()
                    st.did(dve.tensor_reduce(cmx[:, :], eq[:, :, :], AX.X, ALU.max))
                    st.wait()
                    st.did(dve.tensor_tensor(oh[:, kk, :, :], rank_b, over_e(cmx[:, :]), ALU.is_equal))
                    st.wait()
                    if kk == 0:
                        st.did(dve.scalar_tensor_tensor(out=lg2[:, :, :], in0=oh[:, 0, :, :], scalar=-BIG, in1=lg[:, :, :],
                                                        op0=ALU.mult, op1=ALU.add))
                dve.tensor_tensor(member[:, :, :], oh[:, 0, :, :], oh[:, 1, :, :], ALU.add).then_inc(f["member"], 1)
                dve.nop().then_inc(f["top"], 1)

                dve.wait_ge(f["count"], 1)
                st.did(dve.tensor_copy(tot[:, :, :].rearrange("p e t -> p (e t)"), bank[3][:, E * NT:2 * E * NT]))
                st.wait()
                st.did(dve.tensor_tensor_scan(cum[:, :, :].rearrange("p e t -> p (e t)"), ones_f[:, :],
                                              tot[:, :, :].rearrange("p e t -> p (e t)"), 0.0, ALU.mult, ALU.add))
                st.wait()
                st.did(dve.tensor_copy(before[:, 1:E], cum[:, 0:E - 1, NT - 1]))
                dve.tensor_tensor(tot[:, :, :], cum[:, :, :], tot[:, :, :], ALU.subtract)
                st.wait()
                st.did(dve.tensor_tensor(cnt[:, :], cum[:, :, NT - 1], before[:, :], ALU.subtract))
                st.wait()
                st.did(dve.tensor_scalar(cnt_i[:, :], cnt[:, :], float(TILE - 1), None, ALU.add))
                st.wait()
                shift = TILE.bit_length() - 1
                st.did(dve.tensor_scalar(cnt_j[:, :], cnt_i[:, :], shift, shift, ALU.logical_shift_right, ALU.logical_shift_left))
                st.wait()
                st.did(dve.tensor_copy(cnt[:, :], cnt_j[:, :]))
                st.wait()
                st.did(dve.tensor_tensor_scan(ends[:, :], ones_f[:, 0:E], cnt[:, :], 0.0, ALU.mult, ALU.add))
                st.wait()
                st.did(dve.tensor_tensor(off[:, :], ends[:, :], cnt[:, :], ALU.subtract))
                st.wait()
                st.did(dve.tensor_tensor(off[:, :], off[:, :], before[:, :], ALU.subtract))
                st.wait()
                st.did(dve.tensor_tensor(tot[:, :, :], tot[:, :, :], off[:, :].unsqueeze(2).broadcast_to([P, E, NT]), ALU.add))
                st.wait()
                st.did(dve.tensor_tensor(cum[:, :, :].rearrange("p e t -> p (e t)"), bank[3][:, 0:E * NT],
                                         tot[:, :, :].rearrange("p e t -> p (e t)"), ALU.add))
                for kk, tmp in enumerate((eq, lg2)):
                    st.wait()
                    st.did(dve.tensor_tensor(tmp[:, :, :], oh[:, kk, :, :], cum[:, :, :].rearrange("p e t -> p t e"), ALU.mult))
                for kk, tmp in enumerate((eq, lg2)):
                    st.wait()
                    st.did(dve.tensor_reduce(pos[:, kk, :], tmp[:, :, :], AX.X, ALU.add))
                st.wait()
                st.did(dve.tensor_copy(pos_i[:, :], pos[:, :, :].rearrange("p k t -> p (k t)")))
                st.wait()
                lop = P.bit_length() - 1
                st.did(dve.tensor_scalar(half_i[:, 0, :], pos_i[:, :], lop, 0, ALU.logical_shift_right, ALU.logical_shift_left))
                st.did(dve.tensor_scalar(half_i[:, 1, :], pos_i[:, :], 32 - lop, 32 - lop, ALU.logical_shift_left, ALU.logical_shift_right))
                st.wait()
                dve.tensor_copy(half[:, :, :], half_i[:, :, :]).then_inc(f["slots"], 1)
                st.did(dve.tensor_tensor(past[:, :, :], ends[0:1, :].unsqueeze(1).broadcast_to([1, NJ, E]),
                                         tile_lo[:, :].unsqueeze(2).broadcast_to([1, NJ, E]), ALU.is_le))
                st.wait()
                st.did(dve.tensor_reduce(exp_f[:, :], past[:, :, :], AX.X, ALU.add))
                st.wait()
                st.did(dve.tensor_scalar(exp_i[:, :], exp_f[:, :], float(E - 1), None, ALU.min))

                dve.wait_ge(f["slots"], 1)
                if k == 0:
                    dve.wait_ge(s_w2l, 1)
                with dve.Fori(0, KT // 8) as i:
                    for m in range(8):
                        kt = i * 8 + m
                        dve.tensor_scalar(oh_lo[:, bass.ds(kt, 1), :].rearrange("p a s -> p (a s)"), iota_lo[:, :],
                                          half[:, 1, bass.ds(kt, 1)], None, ALU.is_equal)
                        ins = dve.tensor_scalar(oh_hi[:, bass.ds(kt, 1), 0, :].rearrange("p a s -> p (a s)"), iota_lo[:, 0:NS],
                                                half[:, 0, bass.ds(kt, 1)], part1[:, 0:1], ALU.is_equal, ALU.mult)
                    ins.then_inc(f["lo"], 1)
                dve.wait_ge(f["gate"], 1)
                st.did(dve.tensor_scalar(gate[:, :, :], gate[:, :, :], 0.5, None, ALU.mult))

                dve.wait_ge(f["inv"], 1)
                st.did(dve.tensor_scalar(used[:, :], bank[4][:, 0:NS], 0.0, None, ALU.is_equal))
                st.did(dve.tensor_scalar(rows[:, :], bank[4][:, NS:2 * NS], float(P), None, ALU.mult))
                st.did(dve.tensor_scalar(rows2[:, :], bank[4][:, NS:2 * NS], float(NT), float(-N), ALU.is_ge, ALU.mult))
                st.wait()
                st.did(dve.tensor_tensor(used[:, :], used[:, :], slot_c[:, :], ALU.mult))
                st.did(dve.tensor_tensor(rows[:, :], bank[4][:, 0:NS], rows[:, :], ALU.add))
                st.wait()
                st.did(dve.tensor_tensor(used[:, :], used[:, :], rows[:, :], ALU.add))
                st.did(dve.tensor_tensor(rows2[:, :], rows2[:, :], rows[:, :], ALU.add))
                st.wait()
                st.did(dve.tensor_scalar(idx[:, 3:NJ + 3, 1, :], used[:, :].rearrange("p (j s) -> p j s", s=SUB), -1.0, None, ALU.add))
                dve.tensor_scalar(idx[:, 0:NJ, 0, :], rows2[:, :].rearrange("p (j s) -> p j s", s=SUB), -1.0, 0.0,
                                  ALU.add, ALU.max).then_inc(f["idx"], 1)
                st.wait()

                def load_x(j, u):
                    dve.wait_ge(f["rows_in"], j + 1)
                    if later(j, 3):
                        dve.wait_ge(f["hmm"], j - 2)
                    dve.tensor_copy(xT[:, u, :, :].rearrange("p h s -> p (h s)"),
                                    bank[6][:, :].bitcast(F16)[:, 0:2 * TILE]).then_inc(f["xT"], 1)

                def split(j, u, i):
                    dve.wait_ge(f["gelu"], j + 1)
                    if later(j, 3):
                        dve.wait_ge(f["ymm"], j - 2)
                    st.did(dve.tensor_copy(hid_hl[:, u, 0, :, :], hid[:, u, :, :]))
                    st.wait()
                    dve.tensor_tensor(hid_hl[:, u, 1, :, :], hid[:, u, :, :], hid_hl[:, u, 0, :, :], ALU.subtract).then_inc(f["hs"], 1)

                def leave(j, u, i):
                    ex = dve.value_load(exp_i[0:1, bass.ds(j, 1)], min_val=0, max_val=E - 1)
                    dve.wait_ge(f["ymm"], j + 1)
                    if later(j, 3):
                        dve.wait_ge(f["put"][u], 32 * i)
                    dve.tensor_tensor(ys[:, u, :, :], bank[7][:, 0:SUB * D].rearrange("p (s d) -> p s d", s=SUB),
                                      b2_r[:, bass.ds(ex * D, D)].unsqueeze(1).broadcast_to([P, SUB, D]),
                                      ALU.add).then_inc(f["y"], 1)

                def steps(i, head=False, tail=False):
                    for u in range(3):
                        j = 3 * i + u
                        if not (tail and u == 2):
                            load_x(j + 1, (u + 1) % 3) if not (head and u < 2) else load_x(j + 1, u + 1)
                        split(j, u, i)
                        if not (head and u == 0):
                            leave(j - 1, (u + 2) % 3, i - (u == 0))

                load_x(0, 0)
                steps(0, head=True)
                with dve.Fori(1, NR - 1) as i:
                    st.enter(i - 1, 3)
                    steps(i)
                st.leave(NR - 2)
                steps(NR - 1, tail=True)
                leave(NJ - 1, 2, NR - 1)

                with dve.Fori(0, NC) as i:
                    st.enter(i, 2)
                    for u in range(2):
                        c = 2 * i + u
                        dve.wait_ge(f["yc"][u], 32 * i + 32)
                        for kk in range(TOPK):
                            for t in range(CH // 2):
                                tt = c * (CH // 2) + t
                                xt = x[:, bass.ds(tt, 1), :].rearrange("p a d -> p (a d)")
                                ins = dve.scalar_tensor_tensor(out=xt, in0=yc[:, u, kk, t, :], scalar=gate[:, kk, bass.ds(tt, 1)],
                                                               in1=xt, op0=ALU.mult, op1=ALU.add)
                            if kk == 0:
                                st.did(ins)
                                st.wait()
                        ins.then_inc(f["comb"], 1)
                st.leave(NC)
                dve.wait_ge(f["comb"], 2 * NC)

            for phase in parts:
                if phase == "at":
                    attention()
                else:
                    ffn(int(phase[1]))


_INS = ["L0_attn_x", "L0_attn_Wq", "L0_attn_Wk", "L0_attn_Wv", "L0_attn_Wo", "L0_ffn_Wg",
        "L0_ffn_W1", "L0_ffn_b1", "L0_ffn_W2", "L0_ffn_b2"]


def rope_tables(length, dk, theta=10000.0):
    f = np.float32
    rates = f(theta) ** (-(f(2.0) * np.arange(dk // 2, dtype=f)) / f(dk))
    angles = np.arange(length, dtype=f)[:, None] * rates[None, :].astype(f)
    cos, sin = np.cos(angles), np.sin(angles)
    return (np.repeat(cos, 2, axis=1).astype(f), np.stack([-sin, sin], axis=-1).reshape(length, dk).astype(f))


def kernel(**inputs):
    import concourse.bacc as bacc
    from concourse.bass_utils import run_bass_kernel_spmd

    nc = bacc.Bacc("TRN2", target_bir_lowering=False, num_devices=1)
    given = {name: np.ascontiguousarray(inputs[name]) for name in _INS}
    B, L, D = given["L0_attn_x"].shape
    given["rope_c"], given["rope_s"] = rope_tables(L, D // 16)
    arrays, args = {}, []
    for name, a in given.items():
        arrays[f"in_{name}"] = a
        args.append(nc.dram_tensor(f"in_{name}", a.shape, mybir.dt.from_np(a.dtype), kind="ExternalInput").ap())
    out = nc.dram_tensor("out_0", (B, L, D), F32, kind="ExternalOutput").ap()
    macaron(nc, *args, out)
    r = run_bass_kernel_spmd(nc, [arrays], core_ids=[0])
    return r.results[0]["out_0"]
```

```python
from contextlib import ExitStack

import numpy as np

import concourse.bass as bass
from concourse import mybir

F32, F16, BF16 = mybir.dt.float32, mybir.dt.float16, mybir.dt.bfloat16
I32, U32 = mybir.dt.int32, mybir.dt.uint32
ALU, ACT, AX = mybir.AluOpType, mybir.ActivationFunctionType, mybir.AxisListType
Offset = bass.IndirectOffsetOnAxis

P = 128
EPS = 1e-5
TOPK = 2
TILE = 256
SUB = TILE // P
SAT = 16.635532
BIG = 1e30
CH = 8


def later(j, n):
    return not isinstance(j, int) or j >= n


class Steps:

    def __init__(self, eng, sem):
        self.eng, self.sem, self.base, self.n = eng, sem, 0, 0

    def did(self, ins):
        self.n += 1
        ins.then_inc(self.sem, 1)

    def wait(self):
        self.eng.wait_ge(self.sem, self.base + self.n)

    def enter(self, i, per):
        self.start, self.per = self.n, per
        self.base, self.n = self.start + i * per, 0

    def leave(self, rounds):
        assert self.n == self.per, (self.n, self.per)
        self.base, self.n = 0, self.start + rounds * self.per


def macaron(nc, x_in, Wq, Wk, Wv, Wo, Wg, W1, b1, W2, b2, rope_c, rope_s, out, parts=("f0", "at", "f1")):
    B, L, D = x_in.shape
    E, _, F = W1.shape
    N = B * L
    NT = N // P
    NC = NT // CH
    FT = F // P
    KT = TOPK * NT
    EB = (E - 1).bit_length()
    NJ = TOPK * N // TILE + E - 1
    NJ += -NJ % 3
    NR = NJ // 3
    NS = NJ * SUB
    H, DK = 16, D // 16
    HW = 32
    G = 4
    QK = 2 * D
    SC = float(DK) ** -0.5
    assert D == P and L == 2 * P

    x_rows = x_in.rearrange("b l d -> (b l) d")
    out_rows = out.rearrange("b l d -> (b l) d")

    ctx = ExitStack()
    with ctx:
        def sb(name, shape, dt):
            return ctx.enter_context(nc.sbuf_tensor(name, shape, dt))

        def sem(name):
            return ctx.enter_context(nc.semaphore(name))

        xn_table = nc.dram_tensor("xn_table", [N, 2 * D], F16, kind="Internal").ap()
        y_table = nc.dram_tensor("y_table", [TOPK * N + NS * P, D], F32, kind="Internal").ap()

        bank = [ctx.enter_context(nc.psum_tensor(f"bank{i}", [P, 512], F32)) for i in range(8)]

        x = sb("x", [P, NT, D], F32)
        stats = sb("stats", [P, CH, 6], F32)
        mean = sb("mean", [P, CH], F32)
        rstd = sb("rstd", [P, CH], F32)
        var = sb("var", [P, CH], F32)
        nrt = sb("nrt", [P, 3, CH], F32)
        ln_a = sb("ln_a", [P, CH], F32)
        ln_b = sb("ln_b", [P, CH], F32)
        ln_c = sb("ln_c", [P, CH], F32)
        ln_d = sb("ln_d", [P, CH], F32)
        warm = sb("warm", [1, 8], F32)
        xf = sb("xf", [P, CH, D], F32)

        ident = sb("ident", [P, P], F32)
        ident_h = sb("ident_h", [P, P], F16)
        ident_b = sb("ident_b", [P, P], BF16)
        below = sb("below", [P, P], F16)
        ones_h = sb("ones_h", [P, P], F16)
        ones_f = sb("ones_f", [P, E * NT], F32)
        iota_lo = sb("iota_lo", [P, P], F16)
        part_c = sb("part_c", [P, 1], F32)
        pow_i = sb("pow_i", [P, KT], I32)
        pow_c = sb("pow_c", [P, KT], F32)
        small = sb("small", [P, 8], F32)
        rank_c = sb("rank_c", [P, E], F32)
        slot_c = sb("slot_c", [P, NS], F32)
        tile_lo = sb("tile_lo", [1, NJ], F32)

        w1_hl = sb("w1_hl", [P, 2, E * F], F16)
        w2_hl = sb("w2_hl", [P, 2, E * F], F16)
        wg_f = sb("wg_f", [P, E], F32)
        wg_hl = sb("wg_hl", [P, 2, E], F16)
        b1_rows = sb("b1_rows", [E * FT, P], F32)
        b1_c = sb("b1_c", [P, E * FT], F32)
        b2_r = sb("b2_r", [P, E * D], F32)

        xn_hl = sb("xn_hl", [P, NT, 2, D], F16)
        xnT = sb("xnT", [P, CH, 2, P], F16)
        lg = sb("lg", [P, NT, E], F32)
        lg2 = sb("lg2", [P, NT, E], F32)
        eq = sb("eq", [P, NT, E], F32)
        top = sb("top", [P, TOPK, NT], F32)
        cmx = sb("cmx", [P, NT], F32)
        oh = sb("oh", [P, TOPK, NT, E], F32)
        member = sb("member", [P, NT, E], F16)
        tot = sb("tot", [P, E, NT], F32)
        cum = sb("cum", [P, E, NT], F32)
        before = sb("before", [P, E], F32)
        cnt = sb("cnt", [P, E], F32)
        cnt_i = sb("cnt_i", [P, E], I32)
        cnt_j = sb("cnt_j", [P, E], I32)
        ends = sb("ends", [P, E], F32)
        off = sb("off", [P, E], F32)
        pos = sb("pos", [P, TOPK, NT], F32)
        pos_i = sb("pos_i", [P, KT], I32)
        half_i = sb("half_i", [P, 2, KT], I32)
        half = sb("half", [P, 2, KT], F32)
        gate = sb("gate", [P, TOPK, NT], F32)
        oh_lo = sb("oh_lo", [P, KT, P], BF16)
        oh_hi = sb("oh_hi", [P, KT, NS], BF16)
        stage = sb("stage", [P, E * F // 2], F32)
        used = sb("used", [P, NS], F32)
        idx = sb("idx", [P, NJ + 6, 2, SUB], U32)
        cur = sb("cur", [P, 3, 2, SUB], U32)
        zero_h = sb("zero_h", [P, P], BF16)
        pos_u = sb("pos_u", [P, NT, TOPK], U32)
        rows_i = sb("rows_i", [P, NS], U32)
        past = sb("past", [1, NJ, E], F32)
        exp_f = sb("exp_f", [1, NJ + 2], F32)
        code_f = sb("code_f", [1, NR], F32)
        code = sb("code", [1, NR], I32)

        xs = sb("xs", [P, 3, SUB, 2 * D], F16)
        xT = sb("xT", [P, 3, 2, TILE], F16)
        hid = sb("hid", [P, 3, FT, TILE], F32)
        hid_hl = sb("hid_hl", [P, 3, 2, FT, TILE], F16)
        ys = sb("ys", [P, 3, SUB, D], F32)
        yc = sb("yc", [P, 2, TOPK, CH // 2, D], F32)

        w_rows = sb("w_rows", [P, 4, D], F32)
        w_qkv = sb("w_qkv", [P, 3 * D], F32)
        w_o = sb("w_o", [P, D], F32)
        cos = sb("cos", [P, 2, DK], F32)
        sin = sb("sin", [P, 2, DK], F32)
        mask_qk = sb("mask_qk", [P, 4, P], BF16)
        mask_kq = sb("mask_kq", [P, 4, P], BF16)
        y_cur = sb("y_cur", [P, 2, 2 * TOPK], U32)
        yg = sb("yg", [P, 2, 2, TOPK, D], F32)
        stats2 = sb("stats2", [P, 2, 2, 6], F32)
        ln_s = sb("ln_s", [P, 8, 2], F32)
        mean_s = sb("mean_s", [P, 2, 2], F32)
        rstd_s = sb("rstd_s", [P, 2, 2], F32)
        xa = sb("xa", [P, 2, D], F32)
        xaT = sb("xaT", [P, L], F32)
        v_tmp = sb("v_tmp", [P, 2, D], F32)
        v_ext = sb("v_ext", [P, 2, 2, H, HW], F32)
        r_a = sb("r_a", [P, 2 * H, DK], F32)
        r_b = sb("r_b", [P, 2 * H, DK], F32)
        rot = sb("rot", [P, 2, 2, H, DK], F32)
        q_s = sb("q_s", [P, 2, 2, H, HW], F16)
        k_s = sb("k_s", [P, 2, H, HW], F16)
        qT, kT, qmT = hid_hl[:, 0], hid_hl[:, 1], hid_hl[:, 2, 0]
        pr = hid[:, :, :, :].rearrange("p a b c -> p (a b c)").rearrange("p (r n k) -> p r n k", r=2, n=3)
        o_sb = xf[:, :, :].rearrange("p a d -> p (a d)").rearrange("p (j s) -> p j s", j=4)
        den = sb("den", [P, 2, 4, G], F32)
        att = sb("att", [P, 2, G, 4, DK], F32)
        attT = sb("attT", [P, L], F32)

        s_x = sem("s_x")
        s_wa = sem("s_wa"); s_wt = sem("s_wt"); s_wtc = sem("s_wtc"); s_aconst = sem("s_aconst"); s_vz = sem("s_vz")
        at = {n: sem(f"at_{n}") for n in (
            "var", "sd", "xa", "xaT", "xaTc", "qkv", "vtmp", "vext", "rot", "hi", "lo", "qkT", "qkTc", "S", "max",
            "qmT", "qmTc", "ST", "exp", "PV", "Oc", "OT", "att", "attT", "attTc", "wo", "xadd", "cur", "yg0", "yg1", "stats", "dev")}
        s_xc = [sem(f"s_xc{c}") for c in range(NC)]
        s_wp = sem("s_wp")
        s_const = sem("s_const")
        s_w1 = sem("s_w1"); s_w2 = sem("s_w2"); s_small = sem("s_small")
        s_w1h = sem("s_w1h"); s_w1l = sem("s_w1l"); s_w2h = sem("s_w2h"); s_w2l = sem("s_w2l")
        s_wg = sem("s_wg"); s_b1 = sem("s_b1")
        s_dve = sem("s_dve")
        s_pool = sem("s_pool"); s_steps = sem("s_steps")
        s_out = sem("s_out")


        def ffn_sems(k):
            one = ("split", "tab", "tr", "trc", "lgt", "member", "count", "top", "gate", "slots", "lo",
                   "hi", "inv", "idx", "rows_in", "xT", "hmm", "gelu", "hs", "ymm", "y", "comb", "cur")
            f = {name: sem(f"f{k}_{name}") for name in one}
            f["got"] = [sem(f"f{k}_got{u}") for u in range(3)]
            f["put"] = [sem(f"f{k}_put{u}") for u in range(3)]
            f["yc"] = [sem(f"f{k}_yc{u}") for u in range(2)]
            return f

        ffns = [ffn_sems(0), ffn_sems(1)]
        todo = [k for k in range(2) if f"f{k}" in parts]

        def wait(eng, name, value):
            if not isinstance(value, int) or value > 0:
                eng.wait_ge(at[name], value)

        def sequences(eng, turn, st=None, per=0):
            def at_b(b):
                turn(b, b % 2, lambda k: 0 <= b + k < B, lambda k: (b + k) // 2)
            for b in range(-4, 2):
                at_b(b)
            rounds = (B - 6) // 2
            with eng.Fori(0, rounds) as i:
                if st is not None:
                    st.enter(i, 2 * per)
                for u in range(2):
                    turn(2 * i + u + 2, u, lambda k: True, lambda k, u=u: i + (u + 2 + k) // 2)
            if st is not None:
                st.leave(rounds)
            for b in range(B - 4, B + 1):
                at_b(b)

        def experts(eng, i):
            word = eng.value_load(code[0:1, bass.ds(i, 1)])
            return [(word >> n * EB if n else word) & ((1 << EB) - 1) for n in range(5)]

        def weight_halves():
            return [(w, slice(n * E * F // 2, (n + 1) * E * F // 2)) for w in (w1_hl, w2_hl) for n in range(2)]

        EVEN_M, HALF, QUARTER, PER_D, EPS_K, MINUS, MAGIC, THREE = range(8)
        SMALL = (0.0, 0.5, D / 4.0, 1.0 / D, EPS, -0.5, float(0x5F3759DF), 1.5)

        def deviation(eng, st, st6, work, mean_out, rstd_out, n, settle=None):
            def c(k):
                return small[:, k:k + 1].broadcast_to([P, n])

            def tt(out_ap, a, b_ap, op, hold=True):
                ins = eng.tensor_tensor(out_ap, a, b_ap, op)
                if hold:
                    st.did(ins)
                    st.wait()
                return ins

            w = work
            even, odd = st6[:, :, 1], st6[:, :, 4]
            tt(w[0], even, odd, ALU.add, False)
            tt(w[1], even, odd, ALU.subtract, False)
            tt(w[2], st6[:, :, 2], st6[:, :, 5], ALU.add)
            tt(mean_out, w[0], c(HALF), ALU.mult, False)
            tt(w[3], w[1], w[1], ALU.mult)
            tt(w[1], w[3], c(QUARTER), ALU.mult)
            tt(w[3], w[1], w[2], ALU.add)
            tt(w[1], w[3], c(PER_D), ALU.mult)
            tt(w[2], w[1], c(EPS_K), ALU.add)
            if settle is None:
                tt(w[0], w[2].bitcast(I32), c(MINUS), ALU.mult, False)
                tt(w[3], w[2], c(MINUS), ALU.mult)
                tt(rstd_out.bitcast(I32), w[0], c(MAGIC), ALU.add)
            else:
                settle()
                st.did(eng.tensor_copy(w[0], w[2].bitcast(I32)))
                tt(w[3], w[2], c(MINUS), ALU.mult)
                tt(w[1], w[0], c(MINUS), ALU.mult)
                tt(w[0], w[1], c(MAGIC), ALU.add)
                settle()
                st.did(eng.tensor_copy(rstd_out.bitcast(I32), w[0]))
                st.wait()
            for k in range(3):
                tt(w[0], rstd_out, rstd_out, ALU.mult)
                tt(w[1], w[0], w[3], ALU.mult)
                tt(w[2], w[1], c(THREE), ALU.add)
                ins = tt(rstd_out, rstd_out, w[2], ALU.mult, k < 2)
            return ins

        DEV_STEPS = 18
        DEV_STEPS_P = 22

        block = ctx.enter_context(nc.Block())

        @block.sync
        def _(sp):
            for c in range(NC):
                sp.dma_start(x[:, c * CH:(c + 1) * CH, :],
                             x_rows[c * CH * P:(c + 1) * CH * P, :].rearrange("(t p) d -> p t d", p=P)).then_inc(s_xc[c], 16)
            sp.dma_start(wg_f[:, :], Wg).then_inc(s_small, 16)
            sp.dma_start(b1_rows[:, :], b1.rearrange("e (t p) -> (e t) p", p=P)).then_inc(s_small, 16)
            sp.dma_start(b2_r[:, :], b2.rearrange("(o e) d -> o (e d)", o=1).broadcast_to([P, E * D])).then_inc(s_small, 16)
            for n, w in enumerate((Wq, Wk, Wv, Wo)):
                sp.dma_start(w_rows[:, n, :], w).then_inc(s_wa, 16)
            for t, r in ((cos, rope_c), (sin, rope_s)):
                sp.dma_start(t[:, :, :], r.rearrange("(t p) d -> p t d", p=P)).then_inc(s_wa, 16)
            for n in range(4):
                if n > 0:
                    sp.wait_ge(s_w1h, n)
                    sp.wait_ge(s_w1l, n)
                e = slice(n % 2 * E // 2, (n % 2 + 1) * E // 2)
                if n < 2:
                    sp.dma_start(stage[:, :].rearrange("p (e f) -> p e f", e=E // 2), W1[e].rearrange("e d f -> d e f")).then_inc(s_w1, 16)
                else:
                    sp.dma_start(stage[:, :].rearrange("p (e t d) -> p e t d", e=E // 2, t=FT),
                                 W2[e].rearrange("e (t p) d -> p e t d", p=P)).then_inc(s_w1, 16)

            def attention():
                pass

            def ffn(k):
                f = ffns[k]
                with sp.Fori(0, NC) as c:
                    sp.wait_ge(f["split"], c + 1)
                    sp.dma_start(xn_table.rearrange("(c t p) w -> c p t w", p=P, t=CH)[bass.ds(c, 1)].rearrange("c p t w -> p (c t) w"),
                                 xn_hl[:, bass.ds(c * CH, CH), :, :].rearrange("p t h d -> p t (h d)")).then_inc(f["tab"], 16)
                if k == 0:
                    def leave(j, u):
                        sp.wait_ge(f["y"], j + 1)
                        sp.dma_start(y_table.rearrange("(j s p) d -> j p s d", p=P, s=SUB)[bass.ds(j, 1)].rearrange("j p s d -> p (j s) d"),
                                     ys[:, u, :, :]).then_inc(f["put"][u], 16)

                    with sp.Fori(0, NR) as i:
                        for u in range(3):
                            leave(3 * i + u, u)
                    return
                for u in range(3):
                    sp.wait_ge(f["put"][u], 32 * NR)
                yt = y_table[0:TOPK * N, :].rearrange("(k c t p) d -> k c p t d", k=TOPK, t=CH // 2, p=P)

                def fetch(c, u):
                    for kk in range(TOPK):
                        sp.dma_start(yc[:, u, kk, :, :], yt[kk][bass.ds(c, 1)].rearrange("c p t d -> p (c t) d")).then_inc(f["yc"][u], 16)

                fetch(0, 0)
                fetch(1, 1)
                with sp.Fori(1, NC) as i:
                    for u in range(2):
                        sp.wait_ge(f["comb"], 2 * i + u - 1)
                        fetch(2 * i + u, u)

            def store(k):
                if k is None:
                    sp.wait_ge(at["xadd"], B)
                    sp.dma_start(out_rows.rearrange("(t p) d -> p t d", p=P), x[:, :, :]).then_inc(s_out, 16)
                    sp.wait_ge(s_out, 16)
                    return
                f = ffns[k]
                with sp.Fori(0, 2 * NC) as c:
                    sp.wait_ge(f["comb"], c + 1)
                    sp.dma_start(out_rows.rearrange("(c t p) d -> c p t d", p=P, t=CH // 2)[bass.ds(c, 1)].rearrange("c p t d -> p (c t) d"),
                                 x[:, bass.ds(c * (CH // 2), CH // 2), :]).then_inc(s_out, 16)
                sp.wait_ge(s_out, 16 * 2 * NC)

            for phase in parts:
                if phase == "at":
                    attention()
                else:
                    ffn(int(phase[1]))
            store(1 if 'f1' in parts else None if 'at' in parts else 0)

        @block.gpsimd
        def _(pool):
            st = Steps(pool, s_pool)
            for k, value in enumerate(SMALL):
                pool.memset(small[:, k:k + 1], value)
            for m in (ident, ident_h, ident_b, zero_h):
                st.did(pool.memset(m[:, :], 0.0))
            st.did(pool.memset(below[:, :], 1.0))
            pool.memset(ones_h[:, :], 1.0)
            pool.memset(ones_f[:, :], 1.0)
            st.wait()
            for m in (ident, ident_h, ident_b):
                pool.affine_select(out=m[:, :], in_=m[:, :], compare_op=ALU.not_equal, fill=1.0, base=0,
                                   pattern=[[-1, P]], channel_multiplier=1)
            pool.affine_select(out=below[:, :], in_=below[:, :], compare_op=ALU.is_gt, fill=0.0, base=0,
                               pattern=[[1, P]], channel_multiplier=-1)
            iota = dict(allow_small_or_imprecise_dtypes=True)
            pool.iota(iota_lo[:, :], pattern=[[1, P]], base=0, channel_multiplier=0, **iota)
            pool.iota(part_c[:, :], pattern=[[0, 1]], base=P, channel_multiplier=1, **iota)
            pool.iota(pow_i[:, :], pattern=[[1, KT]], base=127 - 6, channel_multiplier=0)
            pool.iota(rank_c[:, :], pattern=[[-1, E]], base=E, channel_multiplier=0, **iota)
            pool.iota(slot_c[:, :], pattern=[[P, NS]], base=TOPK * N, channel_multiplier=1, **iota)
            pool.iota(tile_lo[:, :], pattern=[[TILE, NJ]], base=0, channel_multiplier=0, **iota).then_inc(s_const, 1)
            st.did(pool.memset(mask_qk[:, :, :], 0.0))
            st.did(pool.memset(mask_kq[:, :, :], 0.0))
            pool.memset(q_s[:, :, :, :, :], 0.0)
            st.did(pool.memset(k_s[:, :, :, :], 0.0))
            st.did(pool.memset(v_ext[:, :, :, :, :], 0.0))
            st.wait()
            pool.affine_select(out=mask_qk[:, :, :], in_=mask_qk[:, :, :], compare_op=ALU.is_ge, fill=-1e9, base=0,
                               pattern=[[0, 4], [-1, P]], channel_multiplier=1)
            pool.affine_select(out=mask_kq[:, :, :], in_=mask_kq[:, :, :], compare_op=ALU.is_ge, fill=-1e9, base=0,
                               pattern=[[0, 4], [1, P]], channel_multiplier=-1)
            pool.memset(k_s[:, :, :, 3 * DK], 1.0)
            pool.memset(v_ext[:, :, :, :, DK], 1.0).then_inc(s_aconst, 1)
            for n, (w, c) in enumerate(weight_halves()):
                pool.wait_ge(s_w1h, n + 1)
                pool.tensor_tensor(w[:, 1, c], stage[:, :], w[:, 0, c], ALU.subtract).then_inc(s_w1l, 1)

            def settle(j):
                if not isinstance(j, int):
                    pool.sem_inc(s_steps, 1)

            def attention():
                y_rows = y_table[0:NS * P, :]
                yg_sem = (at["yg0"], at["yg1"])

                def turn(b, par, has, pair):
                    if has(4):
                        if not isinstance(b, int) or b >= -2:
                            pool.wait_ge(yg_sem[par], 64 * pair(4))
                        pool.tensor_copy(y_cur[:, par, :], pos_u[:, bass.ds(2 * (b + 4), 2), :].rearrange("p t k -> p (t k)")).then_inc(at["cur"], 1)
                        wait(pool, "stats", b + 3)
                        pool.wait_ge(at["cur"], b + 5)
                        settle(b)
                        for t in range(2):
                            for kk in range(TOPK):
                                n = t * TOPK + kk
                                pool.indirect_dma_start(out=yg[:, par, t, kk, :], out_offset=None, in_=y_rows,
                                                        in_offset=Offset(ap=y_cur[:, par, n:n + 1], axis=0)).then_inc(yg_sem[par], 16)
                    if has(3):
                        pool.wait_ge(at["stats"], b + 4)
                        deviation(pool, st, stats2[:, 1 - par, :, :], [ln_s[:, k, :] for k in range(4)],
                                  mean_s[:, 1 - par, :], rstd_s[:, 1 - par, :], 2, lambda: settle(b)).then_inc(at["dev"], 1)
                    if has(2):
                        wait(pool, "PV", 4 * (b + 1))
                        pool.wait_ge(at["vtmp"], 2 * (b + 3))
                        settle(b)
                        pool.tensor_copy(v_ext[:, par, :, :, 0:DK],
                                         v_tmp[:, :, :].rearrange("p t (h d) -> p t h d", d=DK)).then_inc(at["vext"], 1)
                for u in range(3):
                    pool.wait_ge(ffns[0]["put"][u], 16 * NR)
                sequences(pool, turn, st, DEV_STEPS_P)

            def ffn(k):
                f = ffns[k]
                pool.wait_ge(f["idx"], 1)
                pool.wait_ge(f["tab"], 16 * NC)

                def pick(j, u):
                    pool.tensor_copy(cur[:, u, :, :].rearrange("p a b -> p (a b)"),
                                     idx[:, bass.ds(j, 1), :, :].rearrange("p j a b -> p (j a b)")).then_inc(f["cur"], 1)

                def gather(j, u):
                    pool.wait_ge(f["tab"], 16 * NC)
                    settle(j)
                    for h in range(SUB):
                        pool.indirect_dma_start(out=xs[:, u, h, :], out_offset=None, in_=xn_table,
                                                in_offset=Offset(ap=cur[:, u, 0, h:h + 1], axis=0)).then_inc(f["got"][u], 16)

                def scatter(j, u):
                    pool.wait_ge(f["y"], j - 5)
                    settle(j)
                    for h in range(SUB):
                        pool.indirect_dma_start(out=y_table, out_offset=Offset(ap=cur[:, u, 1, h:h + 1], axis=0),
                                                in_=ys[:, u, h, :], in_offset=None).then_inc(f["put"][u], 16)

                pick(0, 0)
                for j in range(3):
                    if j < 2:
                        pick(j + 1, j + 1)
                    pool.wait_ge(f["cur"], j + 1)
                    gather(j, j)
                
                def step(i, u):
                    j = 3 * i + u
                    pool.wait_ge(f["got"][u], 32 * i)
                    if k > 0 and later(i, 3):
                        pool.wait_ge(f["put"][u], 32 * (i - 2))
                    pick(j, u)
                    pool.wait_ge(f["rows_in"], j - 2)
                    pool.wait_ge(f["cur"], j + 1)
                    gather(j, u)
                    if k > 0 and later(i, 2):
                        scatter(j, u)

                for j in range(3, 9):
                    step(j // 3, j % 3)
                with pool.Fori(3, NR) as i:
                    for u in range(3):
                        step(i, u)
                for j in range(NJ, NJ + 6 if k > 0 else NJ):
                    i, u = divmod(j, 3)
                    pool.wait_ge(f["got"][u], 32 * NR)
                    pool.wait_ge(f["put"][u], 32 * (i - 2))
                    pick(j, u)
                    pool.wait_ge(f["cur"], j + 1)
                    scatter(j, u)

            for phase in parts:
                if phase == "at":
                    attention()
                else:
                    ffn(int(phase[1]))

        @block.tensor
        def _(pe):
            pe.wait_ge(s_const, 1)
            pe.wait_ge(s_small, 48)
            pe.transpose(bank[5][:, 0:E * FT], b1_rows[:, :], ident[0:E * FT, 0:E * FT]).then_inc(s_b1, 1)

            def h16(b):
                return bank[b][:, :].bitcast(F16)

            def attention():
                pe.wait_ge(s_wa, 16 * 6)
                pe.wait_ge(s_b1, 2)
                for n in range(4):
                    ins = pe.transpose(bank[5][:, n * D:(n + 1) * D], w_rows[:, n, :], ident[:, :])
                ins.then_inc(s_wt, 1)
                pe.wait_ge(s_wtc, 1)
                pe.wait_ge(s_aconst, 1)

                def job_s(b, par, n):
                    j, part = (n // 3 + 2) % 4, n % 3
                    wait(pe, "max", 12 * b + n - 1)
                    r = slice(HW * j, HW * j + 3 * DK)
                    dst = bank[n % 2]
                    if part == 0:
                        pe.matmul(dst[:, :], ident_b[:, :], mask_qk[:, :, :], start=True, stop=False, skip_group_check=True)
                        for g in range(G):
                            ins = pe.matmul(dst[:, g * P:(g + 1) * P], qT[r, par, g, 0:P], kT[r, par, g, 0:P],
                                            start=False, stop=True, skip_group_check=True)
                    else:
                        pe.matmul(dst[:, :].rearrange("p (g k) -> p g k", g=2)[:, :, P:L], ident_b[:, :], mask_qk[:, 0:2, :],
                                  start=True, stop=False, skip_group_check=True)
                        for gg in range(2):
                            g = 2 * (part - 1) + gg
                            ins = pe.matmul(dst[:, gg * L:(gg + 1) * L], qT[r, par, g, P:L], kT[r, par, g, :],
                                            start=False, stop=True, skip_group_check=True)
                    ins.then_inc(at["S"], 1)

                def job_st(b, par, n):
                    j, part = n // 3, n % 3
                    wait(pe, "exp", 12 * b + n - 1)
                    r = slice(HW * j, HW * (j + 1))
                    dst = bank[2 + n % 2]
                    if part == 0:
                        pe.matmul(dst[:, :], ident_b[:, :], mask_kq[:, :, :], start=True, stop=False, skip_group_check=True)
                        for g in range(G):
                            ins = pe.matmul(dst[:, g * P:(g + 1) * P], kT[r, par, g, P:L], qmT[r, g, P:L],
                                            start=False, stop=True, skip_group_check=True)
                    else:
                        pe.matmul(dst[:, :].rearrange("p (g q) -> p g q", g=2)[:, :, 0:P], ident_b[:, :], mask_kq[:, 0:2, :],
                                  start=True, stop=False, skip_group_check=True)
                        for gg in range(2):
                            g = 2 * (part - 1) + gg
                            ins = pe.matmul(dst[:, gg * L:(gg + 1) * L], kT[r, par, g, 0:P], qmT[r, g, :],
                                            start=False, stop=True, skip_group_check=True)
                    ins.then_inc(at["ST"], 1)

                def job_pv(b, par, j):
                    pe.wait_ge(at["exp"], 12 * b + 3 * j + 3)
                    pe.wait_ge(at["vext"], b + 1)
                    wait(pe, "Oc", 4 * b + j)
                    for g in range(G):
                        c = slice(HW * g, HW * (g + 1))
                        pe.matmul(bank[4][c, 0:L], v_ext[:, par, 0, 4 * g + j, :],
                                  pr[:, j % 2, 1 + g // 2, (g % 2) * L:(g % 2 + 1) * L], start=True, stop=False)
                    for g in range(G):
                        c = slice(HW * g, HW * (g + 1))
                        ins = pe.matmul(bank[4][c, P:L], v_ext[:, par, 1, 4 * g + j, :],
                                        pr[:, j % 2, 0, g * P:(g + 1) * P], start=False, stop=True)
                    ins.then_inc(at["PV"], 1)

                def turn(b, par, has, pair):
                    scores, maxima, front, back = has(0), has(1), has(2), has(-1)
                    if back:
                        pe.wait_ge(at["Oc"], 4 * b)
                        wait(pe, "qkTc", 2 * (b + 2) if not isinstance(b, int) or b + 1 < B else 2 * B)
                        for j in range(4):
                            for t in range(2):
                                ins = pe.transpose(bank[6 + t][:, j * P:(j + 1) * P], o_sb[:, j, t * P:(t + 1) * P], ident[:, :])
                        ins.then_inc(at["OT"], 1)
                    for n in range(12):
                        if scores:
                            if n == 0:
                                pe.wait_ge(at["qmTc"], b + 1)
                            job_st(b, par, n)
                        if maxima:
                            if n == 0:
                                pe.wait_ge(at["qkTc"], 2 * (b + 2))
                            job_s(b + 1, 1 - par, n)
                        if scores and n % 3 == 0 and n > 0:
                            job_pv(b, par, n // 3 - 1)
                        if front and n == 1:
                            pe.wait_ge(at["xa"], b + 3)
                            wait(pe, "qmTc", b + 1)
                            for t in range(2):
                                ins = pe.transpose(bank[5][:, t * P:(t + 1) * P], xa[:, t, :], ident[:, :])
                            ins.then_inc(at["xaT"], 1)
                        if back and n == 2:
                            pe.wait_ge(at["att"], b)
                            wait(pe, "xaTc", b + 3 if front else B)
                            for t in range(2):
                                ins = pe.transpose(bank[5][:, t * P:(t + 1) * P],
                                                   att[:, t, :, :, :].rearrange("p g j d -> p (g j d)"), ident[:, :])
                            ins.then_inc(at["attT"], 1)
                        if front and n == 4:
                            pe.wait_ge(at["xaTc"], b + 3)
                            wait(pe, "qkTc", 2 * (b + 2))
                            wait(pe, "att", b)
                            for t in range(2):
                                pe.matmul(bank[6 + t][:, 0:3 * D], xaT[:, t * P:(t + 1) * P], w_qkv[:, :],
                                          start=True, stop=True).then_inc(at["qkv"], 1)
                        if back and n == 5:
                            pe.wait_ge(at["attTc"], b)
                            for t in range(2):
                                ins = pe.matmul(bank[5][:, t * P:(t + 1) * P], attT[:, t * P:(t + 1) * P], w_o[:, :],
                                                start=True, stop=True)
                            ins.then_inc(at["wo"], 1)
                    if scores:
                        job_pv(b, par, 3)
                    if front:
                        for t in range(2):
                            pe.wait_ge(at["lo"], 2 * (b + 2) + t + 1)
                            for g in range(G):
                                c = slice(4 * g, 4 * g + 4)
                                pe.transpose(h16(6 + t)[:, g * P:(g + 1) * P],
                                             q_s[:, par, t, c, :].rearrange("p h w -> p (h w)"), ident_h[:, :])
                                ins = pe.transpose(h16(6 + t)[:, (G + g) * P:(G + g + 1) * P],
                                                   k_s[:, t, c, :].rearrange("p h w -> p (h w)"), ident_h[:, :])
                            ins.then_inc(at["qkT"], 1)
                    if maxima:
                        pe.wait_ge(at["max"], 12 * (b + 2))
                        wait(pe, "xadd", b)
                        wait(pe, "xaTc", b + 3 if front else B)
                        for t in range(2):
                            for g in range(G):
                                ins = pe.transpose(h16(5)[:, g * L + t * P:g * L + (t + 1) * P],
                                                   q_s[:, 1 - par, t, 4 * g:4 * g + 4, :].rearrange("p h w -> p (h w)"),
                                                   ident_h[:, :])
                        ins.then_inc(at["qmT"], 1)

                sequences(pe, turn)

            def ffn(k):
                f = ffns[k]
                with pe.Fori(0, NC) as c:
                    pe.wait_ge(f["split"], c + 1)
                    for t in range(CH):
                        for h in range(2):
                            ins = pe.transpose(h16(t // 4)[:, (t % 4 * 2 + h) * P:(t % 4 * 2 + h + 1) * P],
                                               xn_hl[:, bass.ds(c * CH + t, 1), h, :].rearrange("p a d -> p (a d)"), ident_h[:, :])
                        if t % 4 == 3:
                            ins.then_inc(f["tr"], 1)
                    if k == 0:
                        pe.wait_ge(s_wg, 3)
                    for t in range(CH):
                        if t % 4 == 0:
                            pe.wait_ge(f["trc"], c * 2 + t // 4 + 1)
                        dst = bank[2][:, bass.ds((c * CH + t) * E, E)]
                        pe.matmul(dst, xnT[:, t, 0, :], wg_hl[:, 0, :], start=True, stop=False)
                        pe.matmul(dst, xnT[:, t, 1, :], wg_hl[:, 0, :], start=False, stop=False)
                        ins = pe.matmul(dst, xnT[:, t, 0, :], wg_hl[:, 1, :], start=False, stop=True)
                    ins.then_inc(f["lgt"], 1)
                pe.wait_ge(f["member"], 1)
                m = member[:, :, :].rearrange("p t e -> p e t")
                pe.matmul(bank[3][:, 0:E * NT], below[:, :], m, start=True, stop=True)
                pe.matmul(bank[3][:, E * NT:2 * E * NT], ones_h[:, :], m, start=True, stop=True).then_inc(f["count"], 1)
                inv = bank[4][:, 0:NS]
                pe.wait_ge(f["lo"], 1)
                pe.matmul(inv, zero_h[:, :], oh_hi[:, 0, :], start=True, stop=False)
                with pe.Fori(0, KT // 8) as i:
                    pe.wait_ge(f["lo"], i + 1)
                    for mm in range(8):
                        kt = i * 8 + mm
                        pe.matmul(inv, oh_lo[:, bass.ds(kt, 1), :].rearrange("p a s -> p (a s)"),
                                  oh_hi[:, bass.ds(kt, 1), :].rearrange("p a s -> p (a s)"), start=False, stop=False)
                pe.matmul(inv, zero_h[:, :], oh_hi[:, 0, :], start=False, stop=True).then_inc(f["inv"], 1)

                pe.wait_ge(f["idx"], 1)
                if k == 0:
                    pe.wait_ge(s_w1l, 4)
                    pe.wait_ge(s_b1, 2)

                def turn(j, u, i):
                    pe.wait_ge(f["got"][u], 32 * (i + 1))
                    if later(j, 1):
                        pe.wait_ge(f["xT"], j)
                    for s in range(SUB):
                        for h in range(2):
                            ins = pe.transpose(h16(6)[:, h * TILE + s * P:h * TILE + (s + 1) * P],
                                               xs[:, u, s, h * P:(h + 1) * P], ident_h[:, :])
                    ins.then_inc(f["rows_in"], 1)

                def first(j, u, ex):
                    pe.wait_ge(f["xT"], j + 1)
                    if later(j, 3):
                        pe.wait_ge(f["gelu"], j - 2)
                    for ft in range(FT):
                        dst = bank[2 * u + ft // 2][:, (ft % 2) * TILE:(ft % 2 + 1) * TILE]
                        w = [w1_hl[:, h, bass.ds(ex * F + ft * P, P)] for h in range(2)]
                        pe.matmul(dst, w[0], xT[:, u, 0, :], start=True, stop=False)
                        pe.matmul(dst, w[0], xT[:, u, 1, :], start=False, stop=False)
                        ins = pe.matmul(dst, w[1], xT[:, u, 0, :], start=False, stop=True)
                    ins.then_inc(f["hmm"], 1)

                def second(j, u, ex):
                    pe.wait_ge(f["hs"], j + 1)
                    if later(j, 1):
                        pe.wait_ge(f["y"], j)
                    for s in range(SUB):
                        dst = bank[7][:, s * D:(s + 1) * D]
                        for ft in range(FT):
                            hh = [hid_hl[:, u, h, ft, s * P:(s + 1) * P] for h in range(2)]
                            w = [w2_hl[:, h, bass.ds(ex * F + ft * D, D)] for h in range(2)]
                            pe.matmul(dst, hh[0], w[0], start=(ft == 0), stop=False)
                            pe.matmul(dst, hh[0], w[1], start=False, stop=False)
                            ins = pe.matmul(dst, hh[1], w[0], start=False, stop=(ft == FT - 1))
                    ins.then_inc(f["ymm"], 1)

                def steps(i, head=False, tail=False):
                    ex = experts(pe, i)
                    for u in range(3):
                        j = 3 * i + u
                        first(j, u, ex[u + 2])
                        if not (tail and u == 2):
                            turn(j + 1, (u + 1) % 3, i + (u == 2))
                        if not (head and u < 2):
                            second(j - 2, (u + 1) % 3, ex[u])
                    return ex[3:]

                turn(0, 0, 0)
                steps(0, head=True)
                with pe.Fori(1, NR - 1) as i:
                    steps(i)
                for n, ex in enumerate(steps(NR - 1, tail=True)):
                    second(NJ - 2 + n, 1 + n, ex)

            for phase in parts:
                if phase == "at":
                    attention()
                else:
                    ffn(int(phase[1]))

        @block.scalar
        def _(act):
            act.wait_ge(s_const, 1)
            act.wait_ge(s_small, 48)
            act.activation(wg_hl[:, 0, :], wg_f[:, :], ACT.Copy).then_inc(s_wg, 2)
            act.wait_ge(s_b1, 1)
            act.activation(b1_c[:, :], bank[5][:, 0:E * FT], ACT.Copy).then_inc(s_b1, 1)

            def attention():
                act.wait_ge(s_wt, 1)
                act.activation(w_qkv[:, :], bank[5][:, 0:3 * D], ACT.Copy)
                act.activation(w_o[:, :], bank[5][:, 3 * D:4 * D], ACT.Copy).then_inc(s_wtc, 1)
                act.activation(warm[0:1, 7:8], ident[0:1, 0:1], ACT.Exp)
                act.wait_ge(s_aconst, 1)

                def outputs(b, j):
                    act.wait_ge(at["PV"], 4 * b + j + 1)
                    if j == 0:
                        wait(act, "OT", b)
                    act.activation(o_sb[:, j, :], bank[4][:, 0:L], ACT.Copy).then_inc(at["Oc"], 1)

                def turn(b, par, has, pair):
                    scores, maxima, front, back = has(0), has(1), has(2), has(-1)
                    for n in range(12):
                        if scores:
                            j, part = n // 3, n % 3
                            act.wait_ge(at["ST"], 12 * b + n + 1)
                            wait(act, "PV", 4 * b + j - 1)
                            act.activation(pr[:, j % 2, part, :], bank[2 + n % 2][:, :], ACT.Exp, scale=SC).then_inc(at["exp"], 1)
                            if n % 3 == 1 and n > 3:
                                outputs(b, n // 3 - 1)
                        if front and n == 1:
                            act.wait_ge(at["xaT"], b + 3)
                            wait(act, "qkv", 2 * (b + 2))
                            act.activation(xaT[:, :], bank[5][:, 0:L], ACT.Copy).then_inc(at["xaTc"], 1)
                        if back and n == 2:
                            act.wait_ge(at["attT"], b)
                            wait(act, "wo", b - 1)
                            act.activation(attT[:, :], bank[5][:, 0:L], ACT.Copy).then_inc(at["attTc"], 1)
                        if front and n == 4:
                            wait(act, "vext", b + 2)
                            for t in range(2):
                                act.wait_ge(at["qkv"], 2 * (b + 2) + t + 1)
                                act.activation(v_tmp[:, t, :], bank[6 + t][:, 2 * D:3 * D], ACT.Copy).then_inc(at["vtmp"], 1)
                        if front and n in (6, 8):
                            t = n // 2 - 3
                            act.wait_ge(at["rot"], 2 * (b + 2) + t + 1)
                            wait(act, "qmT", b + 1)
                            wait(act, "qkT", 2 * (b + 2))
                            act.activation(q_s[:, par, t, :, 0:2 * DK].rearrange("p h (c d) -> p h c d", c=2),
                                           rot[:, t, 0, :, :].unsqueeze(2).broadcast_to([P, H, 2, DK]), ACT.Copy)
                            act.activation(k_s[:, t, :, 0:4 * DK].rearrange("p h (c d) -> p h c d", c=4)[:, :, 0:3:2, :],
                                           rot[:, t, 1, :, :].unsqueeze(2).broadcast_to([P, H, 2, DK]),
                                           ACT.Copy).then_inc(at["hi"], 1)
                    if scores:
                        outputs(b, 3)
                    if front:
                        act.wait_ge(at["qkT"], 2 * (b + 2) + 2)
                        wait(act, "ST", 12 * (b + 1))
                        wait(act, "S", 12 * (b + 1))
                        for dst, first in ((qT, 0), (kT, G)):
                            ins = act.activation(dst[:, par, :, P:L], bank[7][:, :].bitcast(F16)[:, first * P:(first + G) * P]
                                                 .rearrange("p (g s) -> p g s", g=G), ACT.Copy)
                        ins.then_inc(at["qkTc"], 1)
                    if maxima:
                        act.wait_ge(at["qmT"], b + 2)
                        wait(act, "ST", 12 * (b + 1))
                        act.activation(qmT[:, :, :].rearrange("p g s -> p (g s)"), bank[5][:, :].bitcast(F16), ACT.Copy).then_inc(at["qmTc"], 1)

                sequences(act, turn)

            def ffn(k):
                f = ffns[k]
                with act.Fori(0, NC) as c:
                    for q in range(2):
                        act.wait_ge(f["tr"], 2 * c + q + 1)
                        act.activation(xnT[:, 4 * q:4 * q + 4, :, :].rearrange("p a b c -> p (a b c)"),
                                       bank[q][:, :].bitcast(F16), ACT.Copy).then_inc(f["trc"], 1)
                act.wait_ge(f["top"], 1)
                act.activation(gate[:, :, :], top[:, :, :], ACT.Sigmoid).then_inc(f["gate"], 1)

                if k == 0:
                    for n, (w, c) in enumerate(weight_halves()):
                        act.wait_ge(s_w1, 16 * (n + 1))
                        act.activation(w[:, 0, c], stage[:, :], ACT.Copy).then_inc(s_w1h, 1)
                act.activation(warm[0:1, 3 * k + 1:3 * k + 2], ident[0:1, 0:1], ACT.Gelu_apprx_tanh)
                act.wait_ge(f["idx"], 1)

                def gelu(j, u, ex):
                    act.wait_ge(f["hmm"], j + 1)
                    if later(j, 3):
                        act.wait_ge(f["hs"], j - 2)
                    for ft in range(FT):
                        ins = act.activation(hid[:, u, ft, :], bank[2 * u + ft // 2][:, (ft % 2) * TILE:(ft % 2 + 1) * TILE],
                                             ACT.Gelu_apprx_tanh, bias=b1_c[:, bass.ds(ex * FT + ft, 1)])
                    ins.then_inc(f["gelu"], 1)

                def steps(i):
                    ex = experts(act, i)
                    for u in range(3):
                        gelu(3 * i + u, u, ex[u + 2])

                steps(0)
                with act.Fori(1, NR) as i:
                    steps(i)

            for phase in parts:
                if phase == "at":
                    attention()
                else:
                    ffn(int(phase[1]))

        @block.vector
        def _(dve):
            st = Steps(dve, s_dve)
            dve.memset(idx[:, :, :, :], 0)
            dve.memset(exp_f[:, :], 0.0)
            st.did(dve.memset(before[:, :], 0.0))
            st.wait()
            dve.wait_ge(s_small, 48)
            dve.wait_ge(s_wg, 2)
            dve.tensor_tensor(wg_hl[:, 1, :], wg_f[:, :], wg_hl[:, 0, :], ALU.subtract).then_inc(s_wg, 1)
            dve.wait_ge(s_const, 1)
            st.did(dve.tensor_scalar(pow_c[:, :].bitcast(I32), pow_i[:, :], 23, None, ALU.logical_shift_left))

            def norm(c):
                for t in range(CH):
                    ins = dve.bn_stats(stats[:, t, :], x[:, bass.ds(c * CH + t, 1), :].rearrange("p a d -> p (a d)"))
                st.did(ins)
                st.wait()
                st.did(deviation(dve, st, stats[:, :, :], [ln_a[:, :], ln_b[:, :], ln_c[:, :], ln_d[:, :]],
                                 mean[:, :], rstd[:, :], CH))
                st.wait()
                for t in range(CH):
                    ins = dve.tensor_scalar(xf[:, t, :], x[:, bass.ds(c * CH + t, 1), :].rearrange("p a d -> p (a d)"),
                                            mean[:, t:t + 1], rstd[:, t:t + 1], ALU.subtract, ALU.mult)
                st.did(ins)
                st.wait()

            def attention():
                dve.wait_ge(s_aconst, 1)
                dve.wait_ge(s_wa, 16 * 6)

                def maximum(b, par, n):
                    j, part = (n // 3 + 2) % 4, n % 3
                    dve.wait_ge(at["S"], 12 * b + n + 1)
                    t, g0, ng = (0, 0, G) if part == 0 else (1, 2 * (part - 1), 2)
                    dst = q_s[:, par, t, :, 3 * DK].rearrange("p (g j) -> p g j", g=G)[:, g0:g0 + ng, j]
                    dve.tensor_reduce(dst, bank[n % 2][:, :].rearrange("p (g k) -> p g k", g=ng), AX.X, ALU.max,
                                      negate=True).then_inc(at["max"], 1)

                def row(t):
                    return x[:, bass.ds(t, 1), :].rearrange("p a d -> p (a d)")

                def combine(b, par, n):
                    dve.wait_ge((at["yg0"], at["yg1"])[par], 64 * (n + 1))
                    for kk in range(TOPK):
                        for t in range(2):
                            tt = 2 * b + t
                            ins = dve.scalar_tensor_tensor(out=row(tt), in0=yg[:, par, t, kk, :], scalar=gate[:, kk, bass.ds(tt, 1)],
                                                           in1=row(tt), op0=ALU.mult, op1=ALU.add)
                        st.did(ins)
                        st.wait()
                    wait(dve, "dev", b - 1)
                    if not isinstance(b, int):
                        dve.sem_inc(s_x, 1)
                    for t in range(2):
                        ins = dve.bn_stats(stats2[:, par, t, :], row(2 * b + t))
                    ins.then_inc(at["stats"], 1)

                def rope(b, t):
                    dve.wait_ge(at["qkv"], 2 * b + t + 1)
                    dve.wait_ge(at["vtmp"], 2 * b + t + 1)
                    wait(dve, "lo", 2 * b + t - 1)
                    wait(dve, "hi", 2 * b + t - 1)
                    src = bank[6 + t][:, 0:QK].rearrange("p (h d) -> p h d", d=DK)
                    c = cos[:, t, :].unsqueeze(1).broadcast_to([P, 2 * H, DK])
                    s = sin[:, t, :].rearrange("p (i c) -> p i c", c=2)
                    dve.tensor_tensor(r_a[:, :, :], src, c, ALU.mult)
                    pairs = src.rearrange("p h (i c) -> p h i c", c=2)
                    rb = r_b[:, :, :].rearrange("p h (i c) -> p h i c", c=2)
                    for c in range(2):
                        ins = dve.tensor_tensor(rb[:, :, :, c], pairs[:, :, :, 1 - c],
                                                s[:, :, c].unsqueeze(1).broadcast_to([P, 2 * H, DK // 2]), ALU.mult)
                    st.did(ins)
                    st.wait()
                    dve.tensor_tensor(rot[:, t, :, :, :].rearrange("p a h d -> p (a h) d"), r_a[:, :, :], r_b[:, :, :],
                                      ALU.add).then_inc(at["rot"], 1)
                    dve.wait_ge(at["rot"], 2 * b + t + 1)

                def low(b, par, t):
                    dve.wait_ge(at["hi"], 2 * b + t + 1)
                    dve.tensor_tensor(q_s[:, par, t, :, 2 * DK:3 * DK], rot[:, t, 0, :, :], q_s[:, par, t, :, 0:DK], ALU.subtract)
                    dve.tensor_tensor(k_s[:, t, :, DK:2 * DK], rot[:, t, 1, :, :], k_s[:, t, :, 0:DK],
                                      ALU.subtract).then_inc(at["lo"], 1)

                def turn(b, par, has, pair):
                    scores, maxima, front, back = has(0), has(1), has(2), has(-1)
                    if front:
                        wait(dve, "xaT", b + 2)
                        dve.wait_ge(at["dev"], b + 3)
                        for t in range(2):
                            ins = dve.tensor_scalar(xa[:, t, :], row(2 * (b + 2) + t), mean_s[:, par, t:t + 1],
                                                    rstd_s[:, par, t:t + 1], ALU.subtract, ALU.mult)
                        ins.then_inc(at["xa"], 1)
                    if back:
                        dve.wait_ge(at["OT"], b)
                        wait(dve, "attT", b - 1)
                        views = [bank[6 + t][:, :].rearrange("p (j g w) -> p j g w", j=4, g=G) for t in range(2)]
                        for t in range(2):
                            ins = dve.reciprocal(den[:, t, :, :], views[t][:, :, :, DK])
                        st.did(ins)
                        st.wait()
                        for t in range(2):
                            ins = dve.tensor_tensor(att[:, t, :, :, :].rearrange("p g j d -> p j g d"), views[t][:, :, :, 0:DK],
                                                    den[:, t, :, :].unsqueeze(3).broadcast_to([P, 4, G, DK]), ALU.mult)
                        ins.then_inc(at["att"], 1)
                    for n in range(12):
                        if maxima:
                            maximum(b + 1, 1 - par, n)
                        if back and n == 5:
                            dve.wait_ge(at["wo"], b)
                            xt = x[:, bass.ds(2 * (b - 1), 2), :]
                            dve.tensor_tensor(xt, bank[5][:, 0:L].rearrange("p (t d) -> p t d", t=2), xt, ALU.add).then_inc(at["xadd"], 1)
                        if front and n in (4, 6):
                            rope(b + 2, n // 2 - 2)
                        if front and n in (7, 8):
                            low(b + 2, par, n - 7)
                        if has(3) and n == 1:
                            combine(b + 3, 1 - par, pair(3))
                    if front:
                        dve.wait_ge(at["qkT"], 2 * (b + 2) + 1)
                        wait(dve, "ST", 12 * (b + 1))
                        wait(dve, "S", 12 * (b + 1))
                        for dst, first in ((qT, 0), (kT, G)):
                            ins = dve.tensor_copy(dst[:, par, :, 0:P], bank[6][:, :].bitcast(F16)[:, first * P:(first + G) * P]
                                                  .rearrange("p (g s) -> p g s", g=G))
                        ins.then_inc(at["qkTc"], 1)

                sequences(dve, turn, st, 5)
                dve.wait_ge(at["xadd"], B)

            def ffn(k):
                f = ffns[k]
                def chunk(c):
                    if k == 0:
                        dve.wait_ge(s_xc[c], 16)
                    norm(c)
                    hi = xn_hl[:, bass.ds(c * CH, CH), 0, :]
                    lo = xn_hl[:, bass.ds(c * CH, CH), 1, :]
                    st.did(dve.tensor_copy(hi, xf[:, :, :]))
                    st.wait()
                    dve.tensor_tensor(lo, xf[:, :, :], hi, ALU.subtract).then_inc(f["split"], 1)

                if k == 0:
                    for c in range(NC):
                        chunk(c)
                else:
                    with dve.Fori(0, NC) as c:
                        st.enter(c, DEV_STEPS + 5)
                        chunk(c)
                    st.leave(NC)

                dve.wait_ge(f["lgt"], NC)
                st.did(dve.tensor_scalar(lg[:, :, :].rearrange("p t e -> p (t e)"), bank[2][:, 0:NT * E], SAT, None, ALU.min))
                rank_b = rank_c[:, :].unsqueeze(1).broadcast_to([P, NT, E])

                def over_e(a):
                    return a.unsqueeze(2).broadcast_to([P, NT, E])

                dve.wait_ge(s_const, 1)
                for kk, src in enumerate((lg, lg2)):
                    st.wait()
                    st.did(dve.tensor_reduce(top[:, kk, :], src[:, :, :], AX.X, ALU.max))
                    st.wait()
                    st.did(dve.tensor_tensor(eq[:, :, :], src[:, :, :], over_e(top[:, kk, :]), ALU.is_equal))
                    st.wait()
                    st.did(dve.tensor_tensor(eq[:, :, :], eq[:, :, :], rank_b, ALU.mult))
                    st.wait()
                    st.did(dve.tensor_reduce(cmx[:, :], eq[:, :, :], AX.X, ALU.max))
                    st.wait()
                    st.did(dve.tensor_tensor(oh[:, kk, :, :], rank_b, over_e(cmx[:, :]), ALU.is_equal))
                    st.wait()
                    if kk == 0:
                        st.did(dve.scalar_tensor_tensor(out=lg2[:, :, :], in0=oh[:, 0, :, :], scalar=-BIG, in1=lg[:, :, :],
                                                        op0=ALU.mult, op1=ALU.add))
                dve.tensor_tensor(member[:, :, :], oh[:, 0, :, :], oh[:, 1, :, :], ALU.add).then_inc(f["member"], 1)
                dve.nop().then_inc(f["top"], 1)

                dve.wait_ge(f["count"], 1)
                st.did(dve.tensor_copy(tot[:, :, :].rearrange("p e t -> p (e t)"), bank[3][:, E * NT:2 * E * NT]))
                st.wait()
                st.did(dve.tensor_tensor_scan(cum[:, :, :].rearrange("p e t -> p (e t)"), ones_f[:, :],
                                              tot[:, :, :].rearrange("p e t -> p (e t)"), 0.0, ALU.mult, ALU.add))
                st.wait()
                st.did(dve.tensor_copy(before[:, 1:E], cum[:, 0:E - 1, NT - 1]))
                dve.tensor_tensor(tot[:, :, :], cum[:, :, :], tot[:, :, :], ALU.subtract)
                st.wait()
                st.did(dve.tensor_tensor(cnt[:, :], cum[:, :, NT - 1], before[:, :], ALU.subtract))
                st.wait()
                st.did(dve.tensor_scalar(cnt_i[:, :], cnt[:, :], float(TILE - 1), None, ALU.add))
                st.wait()
                shift = TILE.bit_length() - 1
                st.did(dve.tensor_scalar(cnt_j[:, :], cnt_i[:, :], shift, shift, ALU.logical_shift_right, ALU.logical_shift_left))
                st.wait()
                st.did(dve.tensor_copy(cnt[:, :], cnt_j[:, :]))
                st.wait()
                st.did(dve.tensor_tensor_scan(ends[:, :], ones_f[:, 0:E], cnt[:, :], 0.0, ALU.mult, ALU.add))
                st.wait()
                st.did(dve.tensor_tensor(off[:, :], ends[:, :], cnt[:, :], ALU.subtract))
                st.wait()
                st.did(dve.tensor_tensor(off[:, :], off[:, :], before[:, :], ALU.subtract))
                st.wait()
                st.did(dve.tensor_tensor(tot[:, :, :], tot[:, :, :], off[:, :].unsqueeze(2).broadcast_to([P, E, NT]), ALU.add))
                st.wait()
                st.did(dve.tensor_tensor(cum[:, :, :].rearrange("p e t -> p (e t)"), bank[3][:, 0:E * NT],
                                         tot[:, :, :].rearrange("p e t -> p (e t)"), ALU.add))
                for kk, tmp in enumerate((eq, lg2)):
                    st.wait()
                    st.did(dve.tensor_tensor(tmp[:, :, :], oh[:, kk, :, :], cum[:, :, :].rearrange("p e t -> p t e"), ALU.mult))
                for kk, tmp in enumerate((eq, lg2)):
                    st.wait()
                    st.did(dve.tensor_reduce(pos[:, kk, :], tmp[:, :, :], AX.X, ALU.add))
                st.wait()
                st.did(dve.tensor_copy(pos_i[:, :], pos[:, :, :].rearrange("p k t -> p (k t)")))
                st.did(dve.tensor_copy(pos_u[:, :, :], pos[:, :, :].rearrange("p k t -> p t k")))
                st.wait()
                lop = P.bit_length() - 1
                st.did(dve.tensor_scalar(half_i[:, 0, :], pos_i[:, :], lop, 0, ALU.logical_shift_right, ALU.logical_shift_left))
                st.did(dve.tensor_scalar(half_i[:, 1, :], pos_i[:, :], 32 - lop, 32 - lop, ALU.logical_shift_left, ALU.logical_shift_right))
                st.wait()
                dve.tensor_copy(half[:, :, :], half_i[:, :, :]).then_inc(f["slots"], 1)
                st.did(dve.tensor_tensor(past[:, :, :], ends[0:1, :].unsqueeze(1).broadcast_to([1, NJ, E]),
                                         tile_lo[:, :].unsqueeze(2).broadcast_to([1, NJ, E]), ALU.is_le))
                st.wait()
                st.did(dve.tensor_reduce(exp_f[:, 2:NJ + 2], past[:, :, :], AX.X, ALU.add))
                st.wait()
                st.did(dve.tensor_scalar(exp_f[:, 2:NJ + 2], exp_f[:, 2:NJ + 2], float(E - 1), None, ALU.min))
                st.wait()
                st.did(dve.tensor_copy(code_f[:, :], exp_f[:, 4:NJ + 2:3]))
                for n in (3, 2, 1, 0):
                    st.wait()
                    st.did(dve.scalar_tensor_tensor(out=(code if n == 0 else code_f)[:, :], in0=code_f[:, :], scalar=float(1 << EB),
                                                    in1=exp_f[:, n:n + 3 * NR - 2:3], op0=ALU.mult, op1=ALU.add))

                dve.wait_ge(f["slots"], 1)
                with dve.Fori(0, KT // 8) as i:
                    for m in range(8):
                        kt = i * 8 + m
                        dve.tensor_scalar(oh_lo[:, bass.ds(kt, 1), :].rearrange("p a s -> p (a s)"), iota_lo[:, :],
                                          half[:, 1, bass.ds(kt, 1)], part_c[:, 0:1], ALU.is_equal, ALU.mult)
                        ins = dve.tensor_scalar(oh_hi[:, bass.ds(kt, 1), :].rearrange("p a s -> p (a s)"), iota_lo[:, 0:NS],
                                                half[:, 0, bass.ds(kt, 1)], pow_c[:, bass.ds(kt, 1)], ALU.is_equal, ALU.mult)
                    ins.then_inc(f["lo"], 1)
                dve.wait_ge(f["gate"], 1)
                st.did(dve.tensor_scalar(gate[:, :, :], gate[:, :, :], 0.5, None, ALU.mult))

                dve.wait_ge(f["inv"], 1)
                found = bank[4][:, 0:NS]
                st.did(dve.tensor_scalar(used[:, :], found, 0.0, None, ALU.is_equal))
                st.did(dve.tensor_scalar(rows_i[:, :], found.bitcast(U32), 16, TOPK * N - 1, ALU.logical_shift_right, ALU.bitwise_and))
                st.wait()
                st.did(dve.tensor_tensor(used[:, :], used[:, :], slot_c[:, :], ALU.mult))
                st.wait()
                st.did(dve.tensor_tensor(idx[:, 6:NJ + 6, 1, :], used[:, :].rearrange("p (j s) -> p j s", s=SUB),
                                         rows_i[:, :].rearrange("p (j s) -> p j s", s=SUB), ALU.add))
                dve.tensor_scalar(idx[:, 0:NJ, 0, :], rows_i[:, :].rearrange("p (j s) -> p j s", s=SUB), N - 1, None,
                                  ALU.bitwise_and).then_inc(f["idx"], 1)
                st.wait()

                def load_x(j, u):
                    dve.wait_ge(f["rows_in"], j + 1)
                    if later(j, 3):
                        dve.wait_ge(f["hmm"], j - 2)
                    dve.tensor_copy(xT[:, u, :, :].rearrange("p h s -> p (h s)"),
                                    bank[6][:, :].bitcast(F16)[:, 0:2 * TILE]).then_inc(f["xT"], 1)

                def split(j, u):
                    dve.wait_ge(f["gelu"], j + 1)
                    if later(j, 3):
                        dve.wait_ge(f["ymm"], j - 2)
                    st.did(dve.tensor_copy(hid_hl[:, u, 0, :, :], hid[:, u, :, :]))
                    st.wait()
                    dve.tensor_tensor(hid_hl[:, u, 1, :, :], hid[:, u, :, :], hid_hl[:, u, 0, :, :], ALU.subtract).then_inc(f["hs"], 1)

                def leave(j, u, i, ex):
                    dve.wait_ge(f["ymm"], j + 1)
                    if later(i, 1):
                        dve.wait_ge(f["put"][u], (16 if k == 0 else 32) * i)
                    dve.tensor_tensor(ys[:, u, :, :], bank[7][:, 0:SUB * D].rearrange("p (s d) -> p s d", s=SUB),
                                      b2_r[:, bass.ds(ex * D, D)].unsqueeze(1).broadcast_to([P, SUB, D]),
                                      ALU.add).then_inc(f["y"], 1)

                def steps(i, head=False, tail=False):
                    ex = None if head else experts(dve, i - 1)[2:]
                    for u in range(3):
                        j = 3 * i + u
                        if not head:
                            leave(j - 3, u, i - 1, ex[u])
                        if not (tail and u == 2):
                            load_x(j + 1, (u + 1) % 3)
                        if not (head and u == 0):
                            split(j - 1, (u + 2) % 3)

                load_x(0, 0)
                steps(0, head=True)
                steps(1)
                with dve.Fori(2, NR - 1) as i:
                    st.enter(i - 2, 3)
                    steps(i)
                st.leave(NR - 3)
                steps(NR - 1, tail=True)
                split(NJ - 1, 2)
                for u, ex in enumerate(experts(dve, NR - 1)[2:]):
                    leave(NJ - 3 + u, u, NR - 1, ex)

                if k == 0:
                    return
                with dve.Fori(0, NC) as i:
                    st.enter(i, 2)
                    for u in range(2):
                        c = 2 * i + u
                        dve.wait_ge(f["yc"][u], 32 * i + 32)
                        for kk in range(TOPK):
                            for t in range(CH // 2):
                                tt = c * (CH // 2) + t
                                xt = x[:, bass.ds(tt, 1), :].rearrange("p a d -> p (a d)")
                                ins = dve.scalar_tensor_tensor(out=xt, in0=yc[:, u, kk, t, :], scalar=gate[:, kk, bass.ds(tt, 1)],
                                                               in1=xt, op0=ALU.mult, op1=ALU.add)
                            if kk == 0:
                                st.did(ins)
                                st.wait()
                        ins.then_inc(f["comb"], 1)
                st.leave(NC)
                dve.wait_ge(f["comb"], 2 * NC)

            for phase in parts:
                if phase == "at":
                    attention()
                else:
                    ffn(int(phase[1]))


_INS = ["L0_attn_x", "L0_attn_Wq", "L0_attn_Wk", "L0_attn_Wv", "L0_attn_Wo", "L0_ffn_Wg",
        "L0_ffn_W1", "L0_ffn_b1", "L0_ffn_W2", "L0_ffn_b2"]


def rope_tables(length, dk, theta=10000.0):
    f = np.float32
    rates = f(theta) ** (-(f(2.0) * np.arange(dk // 2, dtype=f)) / f(dk))
    angles = np.arange(length, dtype=f)[:, None] * rates[None, :].astype(f)
    cos, sin = np.cos(angles), np.sin(angles)
    return (np.repeat(cos, 2, axis=1).astype(f), np.stack([-sin, sin], axis=-1).reshape(length, dk).astype(f))


def kernel(**inputs):
    import concourse.bacc as bacc
    from concourse.bass_utils import run_bass_kernel_spmd

    nc = bacc.Bacc("TRN2", target_bir_lowering=False, num_devices=1)
    given = {name: np.ascontiguousarray(inputs[name]) for name in _INS}
    B, L, D = given["L0_attn_x"].shape
    given["rope_c"], given["rope_s"] = rope_tables(L, D // 16)
    arrays, args = {}, []
    for name, a in given.items():
        arrays[f"in_{name}"] = a
        args.append(nc.dram_tensor(f"in_{name}", a.shape, mybir.dt.from_np(a.dtype), kind="ExternalInput").ap())
    out = nc.dram_tensor("out_0", (B, L, D), F32, kind="ExternalOutput").ap()
    macaron(nc, *args, out)
    r = run_bass_kernel_spmd(nc, [arrays], core_ids=[0])
    return r.results[0]["out_0"]
```

```python
from contextlib import ExitStack

import numpy as np

import concourse.bass as bass
from concourse import mybir

F32, F16, BF16 = mybir.dt.float32, mybir.dt.float16, mybir.dt.bfloat16
I32, U32 = mybir.dt.int32, mybir.dt.uint32
ALU, ACT, AX = mybir.AluOpType, mybir.ActivationFunctionType, mybir.AxisListType
Offset = bass.IndirectOffsetOnAxis

P = 128
EPS = 1e-5
TOPK = 2
TILE = 256
SUB = TILE // P
SAT = 16.635532
BIG = 1e30
CH = 8


def later(j, n):
    return not isinstance(j, int) or j >= n


class Steps:

    def __init__(self, eng, sem):
        self.eng, self.sem, self.base, self.n = eng, sem, 0, 0

    def did(self, ins):
        self.n += 1
        ins.then_inc(self.sem, 1)

    def wait(self):
        self.eng.wait_ge(self.sem, self.base + self.n)

    def enter(self, i, per):
        self.start, self.per = self.n, per
        self.base, self.n = self.start + i * per, 0

    def leave(self, rounds):
        assert self.n == self.per, (self.n, self.per)
        self.base, self.n = 0, self.start + rounds * self.per


def macaron(nc, x_in, Wq, Wk, Wv, Wo, Wg, W1, b1, W2, b2, rope_c, rope_s, out):
    B, L, D = x_in.shape
    E, _, F = W1.shape
    N = B * L
    NT = N // P
    NC = NT // CH
    FT = F // P
    KT = TOPK * NT
    EB = (E - 1).bit_length()
    NJ = TOPK * N // TILE + E - 1
    NJ += -NJ % 3
    NR = NJ // 3
    NS = NJ * SUB
    H, DK = 16, D // 16
    HW = 32
    G = 4
    QK = 2 * D
    SC = float(DK) ** -0.5
    assert D == P and L == 2 * P

    x_rows = x_in.rearrange("b l d -> (b l) d")
    out_rows = out.rearrange("b l d -> (b l) d")

    ctx = ExitStack()
    with ctx:
        def sb(name, shape, dt):
            return ctx.enter_context(nc.sbuf_tensor(name, shape, dt))

        def sem(name):
            return ctx.enter_context(nc.semaphore(name))

        xn_table = nc.dram_tensor("xn_table", [N, 2 * D], F16, kind="Internal").ap()
        y_table = nc.dram_tensor("y_table", [TOPK * N + NS * P, D], F32, kind="Internal").ap()

        bank = [ctx.enter_context(nc.psum_tensor(f"bank{i}", [P, 512], F32)) for i in range(8)]

        x = sb("x", [P, NT, D], F32)
        stats = sb("stats", [P, 2 * CH, 6], F32)
        mean = sb("mean", [P, 2 * CH], F32)
        rstd = sb("rstd", [P, 2 * CH], F32)
        ln_w = sb("ln_w", [P, 4, 2 * CH], F32)
        warm = sb("warm", [1, 8], F32)

        ident = sb("ident", [P, P], F32)
        ident_h = sb("ident_h", [P, P], F16)
        ident_b = sb("ident_b", [P, P], BF16)
        below = sb("below", [P, P], F16)
        ones_h = sb("ones_h", [P, P], F16)
        ones_f = sb("ones_f", [P, E * NT], F32)
        iota_lo = sb("iota_lo", [P, P], BF16)
        part_c = sb("part_c", [P, 1], F32)
        pow_i = sb("pow_i", [P, KT], I32)
        pow_c = sb("pow_c", [P, KT], F32)
        small = sb("small", [P, 8], F32)
        rank_c = sb("rank_c", [P, E], F32)
        slot_c = sb("slot_c", [P, NS], F32)
        tile_lo = sb("tile_lo", [1, NJ], F32)

        w1_hl = sb("w1_hl", [P, 2, E * F], F16)
        w2_hl = sb("w2_hl", [P, 2, E * F], F16)
        wg_f = sb("wg_f", [P, E], F32)
        wg_hl = sb("wg_hl", [P, 2, E], F16)
        b1_rows = sb("b1_rows", [E * FT, P], F32)
        b1_c = sb("b1_c", [P, E * FT], F32)
        b2_r = sb("b2_r", [P, E * D], F32)

        xn_hl = sb("xn_hl", [P, NT, 2, D], F16)
        xnT = sb("xnT", [P, 2, CH, 2, P], F16)
        lg = sb("lg", [P, NT, E], F32)
        lg2 = sb("lg2", [P, NT, E], F32)
        eq = sb("eq", [P, NT, E], F32)
        top = sb("top", [P, TOPK, NT], F32)
        cmx = sb("cmx", [P, NT], F32)
        oh = sb("oh", [P, TOPK, NT, E], F32)
        member = sb("member", [P, NT, E], F16)
        tot = sb("tot", [P, E, NT], F32)
        cum = sb("cum", [P, E, NT], F32)
        before = sb("before", [P, E], F32)
        cnt = sb("cnt", [P, E], F32)
        cnt_i = sb("cnt_i", [P, E], I32)
        cnt_j = sb("cnt_j", [P, E], I32)
        ends = sb("ends", [P, E], F32)
        off = sb("off", [P, E], F32)
        pos = sb("pos", [P, TOPK, NT], F32)
        pos_i = sb("pos_i", [P, KT], I32)
        half_i = sb("half_i", [P, 2, KT], I32)
        half = sb("half", [P, 2, KT], BF16)
        gate = sb("gate", [P, TOPK, NT], F32)
        oh_lo = sb("oh_lo", [P, KT, P], BF16)
        oh_hi = sb("oh_hi", [P, KT, NS], BF16)
        stage = sb("stage", [P, 2, E * F // 2], F32)
        used = sb("used", [P, NS], F32)
        idx = sb("idx", [P, NJ + 6, 2, SUB], U32)
        cur = sb("cur", [P, 3, 2, SUB], U32)
        zero_h = sb("zero_h", [P, P], BF16)
        pos_u = sb("pos_u", [P, NT, TOPK], U32)
        rows_i = sb("rows_i", [P, NS], U32)
        past = sb("past", [1, NJ, E], F32)
        exp_f = sb("exp_f", [1, NJ + 2], F32)
        code_f = sb("code_f", [1, NR], F32)
        code = sb("code", [1, NR], I32)

        xs = sb("xs", [P, 3, SUB, 2 * D], F16)
        xT = sb("xT", [P, 3, 2, TILE], F16)
        hid = sb("hid", [P, 3, FT, TILE], F32)
        hid_hl = sb("hid_hl", [P, 3, 2, FT, TILE], F16)
        ys = sb("ys", [P, 3, SUB, D], F32)

        w_rows = sb("w_rows", [P, 4, D], F32)
        w_qkv = sb("w_qkv", [P, 3 * D], F32)
        w_o = sb("w_o", [P, D], F32)
        cos = sb("cos", [P, 2, DK], F32)
        sin = sb("sin", [P, 2, DK], F32)
        mask_qk = sb("mask_qk", [P, 4, P], BF16)
        mask_kq = sb("mask_kq", [P, 4, P], BF16)
        y_cur = sb("y_cur", [P, 2, 2 * TOPK], U32)
        yg = sb("yg", [P, 2, 2, TOPK, D], F32)
        stats2 = sb("stats2", [P, 2, 4, 6], F32)
        ln_s = sb("ln_s", [P, 4, 4], F32)
        mean_s = sb("mean_s", [P, 2, 4], F32)
        rstd_s = sb("rstd_s", [P, 2, 4], F32)
        xo = sb("xo", [P, 2, D], F32)
        xa = sb("xa", [P, 2, D], F32)
        xaT = sb("xaT", [P, L], F32)
        v_tmp = sb("v_tmp", [P, 2, D], F32)
        v_ext = sb("v_ext", [P, 2, 2, H, HW], F32)
        r_a = sb("r_a", [P, 2 * H, DK], F32)
        r_b = sb("r_b", [P, 2 * H, DK], F32)
        rot = sb("rot", [P, 2, 2, H, DK], F32)
        q_s = sb("q_s", [P, 2, 2, H, HW], F16)
        k_s = sb("k_s", [P, 2, H, HW], F16)
        qT, kT, qmT = hid_hl[:, 0], hid_hl[:, 1], hid_hl[:, 2, 0]
        pr = hid[:, :, :, :].rearrange("p a b c -> p (a b c)").rearrange("p (r n k) -> p r n k", r=2, n=3)
        o_sb = sb("o_sb", [P, 2, 2, L], F32)
        den = sb("den", [P, 4 * G, 2], F32)
        att = sb("att", [P, 2, G, 4, DK], F32)
        attT = sb("attT", [P, L], F32)

        s_wa, s_wt, s_wtc = sem("s_wa"), sem("s_wt"), sem("s_wtc")
        s_aconst = sem("s_aconst")
        at = {n: sem(f"at_{n}") for n in (
            "xa", "xaT", "xaTc", "qkv", "vtmp", "vext", "rot", "hi", "lo", "qkT", "qkTc", "S", "max",
            "qmT", "qmTc", "ST", "exp", "PV", "Oc", "OT", "att", "attT", "attTc", "wo", "xadd", "cur", "yg0", "yg1", "stats", "dev")}
        s_xc = [sem(f"s_xc{c}") for c in range(NC)]
        s_const = sem("s_const")
        s_half = [sem(f"s_half{n}") for n in range(2)]
        s_high, s_low = sem("s_high"), sem("s_low")
        s_small = sem("s_small")
        s_wg, s_b1 = sem("s_wg"), sem("s_b1")
        s_dve, s_pool = sem("s_dve"), sem("s_pool")
        s_dve_held, s_pool_held = sem("s_dve_held"), sem("s_pool_held")
        s_out = sem("s_out")

        def ffn_sems(k):
            one = ("first", "second", "norm", "high", "split", "tab", "tr", "trc", "lgt", "member", "count", "top", "gate", "slots", "lo",
                   "hi", "inv", "idx", "rows_in", "xT", "hmm", "gelu", "hs", "ymm", "y", "comb", "cur")
            f = {name: sem(f"f{k}_{name}") for name in one}
            f["got"] = [sem(f"f{k}_got{u}") for u in range(3)]
            f["put"] = [sem(f"f{k}_put{u}") for u in range(3)]
            f["yc"] = [sem(f"f{k}_yc{u}") for u in range(2 * NC)] if k else None
            return f

        ffns = [ffn_sems(0), ffn_sems(1)]

        def wait(eng, name, value):
            if not isinstance(value, int) or value > 0:
                eng.wait_ge(at[name], value)

        def sequences(eng, turn, st=None, per=0):
            def at_b(b):
                turn(b, b % 2, lambda k: 0 <= b + k < B, lambda k: (b + k) // 2)
            for b in range(-4, 4):
                at_b(b)
            rounds = (B - 8) // 2
            with eng.Fori(0, rounds) as i:
                if st is not None:
                    st.enter(i, 2 * per)
                for u in range(2):
                    turn(2 * i + u + 4, u, lambda k: True, lambda k, u=u: i + (u + 4 + k) // 2)
            if st is not None:
                st.leave(rounds)
            for b in range(B - 4, B + 3):
                at_b(b)

        def idle(b):
            return isinstance(b, int) and (b < -1 or b >= B + 1)

        def experts(eng, i):
            word = eng.value_load(code[0:1, bass.ds(i, 1)])
            return [(word >> n * EB if n else word) & ((1 << EB) - 1) for n in range(5)]

        def yc(c):
            w = (w1_hl, w2_hl)[c // NC][:, :, :].rearrange("p a b -> p (a b)").bitcast(F32)
            size = TOPK * CH // 2 * D
            return w[:, c % NC * size:(c % NC + 1) * size].rearrange("p (k t d) -> p k t d", k=TOPK, t=CH // 2)

        def xf0(c):
            return hid[:, c % 3, :, :].rearrange("p a b -> p (a b)").rearrange("p (t d) -> p t d", d=D)

        def weight_halves():
            return [(w, slice(n * E * F // 2, (n + 1) * E * F // 2)) for w in (w1_hl, w2_hl) for n in range(2)]

        HALF, QUARTER, PER_D, EPS_K, MINUS, MAGIC, THREE = range(7)
        SMALL = (0.5, D / 4.0, 1.0 / D, EPS, -0.5, float(0x5F3759DF), 1.5)

        def deviation(eng, st, st6, work, mean_out, rstd_out, n, settle=None):
            def c(k):
                return small[:, k:k + 1].broadcast_to([P, n])

            def tt(out_ap, a, b_ap, op, hold=True):
                ins = eng.tensor_tensor(out_ap, a, b_ap, op)
                if hold:
                    st.did(ins)
                    st.wait()
                return ins

            w = work
            even, odd = st6[:, :, 1], st6[:, :, 4]
            tt(w[0], even, odd, ALU.add, False)
            tt(w[1], even, odd, ALU.subtract, False)
            tt(w[2], st6[:, :, 2], st6[:, :, 5], ALU.add)
            tt(mean_out, w[0], c(HALF), ALU.mult, False)
            tt(w[3], w[1], w[1], ALU.mult)
            tt(w[1], w[3], c(QUARTER), ALU.mult)
            tt(w[3], w[1], w[2], ALU.add)
            tt(w[1], w[3], c(PER_D), ALU.mult)
            tt(w[2], w[1], c(EPS_K), ALU.add)
            if settle is None:
                tt(w[0], w[2].bitcast(I32), c(MINUS), ALU.mult, False)
                tt(w[3], w[2], c(MINUS), ALU.mult)
                tt(rstd_out.bitcast(I32), w[0], c(MAGIC), ALU.add)
            else:
                settle()
                st.did(eng.tensor_copy(w[0], w[2].bitcast(I32)))
                tt(w[3], w[2], c(MINUS), ALU.mult)
                tt(w[1], w[0], c(MINUS), ALU.mult)
                tt(w[0], w[1], c(MAGIC), ALU.add)
                settle()
                st.did(eng.tensor_copy(rstd_out.bitcast(I32), w[0]))
                st.wait()
            for k in range(3):
                tt(w[0], rstd_out, rstd_out, ALU.mult)
                tt(w[1], w[0], w[3], ALU.mult)
                tt(w[2], w[1], c(THREE), ALU.add)
                ins = tt(rstd_out, rstd_out, w[2], ALU.mult, k < 2)
            return ins

        DEV_STEPS = 18
        DEV_STEPS_P = 22

        block = ctx.enter_context(nc.Block())

        @block.sync
        def _(sp):
            for c in range(NC):
                sp.dma_start(x[:, c * CH:(c + 1) * CH, :],
                             x_rows[c * CH * P:(c + 1) * CH * P, :].rearrange("(t p) d -> p t d", p=P)).then_inc(s_xc[c], 16)
            sp.dma_start(wg_f[:, :], Wg).then_inc(s_small, 16)
            sp.dma_start(b1_rows[:, :], b1.rearrange("e (t p) -> (e t) p", p=P)).then_inc(s_small, 16)
            sp.dma_start(b2_r[:, :], b2.rearrange("(o e) d -> o (e d)", o=1).broadcast_to([P, E * D])).then_inc(s_small, 16)
            for n, w in enumerate((Wq, Wk, Wv, Wo)):
                sp.dma_start(w_rows[:, n, :], w).then_inc(s_wa, 16)
            for t, r in ((cos, rope_c), (sin, rope_s)):
                sp.dma_start(t[:, :, :], r.rearrange("(t p) d -> p t d", p=P)).then_inc(s_wa, 16)
            for n in range(4):
                if n > 1:
                    sp.wait_ge(s_high, n - 1)
                    sp.wait_ge(s_low, n - 1)
                e = slice(n % 2 * E // 2, (n % 2 + 1) * E // 2)
                if n < 2:
                    sp.dma_start(stage[:, n % 2, :].rearrange("p (e f) -> p e f", e=E // 2), W1[e].rearrange("e d f -> d e f")).then_inc(s_half[n % 2], 16)
                else:
                    sp.dma_start(stage[:, n % 2, :].rearrange("p (e t d) -> p e t d", e=E // 2, t=FT),
                                 W2[e].rearrange("e (t p) d -> p e t d", p=P)).then_inc(s_half[n % 2], 16)

            def ffn(k):
                f = ffns[k]
                with sp.Fori(0, NC) as c:
                    sp.wait_ge(f["split"], (c + 1) * (CH // 2 if k else 1))
                    sp.dma_start(xn_table.rearrange("(c t p) w -> c p t w", p=P, t=CH)[bass.ds(c, 1)].rearrange("c p t w -> p (c t) w"),
                                 xn_hl[:, bass.ds(c * CH, CH), :, :].rearrange("p t h d -> p t (h d)")).then_inc(f["tab"], 16)
                if k == 0:
                    def leave(j, u):
                        sp.wait_ge(f["y"], j + 1)
                        sp.dma_start(y_table.rearrange("(j s p) d -> j p s d", p=P, s=SUB)[bass.ds(j, 1)].rearrange("j p s d -> p (j s) d"),
                                     ys[:, u, :, :]).then_inc(f["put"][u], 16)

                    with sp.Fori(0, NR) as i:
                        for u in range(3):
                            leave(3 * i + u, u)
                    return
                for u in range(3):
                    sp.wait_ge(f["put"][u], 32 * NR)
                yt = y_table[0:TOPK * N, :].rearrange("(k c t p) d -> k c p t d", k=TOPK, t=CH // 2, p=P)

                for c in range(2 * NC):
                    for kk in range(TOPK):
                        sp.dma_start(yc(c)[:, kk, :, :], yt[kk, c]).then_inc(f["yc"][c], 16)

            ffn(0)
            ffn(1)
            with sp.Fori(0, 2 * NC) as c:
                sp.wait_ge(ffns[1]["comb"], c + 1)
                sp.dma_start(out_rows.rearrange("(c t p) d -> c p t d", p=P, t=CH // 2)[bass.ds(c, 1)].rearrange("c p t d -> p (c t) d"),
                             x[:, bass.ds(c * (CH // 2), CH // 2), :]).then_inc(s_out, 16)
            sp.wait_ge(s_out, 16 * 2 * NC)

        @block.gpsimd
        def _(pool):
            st = Steps(pool, s_pool)
            for k, value in enumerate(SMALL):
                pool.memset(small[:, k:k + 1], value)
            for m in (ident, ident_h, ident_b, zero_h):
                st.did(pool.memset(m[:, :], 0.0))
            st.did(pool.memset(below[:, :], 1.0))
            pool.memset(ones_h[:, :], 1.0)
            pool.memset(ones_f[:, :], 1.0)
            st.wait()
            for m in (ident, ident_h, ident_b):
                pool.affine_select(out=m[:, :], in_=m[:, :], compare_op=ALU.not_equal, fill=1.0, base=0,
                                   pattern=[[-1, P]], channel_multiplier=1)
            pool.affine_select(out=below[:, :], in_=below[:, :], compare_op=ALU.is_gt, fill=0.0, base=0,
                               pattern=[[1, P]], channel_multiplier=-1)
            iota = dict(allow_small_or_imprecise_dtypes=True)
            pool.iota(iota_lo[:, :], pattern=[[1, P]], base=0, channel_multiplier=0, **iota)
            pool.iota(part_c[:, :], pattern=[[0, 1]], base=P, channel_multiplier=1, **iota)
            pool.iota(pow_i[:, :], pattern=[[1, KT]], base=127 - 6, channel_multiplier=0)
            pool.iota(rank_c[:, :], pattern=[[-1, E]], base=E, channel_multiplier=0, **iota)
            pool.iota(slot_c[:, :], pattern=[[P, NS]], base=TOPK * N, channel_multiplier=1, **iota)
            pool.iota(tile_lo[:, :], pattern=[[TILE, NJ]], base=0, channel_multiplier=0, **iota).then_inc(s_const, 1)
            st.did(pool.memset(mask_qk[:, :, :], 0.0))
            st.did(pool.memset(mask_kq[:, :, :], 0.0))
            pool.memset(q_s[:, :, :, :, :], 0.0)
            st.did(pool.memset(k_s[:, :, :, :], 0.0))
            st.did(pool.memset(v_ext[:, :, :, :, :], 0.0))
            st.wait()
            pool.affine_select(out=mask_qk[:, :, :], in_=mask_qk[:, :, :], compare_op=ALU.is_ge, fill=-1e9, base=0,
                               pattern=[[0, 4], [-1, P]], channel_multiplier=1)
            pool.affine_select(out=mask_kq[:, :, :], in_=mask_kq[:, :, :], compare_op=ALU.is_ge, fill=-1e9, base=0,
                               pattern=[[0, 4], [1, P]], channel_multiplier=-1)
            pool.memset(k_s[:, :, :, 3 * DK], 1.0)
            pool.memset(v_ext[:, :, :, 1::2, 2 * DK + 1], 1.0)
            pool.memset(v_ext[:, :, :, 0::2, 2 * DK], 1.0).then_inc(s_aconst, 1)
            def low_half(n):
                w, c = weight_halves()[n]
                pool.wait_ge(s_high, n + 1)
                pool.tensor_tensor(w[:, 1, c], stage[:, n % 2, :], w[:, 0, c], ALU.subtract).then_inc(s_low, 1)

            for c in range(NC):
                tiles = slice(c * CH, (c + 1) * CH)
                pool.wait_ge(ffns[0]["high"], c + 1)
                pool.tensor_tensor(xn_hl[:, tiles, 1, :], xf0(c), xn_hl[:, tiles, 0, :], ALU.subtract).then_inc(ffns[0]["split"], 1)
            for n in range(4):
                low_half(n)

            def settle(j):
                if not isinstance(j, int):
                    pool.sem_inc(s_pool_held, 1)

            def attention():
                y_rows = y_table[0:NS * P, :]
                yg_sem = (at["yg0"], at["yg1"])

                def turn(b, par, has, pair):
                    def rows():
                        if has(4):
                            if not isinstance(b, int) or b >= -2:
                                pool.wait_ge(yg_sem[par], 64 * pair(4))
                            pool.tensor_copy(y_cur[:, par, :], pos_u[:, bass.ds(2 * (b + 4), 2), :].rearrange("p t k -> p (t k)")).then_inc(at["cur"], 1)
                            wait(pool, "stats", b + 3)
                            pool.wait_ge(at["cur"], b + 5)
                            settle(b)
                            for t in range(2):
                                for kk in range(TOPK):
                                    n = t * TOPK + kk
                                    pool.indirect_dma_start(out=yg[:, par, t, kk, :], out_offset=None, in_=y_rows,
                                                            in_offset=Offset(ap=y_cur[:, par, n:n + 1], axis=0)).then_inc(yg_sem[par], 16)

                    def deviations():
                        if has(3) or has(-2):
                            pool.wait_ge(at["stats"], b + 4)
                            wait(pool, "dev", b + 3)
                            deviation(pool, st, stats2[:, 1 - par, :, :], [ln_s[:, k, :] for k in range(4)],
                                      mean_s[:, 1 - par, :], rstd_s[:, 1 - par, :], 4, lambda: settle(b)).then_inc(at["dev"], 1)

                    rows()
                    if not idle(b):
                        deviations()
                    if has(2):
                        wait(pool, "PV", 4 * (b + 1))
                        pool.wait_ge(at["vtmp"], 2 * (b + 3))
                        settle(b)
                        v = v_tmp[:, :, :].rearrange("p t (h d) -> p t h d", d=DK)
                        for odd in range(2):
                            ins = pool.tensor_copy(v_ext[:, par, :, odd::2, odd * DK:(odd + 1) * DK], v[:, :, odd::2, :])
                        ins.then_inc(at["vext"], 1)
                for u in range(3):
                    pool.wait_ge(ffns[0]["put"][u], 16 * NR)
                sequences(pool, turn, st, DEV_STEPS_P)

            def ffn(k):
                f = ffns[k]
                with pool.Fori(0, KT // 8) as i:
                    runs = oh_hi[:, bass.ds(i * 8, 8), :]
                    pool.wait_ge(f["lo"], i + 1)
                    pool.tensor_tensor(runs, runs, pow_c[:, bass.ds(i * 8, 8)].unsqueeze(2).broadcast_to([P, 8, NS]),
                                       ALU.mult).then_inc(f["hi"], 1)
                pool.wait_ge(f["idx"], 1)
                pool.wait_ge(f["tab"], 16 * NC)

                def pick(j, u):
                    pool.tensor_copy(cur[:, u, :, :].rearrange("p a b -> p (a b)"),
                                     idx[:, bass.ds(j, 1), :, :].rearrange("p j a b -> p (j a b)")).then_inc(f["cur"], 1)

                def gather(j, u):
                    pool.wait_ge(f["tab"], 16 * NC)
                    settle(j)
                    for h in range(SUB):
                        pool.indirect_dma_start(out=xs[:, u, h, :], out_offset=None, in_=xn_table,
                                                in_offset=Offset(ap=cur[:, u, 0, h:h + 1], axis=0)).then_inc(f["got"][u], 16)

                def scatter(j, u):
                    pool.wait_ge(f["y"], j - 5)
                    settle(j)
                    for h in range(SUB):
                        pool.indirect_dma_start(out=y_table, out_offset=Offset(ap=cur[:, u, 1, h:h + 1], axis=0),
                                                in_=ys[:, u, h, :], in_offset=None).then_inc(f["put"][u], 16)

                pick(0, 0)
                for j in range(3):
                    if j < 2:
                        pick(j + 1, j + 1)
                    pool.wait_ge(f["cur"], j + 1)
                    gather(j, j)
                
                def step(i, u):
                    j = 3 * i + u
                    pool.wait_ge(f["got"][u], 32 * i)
                    if k > 0 and later(i, 3):
                        pool.wait_ge(f["put"][u], 32 * (i - 2))
                    pick(j, u)
                    pool.wait_ge(f["rows_in"], j - 2)
                    pool.wait_ge(f["cur"], j + 1)
                    gather(j, u)
                    if k > 0 and later(i, 2):
                        scatter(j, u)

                for j in range(3, 9):
                    step(j // 3, j % 3)
                with pool.Fori(3, NR) as i:
                    for u in range(3):
                        step(i, u)
                for j in range(NJ, NJ + 6 if k > 0 else NJ):
                    i, u = divmod(j, 3)
                    pool.wait_ge(f["got"][u], 32 * NR)
                    pool.wait_ge(f["put"][u], 32 * (i - 2))
                    pick(j, u)
                    pool.wait_ge(f["cur"], j + 1)
                    scatter(j, u)
                for c in range(2 * NC if k > 0 else 0):
                    xt = x[:, c * (CH // 2):(c + 1) * (CH // 2), :]
                    pool.wait_ge(f["first"], c + 1)
                    pool.wait_ge(f["second"], c + 1)
                    pool.tensor_tensor(xt, xt, yc(c)[:, 1, :, :], ALU.add).then_inc(f["comb"], 1)

            ffn(0)
            attention()
            ffn(1)

        @block.tensor
        def _(pe):
            pe.wait_ge(s_const, 1)
            pe.wait_ge(s_small, 48)
            pe.transpose(bank[5][:, 0:E * FT], b1_rows[:, :], ident[0:E * FT, 0:E * FT]).then_inc(s_b1, 1)

            def h16(b):
                return bank[b][:, :].bitcast(F16)

            def attention():
                pe.wait_ge(s_wa, 16 * 6)
                pe.wait_ge(s_b1, 2)
                for n in range(4):
                    ins = pe.transpose(bank[5][:, n * D:(n + 1) * D], w_rows[:, n, :], ident[:, :])
                ins.then_inc(s_wt, 1)
                pe.wait_ge(s_wtc, 1)
                pe.wait_ge(s_aconst, 1)

                def job_scores(b, par, n, st, mx):
                    j, js, part, qp = n // 3, (n // 3 + 2) % 4, n % 3, 1 - par
                    r, rs = slice(HW * j, HW * (j + 1)), slice(HW * js, HW * js + 3 * DK)
                    dst, dst_s = bank[2 + n % 2], bank[n % 2]
                    two = lambda d: d[:, :].rearrange("p (g k) -> p g k", g=2)
                    if st:
                        wait(pe, "exp", 12 * b + n - 1)
                        if part == 0:
                            pe.matmul(dst[:, :], ident_b[:, :], mask_kq[:, :, :], start=True, stop=False, skip_group_check=True)
                        else:
                            pe.matmul(two(dst)[:, :, 0:P], ident_b[:, :], mask_kq[:, 0:2, :],
                                      start=True, stop=False, skip_group_check=True)
                    if mx:
                        wait(pe, "max", 12 * (b + 1) + n - 1)
                        if part == 0:
                            pe.matmul(dst_s[:, :], ident_b[:, :], mask_qk[:, :, :], start=True, stop=False, skip_group_check=True)
                        else:
                            pe.matmul(two(dst_s)[:, :, P:L], ident_b[:, :], mask_qk[:, 0:2, :],
                                      start=True, stop=False, skip_group_check=True)
                    count = G if part == 0 else 2
                    for m in range(count):
                        g = m if part == 0 else 2 * (part - 1) + m
                        if st:
                            if part == 0:
                                ins = pe.matmul(dst[:, m * P:(m + 1) * P], kT[r, par, g, P:L], qmT[r, g, P:L],
                                                start=False, stop=True, skip_group_check=True)
                            else:
                                ins = pe.matmul(dst[:, m * L:(m + 1) * L], kT[r, par, g, 0:P], qmT[r, g, :],
                                                start=False, stop=True, skip_group_check=True)
                            if m == count - 1:
                                ins.then_inc(at["ST"], 1)
                        if mx:
                            if part == 0:
                                ins = pe.matmul(dst_s[:, m * P:(m + 1) * P], qT[rs, qp, g, 0:P], kT[rs, qp, g, 0:P],
                                                start=False, stop=True, skip_group_check=True)
                            else:
                                ins = pe.matmul(dst_s[:, m * L:(m + 1) * L], qT[rs, qp, g, P:L], kT[rs, qp, g, :],
                                                start=False, stop=True, skip_group_check=True)
                            if m == count - 1:
                                ins.then_inc(at["S"], 1)

                def job_pv(b, par, j):
                    pe.wait_ge(at["exp"], 12 * b + 3 * j + 3)
                    if j == 0:
                        pe.wait_ge(at["vext"], b + 1)
                        wait(pe, "Oc", b)
                    r, odd = j // 2, j % 2
                    for g in range(G):
                        c = slice(HW * g, HW * (g + 1))
                        pe.matmul(bank[4][c, r * L:(r + 1) * L], v_ext[:, par, 0, 4 * g + j, :],
                                  pr[:, j % 2, 1 + g // 2, (g % 2) * L:(g % 2 + 1) * L], start=(odd == 0), stop=False)
                    for g in range(G):
                        c = slice(HW * g, HW * (g + 1))
                        ins = pe.matmul(bank[4][c, r * L + P:(r + 1) * L], v_ext[:, par, 1, 4 * g + j, :],
                                        pr[:, j % 2, 0, g * P:(g + 1) * P], start=False, stop=(odd == 1))
                    ins.then_inc(at["PV"], 1)

                def turn(b, par, has, pair):
                    scores, maxima, front, back = has(0), has(1), has(2), has(-1)
                    for n in range(12):
                        if n == 0:
                            if maxima:
                                pe.wait_ge(at["qkTc"], 2 * (b + 2))
                                job_scores(b, par, 0, False, True)
                                job_scores(b, par, 1, False, True)
                            if scores:
                                pe.wait_ge(at["qmTc"], b + 1)
                                job_scores(b, par, 0, True, False)
                        elif scores and n == 1:
                            job_scores(b, par, 1, True, False)
                        elif n > 1 and (scores or maxima):
                            job_scores(b, par, n, scores, maxima)
                        if scores and n % 3 == 0 and n > 0:
                            job_pv(b, par, n // 3 - 1)
                        if back and n == 1:
                            pe.wait_ge(at["Oc"], b)
                            wait(pe, "qkTc", 2 * (b + 2) if not isinstance(b, int) or b + 1 < B else 2 * B)
                            for m in range(4):
                                ins = pe.transpose(bank[6][:, m * P:(m + 1) * P],
                                                   o_sb[:, 1 - par, m % 2, m // 2 * P:(m // 2 + 1) * P], ident[:, :])
                            ins.then_inc(at["OT"], 1)
                        if front and n == 1:
                            pe.wait_ge(at["xa"], b + 3)
                            wait(pe, "qmTc", b + 1)
                            for t in range(2):
                                ins = pe.transpose(bank[5][:, t * P:(t + 1) * P], xa[:, t, :], ident[:, :])
                            ins.then_inc(at["xaT"], 1)
                        if back and n == 3:
                            pe.wait_ge(at["att"], b)
                            wait(pe, "xaTc", b + 3 if front else B)
                            for t in range(2):
                                ins = pe.transpose(bank[5][:, t * P:(t + 1) * P],
                                                   att[:, t, :, :, :].rearrange("p g j d -> p (g j d)"), ident[:, :])
                            ins.then_inc(at["attT"], 1)
                        if front and n == 4:
                            pe.wait_ge(at["xaTc"], b + 3)
                            wait(pe, "qkTc", 2 * (b + 2))
                            wait(pe, "att", b)
                            for t in range(2):
                                pe.matmul(bank[6 + t][:, 0:3 * D], xaT[:, t * P:(t + 1) * P], w_qkv[:, :],
                                          start=True, stop=True).then_inc(at["qkv"], 1)
                        if back and n == 5:
                            pe.wait_ge(at["attTc"], b)
                            for t in range(2):
                                ins = pe.matmul(bank[5][:, t * P:(t + 1) * P], attT[:, t * P:(t + 1) * P], w_o[:, :],
                                                start=True, stop=True)
                            ins.then_inc(at["wo"], 1)
                    if front:
                        for t in range(2):
                            pe.wait_ge(at["lo"], 2 * (b + 2) + t + 1)
                            for g in range(G):
                                c = slice(4 * g, 4 * g + 4)
                                pe.transpose(h16(6 + t)[:, g * P:(g + 1) * P],
                                             q_s[:, par, t, c, :].rearrange("p h w -> p (h w)"), ident_h[:, :])
                                ins = pe.transpose(h16(6 + t)[:, (G + g) * P:(G + g + 1) * P],
                                                   k_s[:, t, c, :].rearrange("p h w -> p (h w)"), ident_h[:, :])
                            ins.then_inc(at["qkT"], 1)
                    if maxima:
                        pe.wait_ge(at["max"], 12 * (b + 2))
                        wait(pe, "xadd", b)
                        wait(pe, "xaTc", b + 3 if front else B)
                        for t in range(2):
                            for g in range(G):
                                ins = pe.transpose(h16(5)[:, g * L + t * P:g * L + (t + 1) * P],
                                                   q_s[:, 1 - par, t, 4 * g:4 * g + 4, :].rearrange("p h w -> p (h w)"),
                                                   ident_h[:, :])
                        ins.then_inc(at["qmT"], 1)
                    if scores:
                        job_pv(b, par, 3)

                sequences(pe, turn)

            def ffn(k):
                f = ffns[k]
                def transposes(c):
                    pe.wait_ge(f["split"], (c + 1) * (CH // 2 if k else 1))
                    if c >= 2:
                        pe.wait_ge(f["trc"], 2 * (c - 1))
                    for t in range(CH):
                        for h in range(2):
                            ins = pe.transpose(h16(c % 2 * 4 + t // 4)[:, (t % 4 * 2 + h) * P:(t % 4 * 2 + h + 1) * P],
                                               xn_hl[:, c * CH + t, h, :], ident_h[:, :])
                        if t % 4 == 3:
                            ins.then_inc(f["tr"], 1)

                def logits(c):
                    for t in range(CH):
                        if t % 4 == 0:
                            pe.wait_ge(f["trc"], c * 2 + t // 4 + 1)
                        tt = c * CH + t
                        dst = bank[2 + tt // (NT // 2)][:, tt % (NT // 2) * E:(tt % (NT // 2) + 1) * E]
                        pe.matmul(dst, xnT[:, c % 2, t, 0, :], wg_hl[:, 0, :], start=True, stop=False)
                        pe.matmul(dst, xnT[:, c % 2, t, 1, :], wg_hl[:, 0, :], start=False, stop=False)
                        ins = pe.matmul(dst, xnT[:, c % 2, t, 0, :], wg_hl[:, 1, :], start=False, stop=True)
                    ins.then_inc(f["lgt"], 1)

                if k == 0:
                    pe.wait_ge(s_b1, 2)
                for c in range(0, NC, 2):
                    transposes(c)
                    if k == 1 and c == 0:
                        pe.wait_ge(at["xadd"], B)
                    transposes(c + 1)
                    if k == 0 and c == 0:
                        pe.wait_ge(s_wg, 3)
                    logits(c)
                    logits(c + 1)
                pe.wait_ge(f["member"], 1)
                m = member[:, :, :].rearrange("p t e -> p e t")
                pe.matmul(bank[3][:, 0:E * NT], below[:, :], m, start=True, stop=True)
                pe.matmul(bank[3][:, E * NT:2 * E * NT], ones_h[:, :], m, start=True, stop=True).then_inc(f["count"], 1)
                inv = bank[6][:, 0:NS]
                pe.wait_ge(f["hi"], 1)
                pe.matmul(inv, zero_h[:, :], oh_hi[:, 0, :], start=True, stop=False)
                for kt in range(KT):
                    if kt % 8 == 0:
                        pe.wait_ge(f["hi"], kt // 8 + 1)
                    pe.matmul(inv, oh_lo[:, kt, :], oh_hi[:, kt, :], start=False, stop=False)
                pe.matmul(inv, zero_h[:, :], oh_hi[:, 0, :], start=False, stop=True).then_inc(f["inv"], 1)

                pe.wait_ge(f["idx"], 1)
                if k == 0:
                    pe.wait_ge(s_low, 4)

                def turn(j, u, i):
                    pe.wait_ge(f["got"][u], 32 * (i + 1))
                    if later(j, 1):
                        pe.wait_ge(f["xT"], j)
                    for s in range(SUB):
                        for h in range(2):
                            ins = pe.transpose(h16(6)[:, h * TILE + s * P:h * TILE + (s + 1) * P],
                                               xs[:, u, s, h * P:(h + 1) * P], ident_h[:, :])
                    ins.then_inc(f["rows_in"], 1)

                def first(j, u, ex):
                    pe.wait_ge(f["xT"], j + 1)
                    if later(j, 3):
                        pe.wait_ge(f["gelu"], j - 2)
                    for ft in range(FT):
                        dst = bank[2 * u + ft // 2][:, (ft % 2) * TILE:(ft % 2 + 1) * TILE]
                        w = [w1_hl[:, h, bass.ds(ex * F + ft * P, P)] for h in range(2)]
                        pe.matmul(dst, w[0], xT[:, u, 0, :], start=True, stop=False)
                        pe.matmul(dst, w[0], xT[:, u, 1, :], start=False, stop=False)
                        ins = pe.matmul(dst, w[1], xT[:, u, 0, :], start=False, stop=True)
                    ins.then_inc(f["hmm"], 1)

                def second(j, u, ex):
                    pe.wait_ge(f["hs"], j + 1)
                    if later(j, 1):
                        pe.wait_ge(f["y"], j)
                    for s in range(SUB):
                        dst = bank[7][:, s * D:(s + 1) * D]
                        for ft in range(FT):
                            hh = [hid_hl[:, u, h, ft, s * P:(s + 1) * P] for h in range(2)]
                            w = [w2_hl[:, h, bass.ds(ex * F + ft * D, D)] for h in range(2)]
                            pe.matmul(dst, hh[0], w[0], start=(ft == 0), stop=False)
                            pe.matmul(dst, hh[0], w[1], start=False, stop=False)
                            ins = pe.matmul(dst, hh[1], w[0], start=False, stop=(ft == FT - 1))
                    ins.then_inc(f["ymm"], 1)

                def steps(i, head=False, tail=False):
                    ex = experts(pe, i)
                    for u in range(3):
                        j = 3 * i + u
                        first(j, u, ex[u + 2])
                        if not (tail and u == 2):
                            turn(j + 1, (u + 1) % 3, i + (u == 2))
                        if not (head and u < 2):
                            second(j - 2, (u + 1) % 3, ex[u])
                    return ex[3:]

                turn(0, 0, 0)
                steps(0, head=True)
                with pe.Fori(1, NR - 1) as i:
                    steps(i)
                for n, ex in enumerate(steps(NR - 1, tail=True)):
                    second(NJ - 2 + n, 1 + n, ex)

            ffn(0)
            attention()
            ffn(1)

        @block.scalar
        def _(act):
            act.wait_ge(s_const, 1)
            act.wait_ge(s_small, 48)
            act.activation(wg_hl[:, 0, :], wg_f[:, :], ACT.Copy).then_inc(s_wg, 2)
            act.wait_ge(s_b1, 1)
            act.activation(b1_c[:, :], bank[5][:, 0:E * FT], ACT.Copy).then_inc(s_b1, 1)

            def attention():
                act.wait_ge(s_wt, 1)
                act.activation(w_qkv[:, :], bank[5][:, 0:3 * D], ACT.Copy)
                act.activation(w_o[:, :], bank[5][:, 3 * D:4 * D], ACT.Copy).then_inc(s_wtc, 1)
                act.activation(warm[0:1, 7:8], ident[0:1, 0:1], ACT.Exp)
                act.wait_ge(s_aconst, 1)

                def turn(b, par, has, pair):
                    scores, maxima, front, back = has(0), has(1), has(2), has(-1)
                    for n in range(12):
                        if scores:
                            j, part = n // 3, n % 3
                            act.wait_ge(at["ST"], 12 * b + n + 1)
                            wait(act, "PV", 4 * b + j - 1)
                            act.activation(pr[:, j % 2, part, :], bank[2 + n % 2][:, :], ACT.Exp, scale=SC).then_inc(at["exp"], 1)
                        if front and n == 1:
                            act.wait_ge(at["xaT"], b + 3)
                            wait(act, "qkv", 2 * (b + 2))
                            act.activation(xaT[:, :], bank[5][:, 0:L], ACT.Copy).then_inc(at["xaTc"], 1)
                        if back and n == 3:
                            act.wait_ge(at["attT"], b)
                            wait(act, "wo", b - 1)
                            act.activation(attT[:, :], bank[5][:, 0:L], ACT.Copy).then_inc(at["attTc"], 1)
                        if front and n == 4:
                            wait(act, "vext", b + 2)
                            for t in range(2):
                                act.wait_ge(at["qkv"], 2 * (b + 2) + t + 1)
                                act.activation(v_tmp[:, t, :], bank[6 + t][:, 2 * D:3 * D], ACT.Copy).then_inc(at["vtmp"], 1)
                        if front and n in (6, 8):
                            t = n // 2 - 3
                            act.wait_ge(at["rot"], 2 * (b + 2) + t + 1)
                            wait(act, "qmT", b + 1)
                            wait(act, "qkT", 2 * (b + 2))
                            act.activation(q_s[:, par, t, :, 0:2 * DK].rearrange("p h (c d) -> p h c d", c=2),
                                           rot[:, t, 0, :, :].unsqueeze(2).broadcast_to([P, H, 2, DK]), ACT.Copy)
                            act.activation(k_s[:, t, :, 0:4 * DK].rearrange("p h (c d) -> p h c d", c=4)[:, :, 0:3:2, :],
                                           rot[:, t, 1, :, :].unsqueeze(2).broadcast_to([P, H, 2, DK]),
                                           ACT.Copy).then_inc(at["hi"], 1)
                    if front:
                        act.wait_ge(at["qkT"], 2 * (b + 2) + 2)
                        wait(act, "ST", 12 * (b + 1))
                        wait(act, "S", 12 * (b + 1))
                        for dst, first in ((qT, 0), (kT, G)):
                            ins = act.activation(dst[:, par, :, P:L], bank[7][:, :].bitcast(F16)[:, first * P:(first + G) * P]
                                                 .rearrange("p (g s) -> p g s", g=G), ACT.Copy)
                        ins.then_inc(at["qkTc"], 1)
                    if maxima:
                        act.wait_ge(at["qmT"], b + 2)
                        wait(act, "ST", 12 * (b + 1))
                        act.activation(qmT[:, :, :].rearrange("p g s -> p (g s)"), bank[5][:, :].bitcast(F16), ACT.Copy).then_inc(at["qmTc"], 1)
                    if scores:
                        act.wait_ge(at["PV"], 4 * b + 4)
                        wait(act, "OT", b - 1)
                        act.activation(o_sb[:, par, :, :].rearrange("p r s -> p (r s)"), bank[4][:, :], ACT.Copy).then_inc(at["Oc"], 1)

                sequences(act, turn)

            def ffn(k):
                f = ffns[k]
                def transposed(c):
                    for q in range(2):
                        act.wait_ge(f["tr"], 2 * c + q + 1)
                        if c >= 2:
                            act.wait_ge(f["lgt"], c - 1)
                        act.activation(xnT[:, c % 2, 4 * q:4 * q + 4, :, :].rearrange("p a b c -> p (a b c)"),
                                       bank[c % 2 * 4 + q][:, :].bitcast(F16), ACT.Copy).then_inc(f["trc"], 1)

                def high_half(n):
                    w, c = weight_halves()[n]
                    act.wait_ge(s_half[n % 2], 16 * (n // 2 + 1))
                    act.activation(w[:, 0, c], stage[:, n % 2, :], ACT.Copy).then_inc(s_high, 1)

                if k == 0:
                    for c in range(NC):
                        act.wait_ge(f["norm"], c + 1)
                        act.activation(xn_hl[:, c * CH:(c + 1) * CH, 0, :], xf0(c), ACT.Copy).then_inc(f["high"], 1)
                        if c == 1:
                            transposed(0)
                            transposed(1)
                    high_half(0)
                    transposed(2)
                    transposed(3)
                    for n in range(1, 4):
                        high_half(n)
                else:
                    for c in range(NC):
                        transposed(c)
                act.wait_ge(f["top"], 1)
                act.activation(gate[:, :, :], top[:, :, :], ACT.Sigmoid).then_inc(f["gate"], 1)
                act.activation(warm[0:1, 3 * k + 1:3 * k + 2], ident[0:1, 0:1], ACT.Gelu_apprx_tanh)
                act.wait_ge(f["idx"], 1)

                def gelu(j, u, ex):
                    act.wait_ge(f["hmm"], j + 1)
                    if later(j, 3):
                        act.wait_ge(f["hs"], j - 2)
                    for ft in range(FT):
                        ins = act.activation(hid[:, u, ft, :], bank[2 * u + ft // 2][:, (ft % 2) * TILE:(ft % 2 + 1) * TILE],
                                             ACT.Gelu_apprx_tanh, bias=b1_c[:, bass.ds(ex * FT + ft, 1)])
                    ins.then_inc(f["gelu"], 1)

                def steps(i):
                    ex = experts(act, i)
                    for u in range(3):
                        gelu(3 * i + u, u, ex[u + 2])

                steps(0)
                with act.Fori(1, NR) as i:
                    steps(i)
                for c in range(2 * NC if k > 0 else 0):
                    act.wait_ge(f["yc"][c], 32)
                    for t in range(CH // 2):
                        tt = c * (CH // 2) + t
                        ins = act.activation(yc(c)[:, 1, t, :], yc(c)[:, 1, t, :], ACT.Copy, scale=gate[:, 1, tt:tt + 1])
                    ins.then_inc(f["second"], 1)

            ffn(0)
            attention()
            ffn(1)

        @block.vector
        def _(dve):
            st = Steps(dve, s_dve)
            dve.memset(idx[:, :, :, :], 0)
            dve.memset(exp_f[:, :], 0.0)
            st.did(dve.memset(before[:, :], 0.0))
            st.wait()
            dve.wait_ge(s_const, 1)

            def normalise():
                for c in range(0, NC, 2):
                    for t in range(2 * CH):
                        if t % CH == 0:
                            dve.wait_ge(s_xc[c + t // CH], 16)
                        ins = dve.bn_stats(stats[:, t, :], x[:, c * CH + t, :])
                    st.did(ins)
                    st.wait()
                    st.did(deviation(dve, st, stats[:, :, :], [ln_w[:, n, :] for n in range(4)], mean[:, :], rstd[:, :], 2 * CH))
                    st.wait()
                    for t in range(2 * CH):
                        cc = c + t // CH
                        if t % CH == 0 and cc >= 3:
                            dve.wait_ge(ffns[0]["split"], cc - 2)
                        ins = dve.tensor_scalar(xf0(cc)[:, t % CH, :], x[:, c * CH + t, :],
                                                mean[:, t:t + 1], rstd[:, t:t + 1], ALU.subtract, ALU.mult)
                        if t % CH == CH - 1:
                            ins.then_inc(ffns[0]["norm"], 1)
                    if c == 0:
                        constants()
                    if c + 2 < NC:
                        dve.wait_ge(ffns[0]["norm"], c + 2)

            def constants():
                dve.wait_ge(s_small, 48)
                dve.wait_ge(s_wg, 2)
                dve.tensor_tensor(wg_hl[:, 1, :], wg_f[:, :], wg_hl[:, 0, :], ALU.subtract).then_inc(s_wg, 1)
                st.did(dve.tensor_scalar(pow_c[:, :].bitcast(I32), pow_i[:, :], 23, None, ALU.logical_shift_left))
                st.did(dve.memset(stats2[:, :, :, :], 0.0))
                st.wait()
                st.did(dve.tensor_scalar(pow_c[:, :], pow_c[:, :], part_c[:, 0:1], None, ALU.mult))

            def attention():
                dve.wait_ge(s_aconst, 1)
                dve.wait_ge(s_wa, 16 * 6)

                def maximum(b, par, n):
                    j, part = (n // 3 + 2) % 4, n % 3
                    dve.wait_ge(at["S"], 12 * b + n + 1)
                    t, g0, ng = (0, 0, G) if part == 0 else (1, 2 * (part - 1), 2)
                    dst = q_s[:, par, t, :, 3 * DK].rearrange("p (g j) -> p g j", g=G)[:, g0:g0 + ng, j]
                    dve.tensor_reduce(dst, bank[n % 2][:, :].rearrange("p (g k) -> p g k", g=ng), AX.X, ALU.max,
                                      negate=True).then_inc(at["max"], 1)

                def row(t):
                    return x[:, bass.ds(t, 1), :].rearrange("p a d -> p (a d)")

                def combine(b, par, n):
                    dve.wait_ge((at["yg0"], at["yg1"])[par], 64 * (n + 1))
                    for kk in range(TOPK):
                        for t in range(2):
                            tt = 2 * b + t
                            ins = dve.scalar_tensor_tensor(out=row(tt), in0=yg[:, par, t, kk, :], scalar=gate[:, kk, bass.ds(tt, 1)],
                                                           in1=row(tt), op0=ALU.mult, op1=ALU.add)
                        st.did(ins)
                        st.wait()

                def statistics(b, par, has):
                    wait(dve, "dev", b + 2)
                    if has(-2):
                        dve.wait_ge(at["xadd"], b - 1)
                    if not isinstance(b, int):
                        dve.sem_inc(s_dve_held, 1)
                    for n, k in ((0, 3), (2, -2)):
                        for t in range(2):
                            if has(k):
                                ins = dve.bn_stats(stats2[:, par, n + t, :], row(2 * (b + k) + t))
                    ins.then_inc(at["stats"], 1)
                    if idle(b):
                        dve.wait_ge(at["stats"], b + 4)
                        deviation(dve, st, stats2[:, par, :, :], [ln_w[:, n, 0:4] for n in range(4)],
                                  mean_s[:, par, :], rstd_s[:, par, :], 4).then_inc(at["dev"], 1)

                def after(b, par):
                    if later(b, 1):
                        dve.wait_ge(ffns[1]["split"], b)
                    for t in range(2):
                        ins = dve.tensor_scalar(xo[:, t, :], row(2 * b + t), mean_s[:, par, 2 + t:3 + t],
                                                rstd_s[:, par, 2 + t:3 + t], ALU.subtract, ALU.mult)
                    st.did(ins)
                    st.wait()
                    hi = xn_hl[:, bass.ds(2 * b, 2), 0, :]
                    st.did(dve.tensor_copy(hi, xo[:, :, :]))
                    st.wait()
                    dve.tensor_tensor(xn_hl[:, bass.ds(2 * b, 2), 1, :], xo[:, :, :], hi, ALU.subtract).then_inc(ffns[1]["split"], 1)

                def divide(b):
                    dve.wait_ge(at["OT"], b)
                    wait(dve, "attT", b - 1)
                    sums = bank[6][:, :].rearrange("p (x w) -> p x w", w=HW)
                    st.did(dve.reciprocal(den[:, :, :], sums[:, :, 2 * DK:2 * DK + 2]))
                    st.wait()
                    for m in range(4):
                        t, r = m // 2, m % 2
                        x4 = slice(m * G, (m + 1) * G)
                        ins = dve.tensor_tensor(att[:, t, :, 2 * r:2 * r + 2, :],
                                                sums[:, x4, 0:2 * DK].rearrange("p g (j d) -> p g j d", d=DK),
                                                den[:, x4, :].unsqueeze(3).broadcast_to([P, G, 2, DK]), ALU.mult)
                    ins.then_inc(at["att"], 1)

                def rope(b, t):
                    dve.wait_ge(at["qkv"], 2 * b + t + 1)
                    dve.wait_ge(at["vtmp"], 2 * b + t + 1)
                    wait(dve, "lo", 2 * b + t - 1)
                    wait(dve, "hi", 2 * b + t - 1)
                    src = bank[6 + t][:, 0:QK].rearrange("p (h d) -> p h d", d=DK)
                    c = cos[:, t, :].unsqueeze(1).broadcast_to([P, 2 * H, DK])
                    s = sin[:, t, :].rearrange("p (i c) -> p i c", c=2)
                    dve.tensor_tensor(r_a[:, :, :], src, c, ALU.mult)
                    pairs = src.rearrange("p h (i c) -> p h i c", c=2)
                    rb = r_b[:, :, :].rearrange("p h (i c) -> p h i c", c=2)
                    for c in range(2):
                        ins = dve.tensor_tensor(rb[:, :, :, c], pairs[:, :, :, 1 - c],
                                                s[:, :, c].unsqueeze(1).broadcast_to([P, 2 * H, DK // 2]), ALU.mult)
                    st.did(ins)
                    st.wait()
                    dve.tensor_tensor(rot[:, t, :, :, :].rearrange("p a h d -> p (a h) d"), r_a[:, :, :], r_b[:, :, :],
                                      ALU.add).then_inc(at["rot"], 1)
                    dve.wait_ge(at["rot"], 2 * b + t + 1)

                def low(b, par, t):
                    dve.wait_ge(at["hi"], 2 * b + t + 1)
                    dve.tensor_tensor(q_s[:, par, t, :, 2 * DK:3 * DK], rot[:, t, 0, :, :], q_s[:, par, t, :, 0:DK], ALU.subtract)
                    dve.tensor_tensor(k_s[:, t, :, DK:2 * DK], rot[:, t, 1, :, :], k_s[:, t, :, 0:DK],
                                      ALU.subtract).then_inc(at["lo"], 1)

                def turn(b, par, has, pair):
                    scores, maxima, front, back = has(0), has(1), has(2), has(-1)
                    if front:
                        wait(dve, "xaT", b + 2)
                        dve.wait_ge(at["dev"], b + 3)
                        for t in range(2):
                            ins = dve.tensor_scalar(xa[:, t, :], row(2 * (b + 2) + t), mean_s[:, par, t:t + 1],
                                                    rstd_s[:, par, t:t + 1], ALU.subtract, ALU.mult)
                        ins.then_inc(at["xa"], 1)
                    if has(-3):
                        if not front:
                            dve.wait_ge(at["dev"], b + 3)
                        after(b - 3, par)
                    for n in range(12):
                        if maxima:
                            maximum(b + 1, 1 - par, n)
                        if back and n == 1:
                            divide(b)
                        if back and n == 5:
                            dve.wait_ge(at["wo"], b)
                            xt = x[:, bass.ds(2 * (b - 1), 2), :]
                            dve.tensor_tensor(xt, bank[5][:, 0:L].rearrange("p (t d) -> p t d", t=2), xt, ALU.add).then_inc(at["xadd"], 1)
                        if front and n in (5, 7):
                            rope(b + 2, n // 2 - 2)
                        if front and n in (8, 9):
                            low(b + 2, par, n - 8)
                        if has(3) and n == 3:
                            combine(b + 3, 1 - par, pair(3))
                        if (has(3) or has(-2)) and n == 3:
                            statistics(b, 1 - par, has)
                    if front:
                        dve.wait_ge(at["qkT"], 2 * (b + 2) + 1)
                        wait(dve, "ST", 12 * (b + 1))
                        wait(dve, "S", 12 * (b + 1))
                        for dst, first in ((qT, 0), (kT, G)):
                            ins = dve.tensor_copy(dst[:, par, :, 0:P], bank[6][:, :].bitcast(F16)[:, first * P:(first + G) * P]
                                                  .rearrange("p (g s) -> p g s", g=G))
                        ins.then_inc(at["qkTc"], 1)

                sequences(dve, turn, st, 7)
                dve.wait_ge(at["xadd"], B)

            def ffn(k):
                f = ffns[k]
                if k == 0:
                    normalise()

                HT = NT // 2
                for h in range(2):
                    ts = slice(h * HT, (h + 1) * HT)

                    def over_e(a):
                        return a.unsqueeze(2).broadcast_to([P, HT, E])

                    rank_b = rank_c[:, :].unsqueeze(1).broadcast_to([P, HT, E])
                    dve.wait_ge(f["lgt"], (h + 1) * NC // 2)
                    st.did(dve.tensor_scalar(lg[:, ts, :].rearrange("p t e -> p (t e)"), bank[2 + h][:, 0:HT * E], SAT, None, ALU.min))
                    for kk, src in enumerate((lg, lg2)):
                        st.wait()
                        st.did(dve.tensor_reduce(top[:, kk, ts], src[:, ts, :], AX.X, ALU.max))
                        st.wait()
                        st.did(dve.tensor_tensor(eq[:, ts, :], src[:, ts, :], over_e(top[:, kk, ts]), ALU.is_equal))
                        st.wait()
                        st.did(dve.tensor_tensor(eq[:, ts, :], eq[:, ts, :], rank_b, ALU.mult))
                        st.wait()
                        st.did(dve.tensor_reduce(cmx[:, ts], eq[:, ts, :], AX.X, ALU.max))
                        st.wait()
                        st.did(dve.tensor_tensor(oh[:, kk, ts, :], rank_b, over_e(cmx[:, ts]), ALU.is_equal))
                        st.wait()
                        if kk == 0:
                            st.did(dve.scalar_tensor_tensor(out=lg2[:, ts, :], in0=oh[:, 0, ts, :], scalar=-BIG, in1=lg[:, ts, :],
                                                            op0=ALU.mult, op1=ALU.add))
                    ins = dve.tensor_tensor(member[:, ts, :], oh[:, 0, ts, :], oh[:, 1, ts, :], ALU.add)
                ins.then_inc(f["member"], 1)
                dve.nop().then_inc(f["top"], 1)

                dve.wait_ge(f["count"], 1)
                st.did(dve.tensor_copy(tot[:, :, :].rearrange("p e t -> p (e t)"), bank[3][:, E * NT:2 * E * NT]))
                st.wait()
                st.did(dve.tensor_tensor_scan(cum[:, :, :].rearrange("p e t -> p (e t)"), ones_f[:, :],
                                              tot[:, :, :].rearrange("p e t -> p (e t)"), 0.0, ALU.mult, ALU.add))
                st.wait()
                st.did(dve.tensor_copy(before[:, 1:E], cum[:, 0:E - 1, NT - 1]))
                dve.tensor_tensor(tot[:, :, :], cum[:, :, :], tot[:, :, :], ALU.subtract)
                st.wait()
                st.did(dve.tensor_tensor(cnt[:, :], cum[:, :, NT - 1], before[:, :], ALU.subtract))
                st.wait()
                st.did(dve.tensor_scalar(cnt_i[:, :], cnt[:, :], float(TILE - 1), None, ALU.add))
                st.wait()
                shift = TILE.bit_length() - 1
                st.did(dve.tensor_scalar(cnt_j[:, :], cnt_i[:, :], shift, shift, ALU.logical_shift_right, ALU.logical_shift_left))
                st.wait()
                st.did(dve.tensor_copy(cnt[:, :], cnt_j[:, :]))
                st.wait()
                st.did(dve.tensor_tensor_scan(ends[:, :], ones_f[:, 0:E], cnt[:, :], 0.0, ALU.mult, ALU.add))
                st.wait()
                st.did(dve.tensor_tensor(off[:, :], ends[:, :], cnt[:, :], ALU.subtract))
                st.wait()
                st.did(dve.tensor_tensor(off[:, :], off[:, :], before[:, :], ALU.subtract))
                st.wait()
                st.did(dve.tensor_tensor(tot[:, :, :], tot[:, :, :], off[:, :].unsqueeze(2).broadcast_to([P, E, NT]), ALU.add))
                st.wait()
                st.did(dve.tensor_tensor(cum[:, :, :].rearrange("p e t -> p (e t)"), bank[3][:, 0:E * NT],
                                         tot[:, :, :].rearrange("p e t -> p (e t)"), ALU.add))
                for kk, tmp in enumerate((eq, lg2)):
                    st.wait()
                    st.did(dve.tensor_tensor(tmp[:, :, :], oh[:, kk, :, :], cum[:, :, :].rearrange("p e t -> p t e"), ALU.mult))
                for kk, tmp in enumerate((eq, lg2)):
                    st.wait()
                    st.did(dve.tensor_reduce(pos[:, kk, :], tmp[:, :, :], AX.X, ALU.add))
                st.wait()
                st.did(dve.tensor_copy(pos_i[:, :], pos[:, :, :].rearrange("p k t -> p (k t)")))
                st.did(dve.tensor_copy(pos_u[:, :, :], pos[:, :, :].rearrange("p k t -> p t k")))
                st.wait()
                lop = P.bit_length() - 1
                st.did(dve.tensor_scalar(half_i[:, 0, :], pos_i[:, :], lop, 0, ALU.logical_shift_right, ALU.logical_shift_left))
                st.did(dve.tensor_scalar(half_i[:, 1, :], pos_i[:, :], 32 - lop, 32 - lop, ALU.logical_shift_left, ALU.logical_shift_right))
                st.wait()
                dve.tensor_copy(half[:, :, :], half_i[:, :, :]).then_inc(f["slots"], 1)
                dve.wait_ge(f["slots"], 1)
                with dve.Fori(0, KT // 8) as i:
                    for dst, width, n in ((oh_hi, NS, 0), (oh_lo, P, 1)):
                        ins = dve.tensor_tensor(dst[:, bass.ds(i * 8, 8), :], iota_lo[:, 0:width].unsqueeze(1).broadcast_to([P, 8, width]),
                                                half[:, n, bass.ds(i * 8, 8)].unsqueeze(2).broadcast_to([P, 8, width]), ALU.is_equal)
                    ins.then_inc(f["lo"], 1)
                st.did(dve.tensor_tensor(past[:, :, :], ends[0:1, :].unsqueeze(1).broadcast_to([1, NJ, E]),
                                         tile_lo[:, :].unsqueeze(2).broadcast_to([1, NJ, E]), ALU.is_le))
                st.wait()
                st.did(dve.tensor_reduce(exp_f[:, 2:NJ + 2], past[:, :, :], AX.X, ALU.add))
                st.wait()
                st.did(dve.tensor_scalar(exp_f[:, 2:NJ + 2], exp_f[:, 2:NJ + 2], float(E - 1), None, ALU.min))
                st.wait()
                st.did(dve.tensor_copy(code_f[:, :], exp_f[:, 4:NJ + 2:3]))
                for n in (3, 2, 1, 0):
                    st.wait()
                    st.did(dve.scalar_tensor_tensor(out=(code if n == 0 else code_f)[:, :], in0=code_f[:, :], scalar=float(1 << EB),
                                                    in1=exp_f[:, n:n + 3 * NR - 2:3], op0=ALU.mult, op1=ALU.add))
                dve.wait_ge(f["gate"], 1)
                st.did(dve.tensor_scalar(gate[:, :, :], gate[:, :, :], 0.5, None, ALU.mult))

                dve.wait_ge(f["inv"], 1)
                found = bank[6][:, 0:NS]
                st.did(dve.tensor_scalar(used[:, :], found, 0.0, None, ALU.is_equal))
                st.did(dve.tensor_scalar(rows_i[:, :], found.bitcast(U32), 16, TOPK * N - 1, ALU.logical_shift_right, ALU.bitwise_and))
                st.wait()
                st.did(dve.tensor_tensor(used[:, :], used[:, :], slot_c[:, :], ALU.mult))
                st.wait()
                st.did(dve.tensor_tensor(idx[:, 6:NJ + 6, 1, :], used[:, :].rearrange("p (j s) -> p j s", s=SUB),
                                         rows_i[:, :].rearrange("p (j s) -> p j s", s=SUB), ALU.add))
                dve.tensor_scalar(idx[:, 0:NJ, 0, :], rows_i[:, :].rearrange("p (j s) -> p j s", s=SUB), N - 1, None,
                                  ALU.bitwise_and).then_inc(f["idx"], 1)
                st.wait()

                def load_x(j, u):
                    dve.wait_ge(f["rows_in"], j + 1)
                    if later(j, 3):
                        dve.wait_ge(f["hmm"], j - 2)
                    dve.tensor_copy(xT[:, u, :, :].rearrange("p h s -> p (h s)"),
                                    bank[6][:, :].bitcast(F16)[:, 0:2 * TILE]).then_inc(f["xT"], 1)

                def split(j, u):
                    dve.wait_ge(f["gelu"], j + 1)
                    if later(j, 3):
                        dve.wait_ge(f["ymm"], j - 2)
                    st.did(dve.tensor_copy(hid_hl[:, u, 0, :, :], hid[:, u, :, :]))
                    st.wait()
                    dve.tensor_tensor(hid_hl[:, u, 1, :, :], hid[:, u, :, :], hid_hl[:, u, 0, :, :], ALU.subtract).then_inc(f["hs"], 1)

                def leave(j, u, i, ex):
                    dve.wait_ge(f["ymm"], j + 1)
                    if later(i, 1):
                        dve.wait_ge(f["put"][u], (16 if k == 0 else 32) * i)
                    dve.tensor_tensor(ys[:, u, :, :], bank[7][:, 0:SUB * D].rearrange("p (s d) -> p s d", s=SUB),
                                      b2_r[:, bass.ds(ex * D, D)].unsqueeze(1).broadcast_to([P, SUB, D]),
                                      ALU.add).then_inc(f["y"], 1)

                def steps(i, head=False, tail=False):
                    ex = None if head else experts(dve, i - 1)[2:]
                    for u in range(3):
                        j = 3 * i + u
                        if not head:
                            leave(j - 3, u, i - 1, ex[u])
                        if not (tail and u == 2):
                            load_x(j + 1, (u + 1) % 3)
                        if not (head and u == 0):
                            split(j - 1, (u + 2) % 3)

                load_x(0, 0)
                steps(0, head=True)
                steps(1)
                with dve.Fori(2, NR - 1) as i:
                    st.enter(i - 2, 3)
                    steps(i)
                st.leave(NR - 3)
                steps(NR - 1, tail=True)
                split(NJ - 1, 2)
                for u, ex in enumerate(experts(dve, NR - 1)[2:]):
                    leave(NJ - 3 + u, u, NR - 1, ex)

                if k == 0:
                    return
                for c in range(2 * NC):
                    dve.wait_ge(f["yc"][c], 32)
                    for t in range(CH // 2):
                        tt = c * (CH // 2) + t
                        ins = dve.scalar_tensor_tensor(out=x[:, tt, :], in0=yc(c)[:, 0, t, :], scalar=gate[:, 0, tt:tt + 1],
                                                       in1=x[:, tt, :], op0=ALU.mult, op1=ALU.add)
                    ins.then_inc(f["first"], 1)

            ffn(0)
            attention()
            ffn(1)


_INS = ["L0_attn_x", "L0_attn_Wq", "L0_attn_Wk", "L0_attn_Wv", "L0_attn_Wo", "L0_ffn_Wg",
        "L0_ffn_W1", "L0_ffn_b1", "L0_ffn_W2", "L0_ffn_b2"]


def rope_tables(length, dk, theta=10000.0):
    f = np.float32
    rates = f(theta) ** (-(f(2.0) * np.arange(dk // 2, dtype=f)) / f(dk))
    angles = np.arange(length, dtype=f)[:, None] * rates[None, :].astype(f)
    cos, sin = np.cos(angles), np.sin(angles)
    return (np.repeat(cos, 2, axis=1).astype(f), np.stack([-sin, sin], axis=-1).reshape(length, dk).astype(f))


def kernel(**inputs):
    import concourse.bacc as bacc
    from concourse.bass_utils import run_bass_kernel_spmd

    nc = bacc.Bacc("TRN2", target_bir_lowering=False, num_devices=1)
    given = {name: np.ascontiguousarray(inputs[name]) for name in _INS}
    B, L, D = given["L0_attn_x"].shape
    given["rope_c"], given["rope_s"] = rope_tables(L, D // 16)
    arrays, args = {}, []
    for name, a in given.items():
        arrays[f"in_{name}"] = a
        args.append(nc.dram_tensor(f"in_{name}", a.shape, mybir.dt.from_np(a.dtype), kind="ExternalInput").ap())
    out = nc.dram_tensor("out_0", (B, L, D), F32, kind="ExternalOutput").ap()
    macaron(nc, *args, out)
    r = run_bass_kernel_spmd(nc, [arrays], core_ids=[0])
    return r.results[0]["out_0"]
```
